# Optimizing a Trainium2 kernel written in Bass

```python
import numpy as np
import jax
import jax.numpy as jnp

def _softmax(x, axis=-1):
    return jax.nn.softmax(x, axis=axis)

def _gelu(x):
    return jax.nn.gelu(x, approximate=True)

def _silu(x):
    return jax.nn.silu(x)

def _sigmoid(x):
    return jax.nn.sigmoid(x)

def _layernorm(x, axis=-1, eps=1e-05):
    m = jnp.mean(x, axis=axis, keepdims=True)
    v = jnp.var(x, axis=axis, keepdims=True)
    return (x - m) / jnp.sqrt(v + eps)

def _scatter_add(tgt, idx, src, axis=0):
    return tgt.at[idx].add(src)

def _segment_sum(src, seg, n):
    return jax.ops.segment_sum(src, seg, n)
kernel_name = 'mk_macaron_d1_jaxref_r8_ac73be'

def setup_inputs(seed: int=0):
    np.random.seed(seed)
    _w = jnp.asarray

    def _L0_attn_setup():
        import jax, jax.numpy as jnp
        import numpy as np
        from jax import lax
        H = 128
        DI = 256
        N = 16
        DC = 4
        DTR = 64
        B, L = (2, 256)
        EPS = 1e-05

        def _selective_scan(u, delta, A, Bm, Cm, D):

            def step(h, inp):
                d, b, c, ut = inp
                dA = jnp.exp(d[:, :, None] * A)
                h = dA * h + (d * ut)[:, :, None] * b[:, None, :]
                y = jnp.einsum('bdn,bn->bd', h, c)
                return (h, y)
            h0 = jnp.zeros((u.shape[0], A.shape[0], A.shape[1]), u.dtype)
            xs = (delta.transpose(1, 0, 2), Bm.transpose(1, 0, 2), Cm.transpose(1, 0, 2), u.transpose(1, 0, 2))
            _, ys = lax.scan(step, h0, xs)
            return ys.transpose(1, 0, 2) + u * D

        def _mamba(x, in_proj_w, conv_w, conv_b, x_proj_w, dt_proj_w, dt_proj_b, A_log, D, out_proj_w):
            xz = x @ in_proj_w.T
            xi, z = (xz[..., :DI], xz[..., DI:])
            xc = lax.conv_general_dilated(xi.transpose(0, 2, 1), conv_w, window_strides=(1,), padding=[(DC - 1, 0)], feature_group_count=DI) + conv_b[None, :, None]
            xi = jax.nn.silu(xc.transpose(0, 2, 1))
            dbc = xi @ x_proj_w.T
            dt, Bm, Cm = (dbc[..., :DTR], dbc[..., DTR:DTR + N], dbc[..., DTR + N:])
            delta = jax.nn.softplus(dt @ dt_proj_w.T + dt_proj_b)
            A = -jnp.exp(A_log)
            y = _selective_scan(xi, delta, A, Bm, Cm, D)
            y = y * jax.nn.silu(z)
            return y @ out_proj_w.T
        key = jax.random.key(seed)
        ks = jax.random.split(key, 12)
        rn = lambda k, shp, sc=0.02: jax.random.normal(k, shp, jnp.float32) * sc
        return {'x': jax.random.normal(ks[0], (B, L, H), jnp.float32), 'ln_g': jnp.ones((H,), jnp.float32), 'ln_b': jnp.zeros((H,), jnp.float32), 'in_proj_w': rn(ks[1], (2 * DI, H)), 'conv_w': rn(ks[2], (DI, 1, DC), 0.2), 'conv_b': jnp.zeros((DI,), jnp.float32), 'x_proj_w': rn(ks[3], (DTR + 2 * N, DI)), 'dt_proj_w': rn(ks[4], (DI, DTR), 0.1), 'dt_proj_b': jax.random.uniform(ks[5], (DI,), jnp.float32, -4.0, -2.0), 'A_log': jnp.tile(jnp.log(jnp.arange(1, N + 1, dtype=jnp.float32))[None, :], (DI, 1)), 'D': jnp.ones((DI,), jnp.float32), 'out_proj_w': rn(ks[6], (H, DI)), 'dim_reduce_w': rn(ks[7], (H, 2 * H)), 'dim_reduce_b': jnp.zeros((H,), jnp.float32), 'glu_w': rn(ks[8], (2 * H, H)), 'glu_b': jnp.zeros((2 * H,), jnp.float32)}
    _L0_attn_in = _L0_attn_setup()

    def _L0_ffn_setup():
        import jax, jax.numpy as jnp
        import numpy as np
        D_MODEL = 128
        N_HEADS = 16
        N_GROUPS = 4
        D_FF = 512
        N_EXPERTS = 8
        TOP_K = 2
        BATCH = 2
        SEQ = 128
        D_K = D_MODEL // N_HEADS
        HPG = N_HEADS // N_GROUPS
        EPS = 1e-06

        def rms_norm(x, w):
            rms = jnp.sqrt(jnp.mean(x * x, axis=-1, keepdims=True) + EPS)
            return x / rms * w

        def rope(x):
            d = x.shape[-1]
            half = d // 2
            theta = 1.0 / 10000.0 ** (jnp.arange(half, dtype=jnp.float32) / half)
            pos = jnp.arange(x.shape[1], dtype=jnp.float32)[:, None]
            ang = pos * theta[None, :]
            cos, sin = (jnp.cos(ang), jnp.sin(ang))
            xe, xo = (x[..., 0::2], x[..., 1::2])
            return jnp.concatenate([xe * cos - xo * sin, xe * sin + xo * cos], axis=-1)

        def attention(x, Wq, Wk, Wv, Wo):
            B, S, _ = x.shape
            xr = rope(x)
            Q = (xr @ Wq).reshape(B, S, N_HEADS, D_K).transpose(0, 2, 1, 3)
            Q = Q.reshape(B, N_GROUPS, HPG, S, D_K)
            K = (xr @ Wk).reshape(B, S, N_GROUPS, D_K).transpose(0, 2, 1, 3)
            V = (xr @ Wv).reshape(B, S, N_GROUPS, D_K).transpose(0, 2, 1, 3)
            scores = jnp.einsum('bghsd,bgtd->bghst', Q, K) / jnp.sqrt(jnp.float32(D_K))
            mask = jnp.triu(jnp.full((S, S), -1000000000.0, dtype=scores.dtype), k=1)
            attn = jax.nn.softmax(scores + mask, axis=-1)
            out = jnp.einsum('bghst,bgtd->bghsd', attn, V)
            out = out.reshape(B, N_HEADS, S, D_K).transpose(0, 2, 1, 3).reshape(B, S, D_MODEL)
            return out @ Wo

        def moe(x, router_w, router_b, W1, b1, W2, b2, W3, b3):
            B, S, _ = x.shape
            logits = x @ router_w + router_b
            topv, topi = jax.lax.top_k(logits, TOP_K)
            topw = jax.nn.softmax(topv, axis=-1)
            onehot = jax.nn.one_hot(topi, N_EXPERTS, dtype=x.dtype)
            comb = jnp.einsum('bsk,bske->bse', topw, onehot)
            h1 = jnp.einsum('bsd,edf->ebsf', x, W1) + b1[:, None, None, :]
            h2 = jnp.einsum('bsd,edf->ebsf', x, W2) + b2[:, None, None, :]
            h = h2 * jax.nn.silu(h1)
            eo = jnp.einsum('ebsf,efd->ebsd', h, W3) + b3[:, None, None, :]
            return jnp.einsum('bse,ebsd->bsd', comb, eo)
        key = jax.random.key(seed)
        ks = jax.random.split(key, 16)
        s = 0.02
        return {'x': jax.random.normal(ks[0], (BATCH, SEQ, D_MODEL), dtype=jnp.float32), 'norm1_w': jnp.ones((D_MODEL,), jnp.float32), 'Wq': jax.random.normal(ks[1], (D_MODEL, D_MODEL), jnp.float32) * s, 'Wk': jax.random.normal(ks[2], (D_MODEL, N_GROUPS * D_K), jnp.float32) * s, 'Wv': jax.random.normal(ks[3], (D_MODEL, N_GROUPS * D_K), jnp.float32) * s, 'Wo': jax.random.normal(ks[4], (D_MODEL, D_MODEL), jnp.float32) * s, 'norm2_w': jnp.ones((D_MODEL,), jnp.float32), 'router_w': jax.random.normal(ks[5], (D_MODEL, N_EXPERTS), jnp.float32) * s, 'router_b': jnp.zeros((N_EXPERTS,), jnp.float32), 'W1': jax.random.normal(ks[6], (N_EXPERTS, D_MODEL, D_FF), jnp.float32) * s, 'b1': jnp.zeros((N_EXPERTS, D_FF), jnp.float32), 'W2': jax.random.normal(ks[7], (N_EXPERTS, D_MODEL, D_FF), jnp.float32) * s, 'b2': jnp.zeros((N_EXPERTS, D_FF), jnp.float32), 'W3': jax.random.normal(ks[8], (N_EXPERTS, D_FF, D_MODEL), jnp.float32) * s, 'b3': jnp.zeros((N_EXPERTS, D_MODEL), jnp.float32)}
    _L0_ffn_in = _L0_ffn_setup()
    _d = {'L0_attn_x': _L0_attn_in['x'], 'L0_attn_ln_g': _L0_attn_in['ln_g'], 'L0_attn_ln_b': _L0_attn_in['ln_b'], 'L0_attn_in_proj_w': _L0_attn_in['in_proj_w'], 'L0_attn_conv_w': _L0_attn_in['conv_w'], 'L0_attn_conv_b': _L0_attn_in['conv_b'], 'L0_attn_x_proj_w': _L0_attn_in['x_proj_w'], 'L0_attn_dt_proj_w': _L0_attn_in['dt_proj_w'], 'L0_attn_dt_proj_b': _L0_attn_in['dt_proj_b'], 'L0_attn_A_log': _L0_attn_in['A_log'], 'L0_attn_D': _L0_attn_in['D'], 'L0_attn_out_proj_w': _L0_attn_in['out_proj_w'], 'L0_attn_dim_reduce_w': _L0_attn_in['dim_reduce_w'], 'L0_attn_dim_reduce_b': _L0_attn_in['dim_reduce_b'], 'L0_attn_glu_w': _L0_attn_in['glu_w'], 'L0_attn_glu_b': _L0_attn_in['glu_b'], 'L0_ffn_norm1_w': _L0_ffn_in['norm1_w'], 'L0_ffn_Wq': _L0_ffn_in['Wq'], 'L0_ffn_Wk': _L0_ffn_in['Wk'], 'L0_ffn_Wv': _L0_ffn_in['Wv'], 'L0_ffn_Wo': _L0_ffn_in['Wo'], 'L0_ffn_norm2_w': _L0_ffn_in['norm2_w'], 'L0_ffn_router_w': _L0_ffn_in['router_w'], 'L0_ffn_router_b': _L0_ffn_in['router_b'], 'L0_ffn_W1': _L0_ffn_in['W1'], 'L0_ffn_b1': _L0_ffn_in['b1'], 'L0_ffn_W2': _L0_ffn_in['W2'], 'L0_ffn_b2': _L0_ffn_in['b2'], 'L0_ffn_W3': _L0_ffn_in['W3'], 'L0_ffn_b3': _L0_ffn_in['b3']}
    _x0 = _d['L0_attn_x']
    _d['L0_attn_x'] = jax.random.normal(jax.random.fold_in(jax.random.key(seed), 1), (4, 1024, 128), dtype=_x0.dtype)
    del _x0
    return _d

def reference(L0_attn_x, L0_attn_ln_g, L0_attn_ln_b, L0_attn_in_proj_w, L0_attn_conv_w, L0_attn_conv_b, L0_attn_x_proj_w, L0_attn_dt_proj_w, L0_attn_dt_proj_b, L0_attn_A_log, L0_attn_D, L0_attn_out_proj_w, L0_attn_dim_reduce_w, L0_attn_dim_reduce_b, L0_attn_glu_w, L0_attn_glu_b, L0_ffn_norm1_w, L0_ffn_Wq, L0_ffn_Wk, L0_ffn_Wv, L0_ffn_Wo, L0_ffn_norm2_w, L0_ffn_router_w, L0_ffn_router_b, L0_ffn_W1, L0_ffn_b1, L0_ffn_W2, L0_ffn_b2, L0_ffn_W3, L0_ffn_b3):

    def _L0_attn_ref(x, ln_g, ln_b, in_proj_w, conv_w, conv_b, x_proj_w, dt_proj_w, dt_proj_b, A_log, D, out_proj_w, dim_reduce_w, dim_reduce_b, glu_w, glu_b):
        import jax, jax.numpy as jnp
        import numpy as np
        from jax import lax
        H = 128
        DI = 256
        N = 16
        DC = 4
        DTR = 64
        B, L = (2, 256)
        EPS = 1e-05

        def _selective_scan(u, delta, A, Bm, Cm, D):

            def step(h, inp):
                d, b, c, ut = inp
                dA = jnp.exp(d[:, :, None] * A)
                h = dA * h + (d * ut)[:, :, None] * b[:, None, :]
                y = jnp.einsum('bdn,bn->bd', h, c)
                return (h, y)
            h0 = jnp.zeros((u.shape[0], A.shape[0], A.shape[1]), u.dtype)
            xs = (delta.transpose(1, 0, 2), Bm.transpose(1, 0, 2), Cm.transpose(1, 0, 2), u.transpose(1, 0, 2))
            _, ys = lax.scan(step, h0, xs)
            return ys.transpose(1, 0, 2) + u * D

        def _mamba(x, in_proj_w, conv_w, conv_b, x_proj_w, dt_proj_w, dt_proj_b, A_log, D, out_proj_w):
            xz = x @ in_proj_w.T
            xi, z = (xz[..., :DI], xz[..., DI:])
            xc = lax.conv_general_dilated(xi.transpose(0, 2, 1), conv_w, window_strides=(1,), padding=[(DC - 1, 0)], feature_group_count=DI) + conv_b[None, :, None]
            xi = jax.nn.silu(xc.transpose(0, 2, 1))
            dbc = xi @ x_proj_w.T
            dt, Bm, Cm = (dbc[..., :DTR], dbc[..., DTR:DTR + N], dbc[..., DTR + N:])
            delta = jax.nn.softplus(dt @ dt_proj_w.T + dt_proj_b)
            A = -jnp.exp(A_log)
            y = _selective_scan(xi, delta, A, Bm, Cm, D)
            y = y * jax.nn.silu(z)
            return y @ out_proj_w.T
        skip = x
        mu = x.mean(-1, keepdims=True)
        var = ((x - mu) ** 2).mean(-1, keepdims=True)
        xn = (x - mu) * lax.rsqrt(var + EPS) * ln_g + ln_b
        margs = (in_proj_w, conv_w, conv_b, x_proj_w, dt_proj_w, dt_proj_b, A_log, D, out_proj_w)
        x_f = _mamba(xn, *margs)
        x_r = jnp.flip(_mamba(jnp.flip(xn, 1), *margs), 1)
        y = jnp.concatenate([x_f, x_r], axis=-1) @ dim_reduce_w.T + dim_reduce_b
        y = jax.nn.gelu(y, approximate=False)
        g = y @ glu_w.T + glu_b
        y = g[..., :H] * jax.nn.sigmoid(g[..., H:])
        return y + skip

    def _L0_ffn_ref(x, norm1_w, Wq, Wk, Wv, Wo, norm2_w, router_w, router_b, W1, b1, W2, b2, W3, b3):
        import jax, jax.numpy as jnp
        import numpy as np
        D_MODEL = 128
        N_HEADS = 16
        N_GROUPS = 4
        D_FF = 512
        N_EXPERTS = 8
        TOP_K = 2
        BATCH = 2
        SEQ = 128
        D_K = D_MODEL // N_HEADS
        HPG = N_HEADS // N_GROUPS
        EPS = 1e-06

        def rms_norm(x, w):
            rms = jnp.sqrt(jnp.mean(x * x, axis=-1, keepdims=True) + EPS)
            return x / rms * w

        def rope(x):
            d = x.shape[-1]
            half = d // 2
            theta = 1.0 / 10000.0 ** (jnp.arange(half, dtype=jnp.float32) / half)
            pos = jnp.arange(x.shape[1], dtype=jnp.float32)[:, None]
            ang = pos * theta[None, :]
            cos, sin = (jnp.cos(ang), jnp.sin(ang))
            xe, xo = (x[..., 0::2], x[..., 1::2])
            return jnp.concatenate([xe * cos - xo * sin, xe * sin + xo * cos], axis=-1)

        def attention(x, Wq, Wk, Wv, Wo):
            B, S, _ = x.shape
            xr = rope(x)
            Q = (xr @ Wq).reshape(B, S, N_HEADS, D_K).transpose(0, 2, 1, 3)
            Q = Q.reshape(B, N_GROUPS, HPG, S, D_K)
            K = (xr @ Wk).reshape(B, S, N_GROUPS, D_K).transpose(0, 2, 1, 3)
            V = (xr @ Wv).reshape(B, S, N_GROUPS, D_K).transpose(0, 2, 1, 3)
            scores = jnp.einsum('bghsd,bgtd->bghst', Q, K) / jnp.sqrt(jnp.float32(D_K))
            mask = jnp.triu(jnp.full((S, S), -1000000000.0, dtype=scores.dtype), k=1)
            attn = jax.nn.softmax(scores + mask, axis=-1)
            out = jnp.einsum('bghst,bgtd->bghsd', attn, V)
            out = out.reshape(B, N_HEADS, S, D_K).transpose(0, 2, 1, 3).reshape(B, S, D_MODEL)
            return out @ Wo

        def moe(x, router_w, router_b, W1, b1, W2, b2, W3, b3):
            B, S, _ = x.shape
            logits = x @ router_w + router_b
            topv, topi = jax.lax.top_k(logits, TOP_K)
            topw = jax.nn.softmax(topv, axis=-1)
            onehot = jax.nn.one_hot(topi, N_EXPERTS, dtype=x.dtype)
            comb = jnp.einsum('bsk,bske->bse', topw, onehot)
            h1 = jnp.einsum('bsd,edf->ebsf', x, W1) + b1[:, None, None, :]
            h2 = jnp.einsum('bsd,edf->ebsf', x, W2) + b2[:, None, None, :]
            h = h2 * jax.nn.silu(h1)
            eo = jnp.einsum('ebsf,efd->ebsd', h, W3) + b3[:, None, None, :]
            return jnp.einsum('bse,ebsd->bsd', comb, eo)
        h = x + attention(rms_norm(x, norm1_w), Wq, Wk, Wv, Wo)
        h = h + moe(rms_norm(h, norm2_w), router_w, router_b, W1, b1, W2, b2, W3, b3)
        return h
    x = L0_attn_x
    x = x + 0.5 * _L0_ffn_ref(_layernorm(x, axis=-1), L0_ffn_norm1_w, L0_ffn_Wq, L0_ffn_Wk, L0_ffn_Wv, L0_ffn_Wo, L0_ffn_norm2_w, L0_ffn_router_w, L0_ffn_router_b, L0_ffn_W1, L0_ffn_b1, L0_ffn_W2, L0_ffn_b2, L0_ffn_W3, L0_ffn_b3)
    x = x + _L0_attn_ref(_layernorm(x, axis=-1), L0_attn_ln_g, L0_attn_ln_b, L0_attn_in_proj_w, L0_attn_conv_w, L0_attn_conv_b, L0_attn_x_proj_w, L0_attn_dt_proj_w, L0_attn_dt_proj_b, L0_attn_A_log, L0_attn_D, L0_attn_out_proj_w, L0_attn_dim_reduce_w, L0_attn_dim_reduce_b, L0_attn_glu_w, L0_attn_glu_b)
    x = x + 0.5 * _L0_ffn_ref(_layernorm(x, axis=-1), L0_ffn_norm1_w, L0_ffn_Wq, L0_ffn_Wk, L0_ffn_Wv, L0_ffn_Wo, L0_ffn_norm2_w, L0_ffn_router_w, L0_ffn_router_b, L0_ffn_W1, L0_ffn_b1, L0_ffn_W2, L0_ffn_b2, L0_ffn_W3, L0_ffn_b3)
    return x

_drawn_inputs = setup_inputs


def setup_inputs(seed=0):
    import zlib

    import numpy as np

    out = dict(_drawn_inputs(seed))
    spreads = {'L0_attn_ln_g': (1.0, 0.2),
     'L0_attn_ln_b': (0.0, 0.1),
     'L0_attn_conv_b': (0.0, 0.1),
     'L0_attn_D': (1.0, 0.2),
     'L0_attn_dim_reduce_b': (0.0, 0.1),
     'L0_attn_glu_b': (0.0, 0.1),
     'L0_ffn_norm1_w': (1.0, 0.2),
     'L0_ffn_norm2_w': (1.0, 0.2),
     'L0_ffn_router_b': (0.0, 0.1),
     'L0_ffn_b1': (0.0, 0.1),
     'L0_ffn_b2': (0.0, 0.1),
     'L0_ffn_b3': (0.0, 0.1)}
    factors = {}
    for name, (base, spread) in spreads.items():
        noise = np.random.default_rng([zlib.crc32(name.encode()), seed]).standard_normal(out[name].shape)
        drawn = base * np.exp(spread * noise) if base else spread * noise
        out[name] = jnp.asarray(drawn.astype(out[name].dtype))
    for name, factor in factors.items():
        out[name] = (out[name] * factor).astype(out[name].dtype)
    return out
```

```python
from contextlib import ExitStack

import concourse.bass as bass
from concourse import mybir

ALU = mybir.AluOpType
ACT = mybir.ActivationFunctionType
F32 = mybir.dt.float32
BF16 = mybir.dt.bfloat16
AX_X = mybir.AxisListType.X

P = 128
NB, S, D = 4, 1024, 128
TB = S // P
NT = NB * TB
HEADS, GROUPS, DK = 16, 4, 8
HPG = HEADS // GROUPS
NE, FF = 8, 512
FC = FF // P
DI, NS, DTR, DC = 256, 16, 64, 4
CI = DI // P
BANK = 512
LVL = 3
QROWS = 2 * LVL * DK
STACK = QROWS + LVL
VW = DK + 1
MASKED = -1.0e30
RMS_EPS, LN_EPS = 1e-6, 1e-5


class Chain:

    def __init__(self, eng, sem, base=0):
        self.eng, self.sem, self.base, self.n = eng, sem, base, 0

    def link(self, ins):
        self.n += 1
        ins.then_inc(self.sem, 1)
        self.eng.wait_ge(self.sem, self.base + self.n)


class Net:
    pass


def p1_fills():
    fills = [[(3, 0, 512, 0)]] + [[(i, 0, 512, 0)] for i in range(4, 8)] + [[(7, 512, 1024, 0)]]
    for i in (6, 5, 4):
        w = (i + 1) * P - 512
        fills.append([(i, 512, 512 + w, 0), (6 - i, 0, 512 - w, w)])
    return fills


def p2_fills():
    return [[(0, 0)], [(1, 0), (7, 896)], [(2, 0), (6, 768)], [(3, 0), (5, 640)], [(4, 0)]]


P1, P2 = p1_fills(), p2_fills()
P2_LEN = [sum(S - P * j for j, _ in f) for f in P2]
P_OFF = {j: S * f + o for f, fill in enumerate(P2) for j, o in fill}
PROBS = S * (len(P2) - 1) + P2_LEN[-1]


def setup(nc, net):
    sem = net.sem
    s_ld, s_c, s_cv = sem("setup_loads"), sem("setup_consts"), sem("setup_conv")
    s_m = sem("setup_memsets")
    with nc.Block() as block:
        loads = [(net.X[:, :, :], net.x.rearrange("b (i p) d -> p (b i) d", p=P))]
        for name in ("Wq", "Wk", "Wv", "Wo", "router_w", "norm1_w", "norm2_w", "router_b", "b1", "b2", "b3",
                     "in_w", "dt_w", "out_w", "glu_w", "conv_w", "conv_b", "dt_b", "Dv", "A_log", "dr_b", "glu_b",
                     "ln_g", "ln_b"):
            loads.append((net.w[name][:], net.d[name]))
        loads.append((net.w["x_w"][:, :, :], net.d["x_w"].rearrange("(c p) n -> p c n", p=P)))
        loads.append((net.w["dr_w"][:, :, :], net.d["dr_w"].rearrange("(c p) n -> p c n", p=P)))
        for name in ("cos", "sin"):
            loads.append((net.w[name][:, :, :], net.d[name].rearrange("(i p) k -> p i k", p=P)))
        @block.sync
        def _(sp):
            for out, src in loads:
                sp.dma_start(out, src).then_inc(s_ld, 16)
            sp.wait_ge(s_ld, 16 * len(loads))

        @block.gpsimd
        def _(pool):
            pool.memset(net.identf[:, :], 0.0).then_inc(s_m, 1)
            pool.memset(net.mask_st[:, :], 0.0).then_inc(s_m, 1)
            pool.memset(net.mask_ts[:, :], 0.0).then_inc(s_m, 1)
            pool.memset(net.sel[:, :, :], 0.0).then_inc(s_m, 1)
            pool.memset(net.before[:, :, :], 1.0).then_inc(s_m, 1)
            pool.memset(net.mhalf[:, :], -0.5).then_inc(s_m, 1)
            pool.memset(net.VA[:, :, :, :], 1.0).then_inc(s_m, 1)
            pool.wait_ge(s_m, 7)
            pool.affine_select(out=net.identf[:, :], in_=net.identf[:, :], compare_op=ALU.not_equal, fill=1.0,
                               base=0, pattern=[[-1, P]], channel_multiplier=1).then_inc(s_c, 1)
            pool.affine_select(out=net.mask_st[:, :], in_=net.mask_st[:, :], compare_op=ALU.is_ge, fill=MASKED,
                               base=0, pattern=[[-1, P]], channel_multiplier=1).then_inc(s_c, 1)
            pool.affine_select(out=net.mask_ts[:, :], in_=net.mask_ts[:, :], compare_op=ALU.is_ge, fill=MASKED,
                               base=0, pattern=[[1, P]], channel_multiplier=-1).then_inc(s_c, 1)
            pool.affine_select(out=net.before[:, :, :], in_=net.before[:, :, :], compare_op=ALU.is_ge, fill=0.0,
                               base=-1, pattern=[[1, NE], [-1, NE]], channel_multiplier=0).then_inc(s_c, 1)
            for lvl in range(LVL):
                pool.affine_select(out=net.sel[:, :, :], in_=net.sel[:, :, :], compare_op=ALU.not_equal, fill=1.0,
                                   base=-2 * NS * lvl, pattern=[[-1, 2 * NS], [0, P]],
                                   channel_multiplier=1).then_inc(s_c, 1)
                pool.wait_ge(s_c, 5 + lvl)

        @block.vector
        def _(dve):
            dve.wait_ge(s_c, 1)
            dve.tensor_copy(net.identb[:, :], net.identf[:, :]).then_inc(s_cv, 1)


def norm_stats(dve, chain, src, stats, mv):
    for i in range(TB):
        ins = dve.bn_stats(stats[:, i, :], src(i))
    chain.link(ins)
    for i in range(TB):
        ins = dve.bn_aggr(mv[:, i, :], stats[:, i, :])
    chain.link(ins)


def attn_prep(nc, net, pre):
    sem = lambda n: net.sem(pre + n)
    s_chain, s_var, s_pow = sem("dve_chain"), sem("var_ready"), sem("rstd_ready")
    s_y, s_yr, s_rope, s_tp, s_xrt = sem("y_ready"), sem("rope_products"), sem("rope_ready"), sem("xr_turned"), sem("xrt_ready")
    s_qk, s_v, s_hi, s_r, s_mid, s_lo = sem("qk_ready"), sem("v_ready"), sem("hi_ready"), sem("rest_ready"), sem("mid_ready"), sem("lo_ready")
    s_ve, s_st = sem("v_stored"), sem("parts_stored")
    with ExitStack() as ctx:
        sb = lambda n, s, d=F32: ctx.enter_context(nc.sbuf_tensor(pre + n, s, d))
        pb = lambda n, s, d=F32: ctx.enter_context(nc.psum_tensor(pre + n, s, d))
        stats, mv = sb("stats", [P, TB, 6]), sb("mv", [P, TB, 2])
        var, rstd, msq = sb("var", [P, 2, TB]), sb("rstd", [P, 2, TB]), sb("msq", [P, TB])
        y = sb("y", [P, TB, D])
        xr = sb("xr", [P, TB, D])
        ra, rb = sb("ra", [P, TB, D]), sb("rb", [P, TB, D])
        xrT = sb("xrT", [P, S])
        qp, kp = sb("qp", [P, LVL, S], BF16), sb("kp", [GROUPS * DK, LVL, S], BF16)
        qr, kr = sb("qr", [P, S]), sb("kr", [GROUPS * DK, S])
        psT, psQ = pb("psT", [P, TB, P]), pb("psQ", [P, S])
        psK, psV = pb("psK", [GROUPS * DK, S]), pb("psV", [P, TB, GROUPS, DK])
        half = D // 2
        CH = 8
        block = ctx.enter_context(nc.Block())

        @block.vector
        def _(dve):
            for b in range(NB):
                ch = Chain(dve, s_chain, b * CH)
                X = net.X[:, bass.ds(b * TB, TB), :]
                U = net.U[:, bass.ds(b * TB, TB), :]
                norm_stats(dve, ch, lambda i: X[:, i, :], stats, mv)
                dve.tensor_scalar(var[:, 0, :], mv[:, :, 1], LN_EPS, None, ALU.add).then_inc(s_var, 1)
                dve.wait_ge(s_pow, 2 * b + 1)
                for i in range(TB):
                    ins = dve.tensor_scalar(U[:, i, :], X[:, i, :], mv[:, i, 0:1], rstd[:, 0, i:i + 1],
                                            ALU.subtract, ALU.mult)
                ch.link(ins)
                norm_stats(dve, ch, lambda i: U[:, i, :], stats, mv)
                ch.link(dve.tensor_tensor(msq[:, :], mv[:, :, 0], mv[:, :, 0], ALU.mult))
                dve.scalar_tensor_tensor(var[:, 1, :], msq[:, :], RMS_EPS, mv[:, :, 1],
                                         ALU.add, ALU.add).then_inc(s_var, 1)
                dve.wait_ge(s_pow, 2 * b + 2)
                for i in range(TB):
                    ins = dve.scalar_tensor_tensor(y[:, i, :], U[:, i, :], rstd[:, 1, i:i + 1],
                                                   net.w["norm1_w"][:, :], ALU.mult, ALU.mult)
                ins.then_inc(s_y, 1)
                dve.wait_ge(s_y, b + 1)
                cos, sin = net.w["cos"][:, :, :], net.w["sin"][:, :, :]
                dve.tensor_tensor(ra[:, :, 0:half], y[:, :, 0::2], cos, ALU.mult)
                dve.tensor_tensor(rb[:, :, 0:half], y[:, :, 1::2], sin, ALU.mult)
                ch.link(dve.tensor_tensor(ra[:, :, half:D], y[:, :, 0::2], sin, ALU.mult))
                dve.wait_ge(s_yr, b + 1)
                dve.wait_ge(s_tp, b + 1)
                dve.tensor_tensor(xr[:, :, 0:half], ra[:, :, 0:half], rb[:, :, 0:half], ALU.subtract)
                dve.tensor_tensor(xr[:, :, half:D], ra[:, :, half:D], rb[:, :, half:D], ALU.add).then_inc(s_rope, 1)
                dve.wait_ge(s_hi, 2 * b + 2)
                dve.wait_ge(s_lo, 2 * b + 1)
                dve.tensor_tensor(qr[:, :], psQ[:, :], qp[:, 0, :], ALU.subtract)
                dve.tensor_tensor(kr[:, :], psK[:, :], kp[:, 0, :], ALU.subtract).then_inc(s_r, 1)
                dve.wait_ge(s_v, b + 1)
                dve.tensor_copy(net.VA[:, bass.ds(b * TB, TB), :, 0:DK], psV[:, :, :, :]).then_inc(s_ve, 1)
                assert ch.n == CH - 1 or ch.n == CH, ch.n
                while ch.n < CH:
                    ch.link(dve.tensor_copy(msq[:, :], mv[:, :, 0]))

        @block.gpsimd
        def _(pool):
            pool.sem_inc(s_lo, 1)
            for b in range(NB):
                for k in range(2):
                    pool.wait_ge(s_var, 2 * b + k + 1)
                    pool.tensor_tensor(rstd[:, k, :], var[:, k, :], net.mhalf[:, 0:TB], ALU.pow).then_inc(s_pow, 1)
                pool.wait_ge(s_y, b + 1)
                pool.tensor_tensor(rb[:, :, half:D], y[:, :, 1::2], net.w["cos"][:, :, :], ALU.mult).then_inc(s_yr, 1)
                pool.wait_ge(s_r, b + 1)
                pool.tensor_copy(qp[:, 1, :], qr[:, :])
                pool.tensor_copy(kp[:, 1, :], kr[:, :]).then_inc(s_mid, 1)
                pool.wait_ge(s_mid, b + 1)
                pool.tensor_tensor(qp[:, 2, :], qr[:, :], qp[:, 1, :], ALU.subtract).then_inc(s_lo, 1)
                pool.tensor_tensor(kp[:, 2, :], kr[:, :], kp[:, 1, :], ALU.subtract).then_inc(s_lo, 1)

        @block.tensor
        def _(pe):
            pe.sem_inc(s_tp, 1)
            with pe.Fori(0, NB) as b:
                pe.wait_ge(s_rope, b + 1)
                for i in range(TB):
                    ins = pe.transpose(psT[:, i, :], xr[:, i, :], net.identf[:, :])
                ins.then_inc(s_tp, 1)
                pe.wait_ge(s_xrt, b + 1)
                for h in range(2):
                    pe.matmul(psQ[:, h * BANK:(h + 1) * BANK], net.w["Wq"][:, :], xrT[:, h * BANK:(h + 1) * BANK],
                              start=True, stop=True)
                    ins = pe.matmul(psK[:, h * BANK:(h + 1) * BANK], net.w["Wk"][:, :],
                                    xrT[:, h * BANK:(h + 1) * BANK], start=True, stop=True)
                ins.then_inc(s_qk, 1)
                for i in range(TB):
                    ins = pe.matmul(psV[:, i, :, :], xrT[:, i * P:(i + 1) * P], net.w["Wv"][:, :],
                                    start=True, stop=True)
                ins.then_inc(s_v, 1)
                pe.wait_ge(s_r, b + 1)
                pe.wait_ge(s_ve, b + 1)

        @block.scalar
        def _(act):
            act.sem_inc(s_st, 32)
            with act.Fori(0, NB) as b:
                act.wait_ge(s_tp, b + 2)
                act.activation(xrT[:, :], psT[:, :, :].rearrange("p i t -> p (i t)"), ACT.Copy).then_inc(s_xrt, 1)
                act.wait_ge(s_qk, b + 1)
                act.wait_ge(s_st, 32 * b + 32)
                act.activation(qp[:, 0, :], psQ[:, :], ACT.Copy).then_inc(s_hi, 1)
                act.activation(kp[:, 0, :], psK[:, :], ACT.Copy).then_inc(s_hi, 1)

        @block.sync
        def _(sp):
            for name in ("W1", "W2"):
                sp.dma_start(net.w[name][:, :, :], net.d[name].rearrange("e p f -> p e f")).then_inc(net.s_experts, 16)
            sp.dma_start(net.w["W3"][:, :, :, :],
                         net.d["W3"].rearrange("e (c p) n -> p e c n", p=P)).then_inc(net.s_experts, 16)
            for b in range(NB):
                sp.wait_ge(s_lo, 2 * b + 3)
                sp.dma_start(net.qd[bass.ds(b, 1), :, :, :].rearrange("o l p t -> p (o l) t"), qp[:, :, :]).then_inc(s_st, 16)
                sp.dma_start(net.kd[bass.ds(b, 1), :, :, :].rearrange("o l p t -> p (o l) t"), kp[:, :, :]).then_inc(s_st, 16)
                sp.wait_ge(s_st, 32 * b + 64)


def attn_core(nc, net, pre):
    sem = lambda n: net.sem(pre + n)
    s_ld = [sem(f"stacks_loaded{g}") for g in range(GROUPS)]
    s_nml = [sem(f"maxima_loaded{k}") for k in range(2)]
    s_p1f, s_p1r, s_p2f, s_ex = sem("rows_scored"), sem("rows_reduced"), sem("keys_scored"), sem("exp_done")
    s_pv, s_nb, s_tr, s_ntc = sem("pv_done"), sem("maxima_split"), sem("maxima_turned"), sem("maxima_copied")
    s_nst, s_evo, s_ch, s_init = sem("maxima_stored"), sem("pv_read"), sem("core_chain"), sem("core_init")
    NPAIR, NHEAD, NUNIT = NB * HEADS // 2, NB * HEADS, NB * GROUPS
    with ExitStack() as ctx:
        sb = lambda n, s, d=F32: ctx.enter_context(nc.sbuf_tensor(pre + n, s, d))
        pb = lambda n, s, d=F32: ctx.enter_context(nc.psum_tensor(pre + n, s, d))
        QS = sb("QS", [P, HEADS // 2, S], BF16)
        KS = sb("KS", [P, GROUPS, S], BF16)
        probs = [sb(f"probs{k}", [P, PROBS]) for k in range(2)]
        mx = sb("mx", [P, 2, 2, TB, 2])
        nm, nr = sb("nm", [P, 2 * TB]), sb("nr", [P, 2 * TB])
        nb = sb("nb", [P, 2, LVL, 2 * TB], BF16)
        nmT = sb("nmT", [LVL * 2 * TB, 2, P], BF16)
        rec = sb("rec", [P, HPG, TB, 1])
        ps1 = [pb(f"ps1_{k}", [P, BANK]) for k in range(2)]
        ps2 = [pb(f"ps2_{k}", [P, S]) for k in range(2)]
        psO = pb("psO", [P, HPG, TB, VW])
        psR = pb("psR", [LVL * 2 * TB, P], BF16)
        block = ctx.enter_context(nc.Block())

        @block.gpsimd
        def _(pool):
            pool.memset(KS[:, :, :], 1.0).then_inc(s_init, 1)

        @block.sync
        def _(sp):
            def load_unit(u):
                b, g = divmod(u, GROUPS)
                if b:
                    sp.wait_ge(s_pv, HPG * (u - GROUPS + 1))
                for par in range(2):
                    r = 64 * par
                    for r0, lv in ((0, (0, 3)), (24, (0, 2)), (40, (0, 1))):
                        n = lv[1] - lv[0]
                        for l in range(n):
                            src = net.qd[b, l, :, :].rearrange("(k h d) t -> h d k t", h=2, d=DK)
                            sp.dma_start(QS[r + r0 + DK * l:r + r0 + DK * (l + 1), 2 * g:2 * g + 2, :],
                                         src[par, :, 2 * g:2 * g + 2, :]).then_inc(s_ld[g], 16)
                    for slot, l in enumerate((0, 0, 0, 1, 1, 2)):
                        sp.dma_start(KS[r + DK * slot:r + DK * (slot + 1), g, :],
                                     net.kd[b, l, DK * g:DK * (g + 1), :]).then_inc(s_ld[g], 16)

            def maxima(j):
                k = j % 2
                sp.wait_ge(s_ntc, j + 1)
                sp.dma_start(net.nmd[k, :, :], nmT[:, k, :]).then_inc(s_nst, 16)
                sp.wait_ge(s_nst, 16 * (j + 1))
                src = net.nmd[k, :, :].rearrange("(l h i) t -> h l (i t)", l=LVL, h=2)
                for par in range(2):
                    r = 64 * par + QROWS
                    sp.dma_start(QS[r:r + LVL, j % (HEADS // 2), :], src[par]).then_inc(s_nml[k], 16)

            sp.wait_ge(s_init, 1)
            for g in range(GROUPS):
                load_unit(g)
            for j in range(NPAIR):
                maxima(j)
                if j >= 3 and (j - 3) % 2 == 0:
                    u = (j - 3) // 2 + GROUPS
                    if u < NUNIT:
                        load_unit(u)

        @block.tensor
        def _(pe):
            def pass1(H, f):
                b, h = divmod(H, HEADS)
                r, k, g = 64 * (h % 2), h // 2, h // HPG
                n = len(P1) * H + f
                if h % HPG == 0 and f == 0:
                    pe.wait_ge(s_ld[g], 16 * 24 * (b + 1))
                if n >= 2:
                    pe.wait_ge(s_p1r, n - 1)
                bank = ps1[n % 2]
                for i, t0, t1, c in P1[f]:
                    diag = t1 == (i + 1) * P
                    w = t1 - t0
                    ins = pe.matmul(bank[:, c:c + w], QS[r:r + QROWS, k, i * P:(i + 1) * P],
                                    KS[r:r + QROWS, g, t0:t1], start=True, stop=not diag)
                    if diag:
                        ins = pe.matmul(bank[:, c + w - P:c + w], net.identb[:, :], net.mask_st[:, :],
                                        start=False, stop=True)
                ins.then_inc(s_p1f, 1)

            def pass2(H, f):
                b, h = divmod(H, HEADS)
                r, k, g = 64 * (h % 2), h // 2, h // HPG
                n = len(P2) * H + f
                J = H // 2
                if f == 0 and h % 2 == 0:
                    pe.wait_ge(s_nml[J % 2], 32 * (J // 2 + 1))
                if n >= 2:
                    pe.wait_ge(s_ex, n - 1)
                buf = ps2[n % 2]
                for j, o in P2[f]:
                    c, end, s0 = o, o + S - P * j, j * P
                    while c < end:
                        w = min(end, (c // BANK + 1) * BANK) - c
                        ins = pe.matmul(buf[:, c:c + w], KS[r:r + STACK, g, j * P:(j + 1) * P],
                                        QS[r:r + STACK, k, s0:s0 + w], start=True, stop=c > o)
                        if c == o:
                            ins = pe.matmul(buf[:, o:o + P], net.identb[:, :], net.mask_ts[:, :],
                                            start=False, stop=True)
                        c, s0 = c + w, s0 + w
                ins.then_inc(s_p2f, 1)

            def pv(H):
                b, h = divmod(H, HEADS)
                g, hu = divmod(h, HPG)
                pe.wait_ge(s_ex, len(P2) * (H + 1))
                if hu == 0 and H:
                    pe.wait_ge(s_evo, H // HPG)
                for i in range(TB):
                    for j in range(i + 1):
                        c = P_OFF[j] + (i - j) * P
                        ins = pe.matmul(psO[:, hu, i, :], probs[H % 2][:, c:c + P], net.VA[:, b * TB + j, g, :],
                                        start=(j == 0), stop=(j == i))
                ins.then_inc(s_pv, 1)

            def turn_maxima(J):
                pe.wait_ge(s_nb, J + 1)
                if J:
                    pe.wait_ge(s_ntc, J)
                pe.transpose(psR[:, :], nb[:, J % 2, :, :].rearrange("p l c -> p (l c)"),
                             net.identb[:, :]).then_inc(s_tr, 1)

            for H in range(4):
                for f in range(len(P1)):
                    pass1(H, f)
                    if H == 2 and f == 2:
                        turn_maxima(0)
            for H in range(NHEAD):
                for f in range(len(P2)):
                    pass2(H, f)
                    if f == 0 and H % 2 == 0:
                        turn_maxima(H // 2 + 1) if H // 2 + 1 < NPAIR else None
                    if H + 4 < NHEAD:
                        pass1(H + 4, 2 * f)
                        if f < 4:
                            pass1(H + 4, 2 * f + 1)
                    if f == 1 and H:
                        pv(H - 1)
            pv(NHEAD - 1)

        @block.scalar
        def _(act):
            for H in range(NHEAD):
                if H >= 2:
                    act.wait_ge(s_pv, H - 1)
                for f in range(len(P2)):
                    n = len(P2) * H + f
                    act.wait_ge(s_p2f, n + 1)
                    act.activation(probs[H % 2][:, S * f:S * f + P2_LEN[f]], ps2[n % 2][:, 0:P2_LEN[f]], ACT.Exp,
                                   scale=DK ** -0.5).then_inc(s_ex, 1)

        @block.vector
        def _(dve):
            ch = Chain(dve, s_ch)

            def reduce_head(H):
                J, hh = divmod(H, 2)
                for f, pieces in enumerate(P1):
                    n = len(P1) * H + f
                    dve.wait_ge(s_p1f, n + 1)
                    for i, t0, t1, c in pieces:
                        ins = dve.tensor_reduce(mx[:, J % 2, hh, i, t0 // 512:t0 // 512 + 1],
                                                ps1[n % 2][:, c:c + t1 - t0], AX_X, ALU.max)
                    ins.then_inc(s_p1r, 1)

            def split_maxima(J):
                dve.wait_ge(s_p1r, len(P1) * 2 * (J + 1))
                if J >= 2:
                    dve.wait_ge(s_tr, J - 1)
                ch.link(dve.tensor_reduce(nm[:, :], mx[:, J % 2, :, :, :], AX_X, ALU.max, negate=True))
                part = nb[:, J % 2, :, :]
                ch.link(dve.tensor_copy(part[:, 0, :], nm[:, :]))
                ch.link(dve.tensor_tensor(nr[:, :], nm[:, :], part[:, 0, :], ALU.subtract))
                ch.link(dve.tensor_copy(part[:, 1, :], nr[:, :]))
                dve.tensor_tensor(part[:, 2, :], nr[:, :], part[:, 1, :], ALU.subtract).then_inc(s_nb, 1)

            def copy_maxima(J):
                dve.wait_ge(s_tr, J + 1)
                if J >= 2:
                    dve.wait_ge(s_nst, 16 * (J - 1))
                dve.tensor_copy(nmT[:, J % 2, :], psR[:, :]).then_inc(s_ntc, 1)

            def read_unit(u):
                b, g = divmod(u, GROUPS)
                dve.wait_ge(s_pv, HPG * (u + 1))
                ch.link(dve.reciprocal(rec[:, :, :, :], psO[:, :, :, DK:VW]))
                out = net.AO[:, b * TB:(b + 1) * TB, g * HPG * DK:(g + 1) * HPG * DK].rearrange(
                    "p i (h d) -> p h i d", h=HPG)
                dve.tensor_tensor(out, psO[:, :, :, 0:DK], rec[:, :, :, :].to_broadcast([P, HPG, TB, DK]),
                                  ALU.mult).then_inc(s_evo, 1)

            ch.link(dve.memset(mx[:, :, :, :, :], -3.0e38))
            for H in range(4):
                reduce_head(H)
                if H % 2:
                    split_maxima(H // 2)
                if H == 2:
                    copy_maxima(0)
            for H in range(NHEAD):
                if H % HPG == 1 and H > HPG:
                    read_unit(H // HPG - 1)
                if H % 2 == 0 and H // 2 + 1 < NPAIR:
                    copy_maxima(H // 2 + 1)
                if H + 4 < NHEAD:
                    reduce_head(H + 4)
                    if H % 2:
                        split_maxima(H // 2 + 2)
            read_unit(NUNIT - 1)


def attn_out(nc, net, pre):
    sem = lambda n: net.sem(pre + n)
    s_ch, s_aot, s_aoc, s_o, s_var, s_pow = sem("dve_chain"), sem("ao_turned"), sem("ao_copied"), sem("proj_done"), sem("var_ready"), sem("rstd_ready")
    s_y, s_yt, s_yc, s_lg, s_lgm, s_e = sem("y_ready"), sem("y_turned"), sem("y_copied"), sem("logits_ready"), sem("logits_shifted"), sem("exp_done")
    s_cb, s_ct, s_cc, s_b3, s_h = sem("comb_ready"), sem("comb_turned"), sem("comb_copied"), sem("b3_done"), sem("h_ready")
    CH = 16
    with ExitStack() as ctx:
        sb = lambda n, s, d=F32: ctx.enter_context(nc.sbuf_tensor(pre + n, s, d))
        pb = lambda n, s, d=F32: ctx.enter_context(nc.psum_tensor(pre + n, s, d))
        stats, mv = sb("stats", [P, TB, 6]), sb("mv", [P, TB, 2])
        var, rstd, msq = sb("var", [P, TB]), sb("rstd", [P, TB]), sb("msq", [P, TB])
        aoT, y = sb("aoT", [P, S]), sb("y", [P, TB, D])
        lg, lm = sb("lg", [P, TB, NE]), sb("lm", [P, TB, NE])
        top, ssum, rsum = sb("top", [P, TB, 1]), sb("ssum", [P, TB, 1]), sb("rsum", [P, TB, 1])
        gt, eq = sb("gt", [P, TB, NE, NE]), sb("eq", [P, TB, NE, NE])
        rank, ex = sb("rank", [P, TB, NE, 1]), sb("ex", [P, TB, NE])
        combT = sb("combT", [NE, TB, P])
        psA, psH, psY = pb("psA", [P, TB, P]), pb("psH", [P, TB, P]), pb("psY", [P, TB, P])
        psL, psC = pb("psL", [P, TB, NE]), pb("psC", [NE, 4, P])
        block = ctx.enter_context(nc.Block())

        @block.tensor
        def _(pe):
            with pe.Fori(0, NB) as b:
                pe.wait_ge(s_h, 2 * b + 1)
                for i in range(TB):
                    ins = pe.transpose(psA[:, i, :], y[:, i, :], net.identf[:, :])
                ins.then_inc(s_aot, 1)
                pe.wait_ge(s_aoc, b + 1)
                for i in range(TB):
                    ins = pe.matmul(psH[:, i, :], aoT[:, i * P:(i + 1) * P], net.w["Wo"][:, :], start=True, stop=True)
                ins.then_inc(s_o, 1)
                pe.wait_ge(s_y, b + 1)
                for i in range(TB):
                    ins = pe.transpose(psY[:, i, :], y[:, i, :], net.identf[:, :])
                ins.then_inc(s_yt, 1)
                pe.wait_ge(s_yc, b + 1)
                for i in range(TB):
                    ins = pe.matmul(psL[:, i, :], aoT[:, i * P:(i + 1) * P], net.w["router_w"][:, :],
                                    start=True, stop=True)
                ins.then_inc(s_lg, 1)
                pe.wait_ge(s_cb, b + 1)
                for half in range(2):
                    if half:
                        pe.wait_ge(s_cc, 2 * b + 1)
                    for i in range(4):
                        ins = pe.transpose(psC[:, i, :], ex[:, half * 4 + i, :], net.identf[:, :])
                    ins.then_inc(s_ct, 1)
                pe.wait_ge(s_cc, 2 * b + 2)
                for i in range(TB):
                    ins = pe.matmul(psH[:, i, :], combT[:, i, :], net.w["b3"][:, :], start=True, stop=True)
                ins.then_inc(s_b3, 1)

        @block.scalar
        def _(act):
            with act.Fori(0, NB) as b:
                act.wait_ge(s_aot, b + 1)
                act.activation(aoT[:, :], psA[:, :, :].rearrange("p i t -> p (i t)"), ACT.Copy).then_inc(s_aoc, 1)
                act.wait_ge(s_yt, b + 1)
                act.activation(net.yT[:, bass.ds(b * S, S)], psY[:, :, :].rearrange("p i t -> p (i t)"), ACT.Copy)
                act.wait_ge(s_o, b + 1)
                act.activation(aoT[:, :], psY[:, :, :].rearrange("p i t -> p (i t)"), ACT.Copy).then_inc(s_yc, 1)
                act.wait_ge(s_lgm, b + 1)
                act.activation(ex[:, :, :], lm[:, :, :], ACT.Exp).then_inc(s_e, 1)
                for half in range(2):
                    act.wait_ge(s_ct, 2 * b + half + 1)
                    act.activation(combT[:, half * 4:half * 4 + 4, :], psC[:, :, :], ACT.Copy).then_inc(s_cc, 1)

        @block.gpsimd
        def _(pool):
            for b in range(NB):
                pool.wait_ge(s_var, b + 1)
                pool.tensor_tensor(rstd[:, :], var[:, :], net.mhalf[:, 0:TB], ALU.pow).then_inc(s_pow, 1)

        @block.vector
        def _(dve):
            for b in range(NB):
                ch = Chain(dve, s_ch, b * CH)
                U = net.U[:, bass.ds(b * TB, TB), :]
                comb = net.comb[:, bass.ds(b * TB, TB), :]
                dve.tensor_copy(y[:, :, :], net.AO[:, bass.ds(b * TB, TB), :]).then_inc(s_h, 1)
                dve.wait_ge(s_o, b + 1)
                ch.link(dve.tensor_tensor(U, psH[:, :, :], U, ALU.add))
                norm_stats(dve, ch, lambda i: U[:, i, :], stats, mv)
                ch.link(dve.tensor_tensor(msq[:, :], mv[:, :, 0], mv[:, :, 0], ALU.mult))
                dve.scalar_tensor_tensor(var[:, :], msq[:, :], RMS_EPS, mv[:, :, 1], ALU.add, ALU.add).then_inc(s_var, 1)
                dve.wait_ge(s_pow, b + 1)
                for i in range(TB):
                    ins = dve.scalar_tensor_tensor(y[:, i, :], U[:, i, :], rstd[:, i:i + 1], net.w["norm2_w"][:, :],
                                                   ALU.mult, ALU.mult)
                ins.then_inc(s_y, 1)
                dve.wait_ge(s_lg, b + 1)
                rbias = net.w["router_b"][:, :].rearrange("p (o e) -> p o e", o=1).to_broadcast([P, TB, NE])
                ch.link(dve.tensor_tensor(lg[:, :, :], psL[:, :, :], rbias, ALU.add))
                mine = lg[:, :, :].rearrange("p i (e o) -> p i e o", o=1).to_broadcast([P, TB, NE, NE])
                other = lg[:, :, :].rearrange("p i (o e) -> p i o e", o=1).to_broadcast([P, TB, NE, NE])
                before = net.before[:, :, :].rearrange("p (o e) f -> p o e f", o=1).to_broadcast([P, TB, NE, NE])
                dve.tensor_tensor(gt[:, :, :, :], other, mine, ALU.is_gt)
                dve.tensor_tensor(eq[:, :, :, :], other, mine, ALU.is_equal)
                ch.link(dve.tensor_reduce(top[:, :, :], lg[:, :, :], AX_X, ALU.max))
                dve.tensor_tensor(lm[:, :, :], lg[:, :, :], top[:, :, :].to_broadcast([P, TB, NE]),
                                  ALU.subtract).then_inc(s_lgm, 1)
                ch.link(dve.tensor_tensor(eq[:, :, :, :], eq[:, :, :, :], before, ALU.mult))
                ch.link(dve.tensor_tensor(gt[:, :, :, :], gt[:, :, :, :], eq[:, :, :, :], ALU.add))
                ch.link(dve.tensor_reduce(rank[:, :, :, :], gt[:, :, :, :], AX_X, ALU.add))
                dve.wait_ge(s_e, b + 1)
                rk = rank[:, :, :, :].rearrange("p i e o -> p i (e o)")
                ch.link(dve.scalar_tensor_tensor(lm[:, :, :], rk, 1.5, ex[:, :, :], ALU.is_lt, ALU.mult))
                ch.link(dve.tensor_reduce(ssum[:, :, :], lm[:, :, :], AX_X, ALU.add))
                ch.link(dve.reciprocal(rsum[:, :, :], ssum[:, :, :]))
                dve.tensor_tensor(comb, lm[:, :, :], rsum[:, :, :].to_broadcast([P, TB, NE]), ALU.mult)
                dve.tensor_tensor(ex[:, :, :], lm[:, :, :], rsum[:, :, :].to_broadcast([P, TB, NE]),
                                  ALU.mult).then_inc(s_cb, 1)
                dve.wait_ge(s_b3, b + 1)
                dve.tensor_tensor(U, psH[:, :, :], U, ALU.add).then_inc(s_h, 1)
                while ch.n < CH:
                    ch.link(dve.tensor_copy(msq[:, :], mv[:, :, 0]))


def moe(nc, net, pre):
    sem = lambda n: net.sem(pre + n)
    s_h, s_sil, s_g, s_eo, s_acc, s_x = sem("h_ready"), sem("silu_done"), sem("gated"), sem("expert_out"), sem("expert_added"), sem("x_done")
    NCH = NT // 4
    N = NE * FC
    CREDIT = 2
    with ExitStack() as ctx:
        sb = lambda n, s, d=F32: ctx.enter_context(nc.sbuf_tensor(pre + n, s, d))
        pb = lambda n, s, d=F32: ctx.enter_context(nc.psum_tensor(pre + n, s, d))
        sil = [sb(f"sil{k}", [P, BANK]) for k in range(2)]
        hb = [sb(f"hb{k}", [P, FC, BANK]) for k in range(2)]
        ps1 = [pb(f"h1_{k}", [P, BANK]) for k in range(2)]
        ps2 = [pb(f"h2_{k}", [P, BANK]) for k in range(2)]
        pse = [pb(f"eo_{k}", [P, 4, D]) for k in range(2)]
        block = ctx.enter_context(nc.Block())

        @block.tensor
        def _(pe):
            pe.sem_inc(s_eo, CREDIT)
            pe.wait_ge(net.s_experts, 48)
            with pe.Fori(0, NCH) as c:
                xs = net.yT[:, bass.ds(c * BANK, BANK)]

                def up(e, fc):
                    n = e * FC + fc
                    pe.wait_ge(s_g, N * c + n + 1)
                    cols = slice(fc * P, (fc + 1) * P)
                    pe.matmul(ps1[n % 2][:, :], net.w["W1"][:, e, cols], xs, start=True, stop=True)
                    pe.matmul(ps2[n % 2][:, :], net.w["W2"][:, e, cols], xs, start=True, stop=True).then_inc(s_h, 1)

                def down(e):
                    pe.wait_ge(s_g, N * c + (e + 1) * FC + CREDIT)
                    pe.wait_ge(s_acc, NE * c + e + 1)
                    for t in range(4):
                        for fc in range(FC):
                            ins = pe.matmul(pse[e % 2][:, t, :], hb[e % 2][:, fc, t * P:(t + 1) * P],
                                            net.w["W3"][:, e, fc, :], start=(fc == 0), stop=(fc == FC - 1))
                    ins.then_inc(s_eo, 1)

                for e in range(NE):
                    for fc in range(FC):
                        up(e, fc)
                        if fc == 1 and e:
                            down(e - 1)
                down(NE - 1)

        @block.scalar
        def _(act):
            with act.Fori(0, NCH) as c:
                for n in range(N):
                    act.wait_ge(s_h, N * c + n + 1)
                    act.wait_ge(s_g, N * c + n + 1)
                    act.activation(sil[n % 2][:, :], ps1[n % 2][:, :], ACT.Silu,
                                   bias=net.w["b1"][:, n:n + 1]).then_inc(s_sil, 1)

        @block.vector
        def _(dve):
            dve.sem_inc(s_g, CREDIT)
            dve.sem_inc(s_acc, CREDIT)
            with dve.Fori(0, NCH) as c:
                H = net.U[:, bass.ds(c * 4, 4), :]
                X = net.X[:, bass.ds(c * 4, 4), :]
                comb = net.comb[:, bass.ds(c * 4, 4), :]

                def add(e):
                    dve.wait_ge(s_eo, NE * c + e + 1 + CREDIT)
                    dve.wait_ge(s_acc, NE * c + e + CREDIT)
                    for t in range(4):
                        ins = dve.scalar_tensor_tensor(H[:, t, :], pse[e % 2][:, t, :], comb[:, t, e:e + 1],
                                                       H[:, t, :], ALU.mult, ALU.add)
                    ins.then_inc(s_acc, 1)

                for e in range(NE):
                    dve.wait_ge(s_eo, NE * c + e + 1)
                    for fc in range(FC):
                        n = e * FC + fc
                        dve.wait_ge(s_sil, N * c + n + 1)
                        dve.scalar_tensor_tensor(hb[e % 2][:, fc, :], ps2[n % 2][:, :], net.w["b2"][:, n:n + 1],
                                                 sil[n % 2][:, :], ALU.add, ALU.mult).then_inc(s_g, 1)
                        if fc == 3 and e:
                            add(e - 1)
                add(NE - 1)
                dve.wait_ge(s_acc, NE * c + NE + CREDIT)
                dve.scalar_tensor_tensor(X, H, 0.5, X, ALU.mult, ALU.add).then_inc(s_x, 1)


def mamba_norm(nc, net, pre):
    sem = lambda n: net.sem(pre + n)
    s_ch, s_var, s_pow, s_y, s_yg, s_yb, s_t, s_c = (sem(n) for n in (
        "dve_chain", "var_ready", "rstd_ready", "y_ready", "y_scaled", "y_shifted", "y_turned", "y_copied"))
    CH = 6
    with ExitStack() as ctx:
        sb = lambda n, s, d=F32: ctx.enter_context(nc.sbuf_tensor(pre + n, s, d))
        pb = lambda n, s, d=F32: ctx.enter_context(nc.psum_tensor(pre + n, s, d))
        stats, mv = sb("stats", [P, TB, 6]), sb("mv", [P, TB, 2])
        var, rstd = sb("var", [P, 2, TB]), sb("rstd", [P, 2, TB])
        y = sb("y", [P, TB, D])
        psT = pb("psT", [P, TB, P])
        block = ctx.enter_context(nc.Block())

        @block.vector
        def _(dve):
            for b in range(NB):
                ch = Chain(dve, s_ch, b * CH)
                X = net.X[:, bass.ds(b * TB, TB), :]
                U = net.U[:, bass.ds(b * TB, TB), :]
                for k, src in enumerate((X, U)):
                    norm_stats(dve, ch, lambda i: src[:, i, :], stats, mv)
                    dve.tensor_scalar(var[:, k, :], mv[:, :, 1], LN_EPS, None, ALU.add).then_inc(s_var, 1)
                    dve.wait_ge(s_pow, 2 * b + k + 1)
                    if k == 1:
                        dve.wait_ge(s_t, b + 1)
                    for i in range(TB):
                        out = U[:, i, :] if k == 0 else y[:, i, :]
                        ins = dve.tensor_scalar(out, src[:, i, :], mv[:, i, 0:1], rstd[:, k, i:i + 1],
                                                ALU.subtract, ALU.mult)
                    if k == 0:
                        ch.link(ins)
                ins.then_inc(s_y, 1)
                ch.link(dve.tensor_tensor(X, X, U, ALU.add))

        @block.gpsimd
        def _(pool):
            for b in range(NB):
                for k in range(2):
                    pool.wait_ge(s_var, 2 * b + k + 1)
                    pool.tensor_tensor(rstd[:, k, :], var[:, k, :], net.mhalf[:, 0:TB], ALU.pow).then_inc(s_pow, 1)
                pool.wait_ge(s_y, b + 1)
                g = net.w["ln_g"][:, :].rearrange("p (o d) -> p o d", o=1).to_broadcast([P, TB, D])
                bb = net.w["ln_b"][:, :].rearrange("p (o d) -> p o d", o=1).to_broadcast([P, TB, D])
                pool.tensor_tensor(y[:, :, :], y[:, :, :], g, ALU.mult).then_inc(s_yg, 1)
                pool.wait_ge(s_yg, b + 1)
                pool.tensor_tensor(y[:, :, :], y[:, :, :], bb, ALU.add).then_inc(s_yb, 1)

        @block.tensor
        def _(pe):
            pe.sem_inc(s_t, 1)
            with pe.Fori(0, NB) as b:
                pe.wait_ge(s_yb, b + 1)
                pe.wait_ge(s_c, b + 1)
                for i in range(TB):
                    ins = pe.transpose(psT[:, i, :], y[:, i, :], net.identf[:, :])
                ins.then_inc(s_t, 1)

        @block.scalar
        def _(act):
            act.sem_inc(s_c, 1)
            with act.Fori(0, NB) as b:
                act.wait_ge(s_t, b + 2)
                act.activation(net.yT[:, bass.ds(b * S, S)], psT[:, :, :].rearrange("p i t -> p (i t)"),
                               ACT.Copy).then_inc(s_c, 1)


def mamba_scan(nc, net, pre):
    sem = lambda n: net.sem(pre + n)
    s_w0, s_w1, s_w2, s_w3 = sem("weights_product"), sem("weights_copied"), sem("a_exp"), sem("a_ready")
    s_pad = sem("pads_zero")
    s_in, s_ev, s_conv, s_cc = sem("in_proj"), sem("in_read"), sem("conv_done"), sem("conv_chain")
    s_u, s_xp, s_hi, s_r, s_mid, s_bc = sem("u_ready"), sem("x_proj"), sem("bc_hi"), sem("bc_rest"), sem("bc_mid"), sem("bc_ready")
    s_dts, s_dp, s_ab, s_sp, s_mxd, s_dl, s_du = sem("dt_ready"), sem("dt_proj"), sem("sp_chain"), sem("sp_log"), sem("sp_max"), sem("delta_ready"), sem("du_ready")
    s_B, s_C, s_Cc, s_da, s_bx, s_sc = sem("b_spread"), sem("c_spread"), sem("c_copied"), sem("decay_ready"), sem("input_ready"), sem("scanned")
    s_hc, s_y, s_yr, s_g, s_o, s_oc = sem("hc_ready"), sem("y_added"), sem("y_read"), sem("gated"), sem("out_proj"), sem("out_copied")
    PAD = DC - 1
    with ExitStack() as ctx:
        sb = lambda n, s, d=F32: ctx.enter_context(nc.sbuf_tensor(pre + n, s, d))
        pb = lambda n, s, d=F32: ctx.enter_context(nc.psum_tensor(pre + n, s, d))
        MT = sb("MT", [P, 2, CI, D])
        negA = sb("negA", [P, CI, NS])
        diagD = sb("diagD", [P, CI, P])
        xi = sb("xi", [P, CI, S + 2 * PAD])
        sz = sb("sz", [P, CI, S])
        u = sb("u", [P, CI, S])
        cv = sb("cv", [P, CI, S])
        bc = sb("bc", [LVL * 2 * NS, S], BF16)
        delta, du = sb("delta", [P, CI, S]), sb("du", [P, CI, S])
        dA = [sb(f"dA{k}", [P, S]) for k in range(2)]
        bx = [sb(f"bx{k}", [P, S]) for k in range(2)]
        hs = [sb(f"hs{k}", [P, S]) for k in range(2)]
        hc = [sb(f"hc{k}", [P, S]) for k in range(2)]
        Cs = sb("Cs", [P, 2, S])
        dts, bcr = hc[0][0:DTR, :], hc[1]
        g = net.U[:, :, :].rearrange("p (k c i) d -> p k c (i d)", k=2, c=CI)
        psB, psC = pb("psB", [P, S]), pb("psC", [P, S])
        psY = [pb(f"psY{c}", [P, S]) for c in range(CI)]
        block = ctx.enter_context(nc.Block())
        halves = [slice(0, BANK), slice(BANK, S)]
        NIN = 2 * CI
        ND = NB * 2

        @block.tensor
        def _(pe):
            for k in range(2):
                for c in range(CI):
                    ins = pe.matmul(psB[:, (k * CI + c) * P:(k * CI + c + 1) * P], net.w["out_w"][:, c * P:(c + 1) * P],
                                    net.w["dr_w"][:, k, :], start=True, stop=True)
            ins.then_inc(s_w0, 1)
            pe.wait_ge(s_w1, 1)
            pe.sem_inc(s_y, 2)
            with pe.Fori(0, NB) as b:
                xs = net.yT[:, bass.ds(b * S, S)]
                pe.wait_ge(s_oc, b + 1)
                for m in range(NIN):
                    out = (psY + [psB, psC])[m]
                    for hf in halves:
                        ins = pe.matmul(out[:, hf], net.w["in_w"][:, m * P:(m + 1) * P], xs[:, hf],
                                        start=True, stop=True)
                    ins.then_inc(s_in, 1)
                for d in range(2):
                    st = 2 * b + d
                    pe.wait_ge(s_u, CI * st + CI)
                    pe.wait_ge(s_ev, NIN * b + NIN)
                    for hf in halves:
                        for c in range(CI):
                            ins = pe.matmul(psB[0:DTR + 2 * NS, hf], net.w["x_w"][:, c, :], u[:, c, hf],
                                            start=(c == 0), stop=(c == CI - 1))
                    ins.then_inc(s_xp, 1)
                    pe.wait_ge(s_dts, st + 1)
                    for c in range(CI):
                        for hf in halves:
                            ins = pe.matmul(psY[c][:, hf], net.w["dt_w"][:, c * P:(c + 1) * P], dts[:, hf],
                                            start=True, stop=True)
                    ins.then_inc(s_dp, 1)
                    pe.wait_ge(s_mxd, CI * st + CI)
                    pe.wait_ge(s_ab, 2 * CI * st + 2 * CI)
                    for c in range(CI):
                        for hf in halves:
                            pe.matmul(psY[c][:, hf], diagD[:, c, :], u[:, c, hf], start=True, stop=False,
                                      skip_group_check=True)
                    pe.wait_ge(s_bc, st + 1)

                    def spread(n):
                        k = NS * st + n
                        if n:
                            pe.wait_ge(s_bx, CI * k)
                        for hf in halves:
                            ins = pe.matmul(psB[:, hf], net.sel[:, n, :], bc[:, hf], start=True, stop=True)
                        ins.then_inc(s_B, 1)
                        if n:
                            pe.wait_ge(s_Cc, k)
                        for hf in halves:
                            ins = pe.matmul(psC[:, hf], net.sel[:, NS + n, :], bc[:, hf], start=True, stop=True)
                        ins.then_inc(s_C, 1)

                    def add_y(n):
                        k = NS * st + n
                        for c in range(CI):
                            pe.wait_ge(s_hc, CI * k + c + 1)
                            for hf in halves:
                                ins = pe.matmul(psY[c][:, hf], net.identf[:, :], hc[c][:, hf], start=False,
                                                stop=(n == NS - 1), skip_group_check=True)
                            ins.then_inc(s_y, 1)

                    for n in range(NS):
                        spread(n)
                        if n:
                            add_y(n - 1)
                    add_y(NS - 1)
                pe.wait_ge(s_g, 2 * CI * b + 2 * CI)
                for hf in halves:
                    for k in range(2 * CI):
                        ins = pe.matmul(psB[:, hf], MT[:, k // CI, k % CI, :], g[:, k // CI, k % CI, hf],
                                        start=(k == 0), stop=(k == 2 * CI - 1))
                ins.then_inc(s_o, 1)

        @block.scalar
        def _(act):
            act.activation(negA[:, :, :], net.w["A_log"][:, :, :], ACT.Exp).then_inc(s_w2, 1)
            act.wait_ge(s_w0, 1)
            act.activation(MT[:, :, :, :].rearrange("p k c o -> p (k c o)"), psB[:, 0:2 * CI * P], ACT.Copy).then_inc(s_w1, 1)
            act.sem_inc(s_oc, 1)
            act.wait_ge(s_w3, 1)
            with act.Fori(0, NB) as b:
                for m in range(CI):
                    act.wait_ge(s_in, NIN * b + m + 1)
                    act.activation(xi[:, m, PAD:PAD + S], psY[m][:, :], ACT.Copy).then_inc(s_ev, 1)
                for m in range(CI):
                    act.wait_ge(s_in, NIN * b + CI + m + 1)
                    act.activation(sz[:, m, :], [psB, psC][m][:, :], ACT.Silu).then_inc(s_ev, 1)
                for d in range(2):
                    st = 2 * b + d
                    for c in range(CI):
                        act.wait_ge(s_conv, CI * st + c + 1)
                        act.activation(u[:, c, :], cv[:, c, :], ACT.Silu).then_inc(s_u, 1)
                    act.wait_ge(s_xp, st + 1)
                    act.activation(dts[:, :], psB[0:DTR, :], ACT.Copy).then_inc(s_dts, 1)
                    act.activation(bc[0:2 * NS, :], psB[DTR:DTR + 2 * NS, :], ACT.Copy).then_inc(s_hi, 1)
                    act.wait_ge(s_dp, st + 1)
                    for c in range(CI):
                        act.activation(cv[:, c, :], psY[c][:, :], ACT.Abs, bias=net.w["dt_b"][:, c:c + 1]).then_inc(s_ab, 1)
                    act.wait_ge(s_ab, 2 * CI * st + CI)
                    for c in range(CI):
                        act.activation(cv[:, c, :], cv[:, c, :], ACT.Exp, scale=-1.0).then_inc(s_ab, 1)
                    act.wait_ge(s_ab, 2 * CI * st + 2 * CI)
                    for c in range(CI):
                        act.activation(cv[:, c, :], cv[:, c, :], ACT.Ln, bias=1.0).then_inc(s_sp, 1)
                    for n in range(NS):
                        k = NS * st + n
                        for c in range(CI):
                            if c == 0 and n == 0:
                                act.wait_ge(s_dl, CI * st + CI)
                            if n:
                                act.wait_ge(s_sc, CI * (k - 1) + c + 1)
                            act.activation(dA[c][:, :], delta[:, c, :], ACT.Exp,
                                           scale=negA[:, c, n:n + 1]).then_inc(s_da, 1)
                        act.wait_ge(s_C, k + 1)
                        if n >= 2:
                            act.wait_ge(s_hc, CI * (k - 1))
                        act.activation(Cs[:, n % 2, :], psC[:, :], ACT.Copy).then_inc(s_Cc, 1)
                act.wait_ge(s_o, b + 1)
                act.activation(net.yT[:, bass.ds(b * S, S)], psB[:, :], ACT.Copy).then_inc(s_oc, 1)

        @block.vector
        def _(dve):
            dve.memset(xi[:, :, 0:PAD], 0.0).then_inc(s_pad, 1)
            dve.memset(xi[:, :, PAD + S:], 0.0).then_inc(s_pad, 1)
            dve.wait_ge(s_pad, 2)
            dve.wait_ge(s_w2, 1)
            dve.tensor_scalar(negA[:, :, :], negA[:, :, :], -1.0, None, ALU.mult).then_inc(s_pad, 1)
            for c in range(CI):
                ins = dve.tensor_scalar(diagD[:, c, :], net.identf[:, :], net.w["Dv"][:, c:c + 1], None, ALU.mult)
            ins.then_inc(s_w3, 1)
            with dve.Fori(0, NB) as b:
                for d in range(2):
                    st = 2 * b + d
                    for k in range(DC):
                        for c in range(CI):
                            if d == 0 and k == 0:
                                dve.wait_ge(s_ev, NIN * b + c + 1)
                            o = k if d == 0 else 2 * PAD - k
                            tap = net.w["conv_w"][:, c, k:k + 1]
                            src = xi[:, c, o:o + S]
                            if k == 0:
                                ins = dve.tensor_scalar(cv[:, c, :], src, tap, net.w["conv_b"][:, c:c + 1], ALU.mult, ALU.add)
                            else:
                                dve.wait_ge(s_cc, (DC - 1) * CI * st + (k - 1) * CI + c + 1)
                                ins = dve.scalar_tensor_tensor(cv[:, c, :], src, tap, cv[:, c, :], ALU.mult, ALU.add)
                            ins.then_inc(s_conv if k == DC - 1 else s_cc, 1)
                    dve.wait_ge(s_hi, st + 1)
                    dve.tensor_tensor(bcr[2 * NS:4 * NS, :], psB[DTR:DTR + 2 * NS, :], bc[0:2 * NS, :],
                                      ALU.subtract).then_inc(s_r, 1)
                    dve.wait_ge(s_r, st + 1)
                    dve.tensor_copy(bc[2 * NS:4 * NS, :], bcr[2 * NS:4 * NS, :]).then_inc(s_mid, 1)
                    dve.wait_ge(s_mid, st + 1)
                    dve.tensor_tensor(bc[4 * NS:6 * NS, :], bcr[2 * NS:4 * NS, :], bc[2 * NS:4 * NS, :],
                                      ALU.subtract).then_inc(s_bc, 1)
                    dve.wait_ge(s_dp, st + 1)
                    dve.wait_ge(s_ab, 2 * CI * st + CI)
                    for c in range(CI):
                        ins = dve.tensor_scalar(delta[:, c, :], psY[c][:, :], net.w["dt_b"][:, c:c + 1], 0.0,
                                                ALU.add, ALU.max).then_inc(s_mxd, 1)
                    dve.wait_ge(s_mxd, CI * st + CI)
                    for c in range(CI):
                        dve.wait_ge(s_sp, CI * st + c + 1)
                        dve.tensor_tensor(delta[:, c, :], delta[:, c, :], cv[:, c, :], ALU.add).then_inc(s_dl, 1)
                    for c in range(CI):
                        dve.wait_ge(s_dl, CI * st + c + 1)
                        dve.tensor_tensor(du[:, c, :], delta[:, c, :], u[:, c, :], ALU.mult).then_inc(s_du, 1)
                    dve.wait_ge(s_du, CI * st + CI)
                    way = slice(None) if d == 0 else slice(None, None, -1)
                    for n in range(NS):
                        k = NS * st + n
                        dve.wait_ge(s_B, k + 1)
                        for c in range(CI):
                            if n:
                                dve.wait_ge(s_sc, CI * (k - 1) + c + 1)
                            dve.tensor_tensor(bx[c][:, :], psB[:, :], du[:, c, :], ALU.mult).then_inc(s_bx, 1)
                        for c in range(CI):
                            dve.wait_ge(s_bx, CI * k + c + 1)
                            dve.wait_ge(s_da, CI * k + c + 1)
                            if n:
                                dve.wait_ge(s_hc, CI * (k - 1) + c + 1)
                            dve.tensor_tensor_scan(hs[c][:, way], dA[c][:, way], bx[c][:, way], 0.0,
                                                   ALU.mult, ALU.add).then_inc(s_sc, 1)
                    for c in range(CI):
                        dve.wait_ge(s_y, CI * NS * st + CI * NS + 2)
                        dve.tensor_tensor(g[:, d, c, :], psY[c][:, :], sz[:, c, :], ALU.mult).then_inc(s_g, 1)

        @block.gpsimd
        def _(pool):
            with pool.Fori(0, NB) as b:
                for d in range(2):
                    st = 2 * b + d
                    for n in range(NS):
                        k = NS * st + n
                        pool.wait_ge(s_Cc, k + 1)
                        for c in range(CI):
                            pool.wait_ge(s_sc, CI * k + c + 1)
                            pool.wait_ge(s_y, CI * k + c + 1)
                            pool.tensor_tensor(hc[c][:, :], hs[c][:, :], Cs[:, n % 2, :], ALU.mult).then_inc(s_hc, 1)


def mamba_out(nc, net, pre):
    sem = lambda n: net.sem(pre + n)
    s_ge, s_p, s_sg, s_m, s_t, s_x = (sem(n) for n in ("gelu_done", "glu_ready", "sigmoid_done", "glu_done", "turned", "added"))
    NCH = NT // 4
    with ExitStack() as ctx:
        sb = lambda n, s, d=F32: ctx.enter_context(nc.sbuf_tensor(pre + n, s, d))
        pb = lambda n, s, d=F32: ctx.enter_context(nc.psum_tensor(pre + n, s, d))
        gl = sb("gl", [P, NT * P])
        sg = [sb(f"sg{k}", [P, BANK]) for k in range(2)]
        yy = [sb(f"yy{k}", [P, BANK]) for k in range(2)]
        psA = [pb(f"psA{k}", [P, BANK]) for k in range(2)]
        psG = [pb(f"psG{k}", [P, BANK]) for k in range(2)]
        psT = [pb(f"psT{k}", [P, 4, P]) for k in range(2)]
        block = ctx.enter_context(nc.Block())

        @block.scalar
        def _(act):
            for c in range(NB):
                act.activation(gl[:, c * S:(c + 1) * S], net.yT[:, c * S:(c + 1) * S], ACT.Gelu,
                               bias=net.w["dr_b"][:, 0:1]).then_inc(s_ge, 1)
            for c in range(NCH):
                act.wait_ge(s_p, c + 1)
                if c >= 2:
                    act.wait_ge(s_m, c - 1)
                act.activation(sg[c % 2][:, :], psG[c % 2][:, :], ACT.Sigmoid, bias=net.w["glu_b"][:, 1:2]).then_inc(s_sg, 1)

        @block.tensor
        def _(pe):
            def turn(c):
                pe.wait_ge(s_m, c + 1)
                if c >= 2:
                    pe.wait_ge(s_x, c - 1)
                for t in range(4):
                    ins = pe.transpose(psT[c % 2][:, t, :], yy[c % 2][:, t * P:(t + 1) * P], net.identf[:, :])
                ins.then_inc(s_t, 1)

            for c in range(NCH):
                pe.wait_ge(s_ge, c // 2 + 1)
                if c >= 2:
                    pe.wait_ge(s_m, c - 1)
                src = gl[:, c * BANK:(c + 1) * BANK]
                pe.matmul(psA[c % 2][:, :], net.w["glu_w"][:, 0:D], src, start=True, stop=True)
                pe.matmul(psG[c % 2][:, :], net.w["glu_w"][:, D:2 * D], src, start=True, stop=True).then_inc(s_p, 1)
                if c:
                    turn(c - 1)
            turn(NCH - 1)

        @block.vector
        def _(dve):
            def add(c):
                dve.wait_ge(s_t, c + 1)
                X = net.X[:, 4 * c:4 * c + 4, :]
                dve.tensor_tensor(X, psT[c % 2][:, :, :], X, ALU.add).then_inc(s_x, 1)

            for c in range(NCH):
                dve.wait_ge(s_sg, c + 1)
                if c >= 2:
                    dve.wait_ge(s_t, c - 1)
                dve.scalar_tensor_tensor(yy[c % 2][:, :], psA[c % 2][:, :], net.w["glu_b"][:, 0:1], sg[c % 2][:, :],
                                         ALU.add, ALU.mult).then_inc(s_m, 1)
                if c:
                    add(c - 1)
            add(NCH - 1)


def store(nc, net):
    s_out = net.sem("stored")
    with nc.Block() as block:
        @block.sync
        def _(sp):
            sp.dma_start(net.out.rearrange("b (i p) d -> p (b i) d", p=P), net.X[:, :, :]).then_inc(s_out, 16)
            sp.wait_ge(s_out, 16)


SMALL = {
    "Wq": [P, D], "Wk": [P, GROUPS * DK], "Wv": [P, GROUPS * DK], "Wo": [P, D], "router_w": [P, NE],
    "norm1_w": [P, D], "norm2_w": [P, D], "router_b": [P, NE], "b1": [P, NE * FC], "b2": [P, NE * FC],
    "b3": [NE, D], "in_w": [P, 2 * DI], "x_w": [P, CI, DTR + 2 * NS], "dt_w": [DTR, DI], "out_w": [P, DI],
    "dr_w": [P, 2, D], "glu_w": [P, 2 * D], "conv_w": [P, CI, DC], "conv_b": [P, CI], "dt_b": [P, CI],
    "Dv": [P, CI], "A_log": [P, CI, NS], "dr_b": [P, 1], "glu_b": [P, 2], "ln_g": [P, D], "ln_b": [P, D],
    "cos": [P, TB, D // 2], "sin": [P, TB, D // 2],
}
EXPERTS = {"W1": [P, NE, FF], "W2": [P, NE, FF], "W3": [P, NE, FC, D]}


def program(nc, x, d, out):
    with ExitStack() as ctx:
        net = Net()
        sb = lambda n, s, t=F32: ctx.enter_context(nc.sbuf_tensor(n, s, t))

        def phase(build, *name):
            own = []

            def sem(n):
                own.append(nc.alloc_semaphore(name=n))
                return own[-1]

            net.sem = sem
            build(nc, net, *name)
            nc.clear_and_free_semaphores(own)
            nc.all_engine_barrier()

        net.x, net.d, net.out = x, d, out
        net.w = {n: sb(f"w_{n}", s) for n, s in SMALL.items()}
        net.X, net.U = sb("X", [P, NT, D]), sb("U", [P, NT, D])
        net.yT = sb("yT", [P, NT * P])
        net.VA = sb("VA", [P, NT, GROUPS, VW])
        net.comb = sb("comb", [P, NT, NE])
        net.identf, net.identb = sb("identf", [P, P]), sb("identb", [P, P], BF16)
        net.mask_st, net.mask_ts = sb("mask_st", [P, P], BF16), sb("mask_ts", [P, P], BF16)
        net.sel = sb("sel", [LVL * 2 * NS, 2 * NS, P], BF16)
        net.before, net.mhalf = sb("before", [P, NE, NE]), sb("mhalf", [P, TB])
        net.qd = nc.dram_tensor("q_parts", (NB, LVL, P, S), BF16, kind="Internal").ap()
        net.kd = nc.dram_tensor("k_parts", (NB, LVL, GROUPS * DK, S), BF16, kind="Internal").ap()
        net.nmd = nc.dram_tensor("max_parts", (2, LVL * 2 * TB, P), BF16, kind="Internal").ap()
        net.AO = net.yT[:, :].rearrange("p (i d) -> p i d", d=D)
        phase(setup)
        for k in range(2):
            with ExitStack() as layer:
                net.s_experts = layer.enter_context(nc.semaphore(f"f{k}_experts_loaded"))
                for n, s in EXPERTS.items():
                    net.w[n] = layer.enter_context(nc.sbuf_tensor(f"f{k}_{n}", s, F32))
                phase(attn_prep, f"f{k}p_")
                phase(attn_core, f"f{k}c_")
                phase(attn_out, f"f{k}o_")
                phase(moe, f"f{k}m_")
            if k == 0:
                phase(mamba_norm, "mn_")
                phase(mamba_scan, "ms_")
                phase(mamba_out, "mo_")
        phase(store)


def layouts(inputs):
    import numpy as np

    f = lambda n: np.asarray(inputs["L0_ffn_" + n])
    a = lambda n: np.asarray(inputs["L0_attn_" + n])
    rows = lambda v: np.broadcast_to(v[None, :], (P, v.shape[0]))
    cols = lambda v: v.reshape(-1, P).T
    d = {n: f(n) for n in ("Wq", "Wk", "Wv", "Wo", "router_w", "W1", "W2", "W3", "b3")}
    d |= {n: rows(f(n)) for n in ("norm1_w", "norm2_w", "router_b")}
    d |= {n: cols(f(n)) for n in ("b1", "b2")}
    d |= {"in_w": a("in_proj_w").T, "x_w": a("x_proj_w").T, "dt_w": a("dt_proj_w").T, "out_w": a("out_proj_w"),
          "dr_w": a("dim_reduce_w").T, "glu_w": a("glu_w").T, "conv_b": cols(a("conv_b")), "dt_b": cols(a("dt_proj_b")),
          "Dv": cols(a("D")), "dr_b": cols(a("dim_reduce_b")), "glu_b": cols(a("glu_b")),
          "conv_w": a("conv_w").reshape(CI, P, DC).transpose(1, 0, 2),
          "A_log": a("A_log").reshape(CI, P, NS).transpose(1, 0, 2), "ln_g": rows(a("ln_g")), "ln_b": rows(a("ln_b"))}
    half = D // 2
    theta = np.float32(1.0) / np.power(np.float32(10000.0), np.arange(half, dtype=np.float32) / np.float32(half))
    ang = np.arange(S, dtype=np.float32)[:, None] * theta[None, :]
    d |= {"cos": np.cos(ang).astype(np.float32), "sin": np.sin(ang).astype(np.float32)}
    return {n: np.ascontiguousarray(v) for n, v in d.items()}


def kernel(**inputs):
    import numpy as _np
    import concourse.bacc as _bacc
    from concourse import mybir as _mybir
    from concourse.bass_utils import run_bass_kernel_spmd as _run

    nc = _bacc.Bacc("TRN2", target_bir_lowering=False, num_devices=1)
    arrays = {"in_x": _np.ascontiguousarray(inputs["L0_attn_x"])}
    arrays |= {f"in_{n}": v for n, v in layouts(inputs).items()}
    args = {k: nc.dram_tensor(k, v.shape, _mybir.dt.from_np(v.dtype), kind="ExternalInput").ap()
            for k, v in arrays.items()}
    out = nc.dram_tensor("out_x", (NB, S, D), F32, kind="ExternalOutput").ap()
    program(nc, args["in_x"], {k[3:]: v for k, v in args.items()}, out)
    r = _run(nc, [arrays], core_ids=[0])
    return r.results[0]["out_x"]
```

```python
from contextlib import ExitStack

import concourse.bass as bass
from concourse import mybir

ALU = mybir.AluOpType
ACT = mybir.ActivationFunctionType
F32 = mybir.dt.float32
BF16 = mybir.dt.bfloat16
AX_X = mybir.AxisListType.X

P = 128
NB, S, D = 4, 1024, 128
TB = S // P
NT = NB * TB
HEADS, GROUPS, DK = 16, 4, 8
HPG = HEADS // GROUPS
NE, FF = 8, 512
FC = FF // P
DI, NS, DTR, DC = 256, 16, 64, 4
CI = DI // P
BANK = 512
LVL = 3
QROWS = 2 * LVL * DK
STACK = QROWS + LVL
VW = 32
MASKED = -1.0e30
RMS_EPS, LN_EPS = 1e-6, 1e-5


class Chain:

    def __init__(self, eng, sem, base=0):
        self.eng, self.sem, self.base, self.n = eng, sem, base, 0

    def link(self, ins):
        self.n += 1
        ins.then_inc(self.sem, 1)
        self.eng.wait_ge(self.sem, self.base + self.n)


class Net:
    pass


def p1_fills():
    fills = [[(3, 0, 512, 0)]] + [[(i, 0, 512, 0)] for i in range(4, 8)] + [[(7, 512, 1024, 0)]]
    for i in (6, 5, 4):
        w = (i + 1) * P - 512
        fills.append([(i, 512, 512 + w, 0), (6 - i, 0, 512 - w, w)])
    return fills


def p2_fills():
    right = [[(j, 512, 1024, 0)] for j in range(5)]
    left = [[(1, 128, 512, 0), (3, 384, 512, 384)], [(2, 256, 512, 0), (6, 768, 1024, 256)],
            [(5, 640, 1024, 0), (7, 896, 1024, 384)]]
    return [[(0, 0, 512, 0)]] + right + left


P1, P2 = p1_fills(), p2_fills()


def setup(nc, net):
    sem = net.sem
    s_ld, s_c, s_cv = sem("setup_loads"), sem("setup_consts"), sem("setup_conv")
    s_m = sem("setup_memsets")
    with nc.Block() as block:
        loads = [(net.X[:, :, :], net.x.rearrange("b (i p) d -> p (b i) d", p=P))]
        for name in ("Wq", "Wk", "Wv", "Wo", "router_w", "norm1_w", "norm2_w", "router_b", "b1", "b2", "b3",
                     "in_w", "dt_w", "out_w", "glu_w", "conv_w", "conv_b", "dt_b", "Dv", "A_log", "dr_b", "glu_b",
                     "ln_g", "ln_b"):
            loads.append((net.w[name][:], net.d[name]))
        loads.append((net.w["x_w"][:, :, :], net.d["x_w"].rearrange("(c p) n -> p c n", p=P)))
        loads.append((net.w["dr_w"][:, :, :], net.d["dr_w"].rearrange("(c p) n -> p c n", p=P)))
        for name in ("cos", "sin"):
            loads.append((net.w[name][:, :, :], net.d[name].rearrange("(i p) k -> p i k", p=P)))
        @block.sync
        def _(sp):
            for out, src in loads:
                sp.dma_start(out, src).then_inc(s_ld, 16)
            sp.wait_ge(s_ld, 16 * len(loads))

        @block.gpsimd
        def _(pool):
            pool.memset(net.identf[:, :], 0.0).then_inc(s_m, 1)
            pool.memset(net.mask_st[:, :], 0.0).then_inc(s_m, 1)
            pool.memset(net.mask_ts[:, :], 0.0).then_inc(s_m, 1)
            pool.memset(net.sel[:, :, :], 0.0).then_inc(s_m, 1)
            pool.memset(net.before[:, :, :], 1.0).then_inc(s_m, 1)
            pool.memset(net.mhalf[:, :], -0.5).then_inc(s_m, 1)
            pool.memset(net.VA[:, :, :, :], 1.0).then_inc(s_m, 1)
            pool.wait_ge(s_m, 7)
            pool.affine_select(out=net.identf[:, :], in_=net.identf[:, :], compare_op=ALU.not_equal, fill=1.0,
                               base=0, pattern=[[-1, P]], channel_multiplier=1).then_inc(s_c, 1)
            pool.affine_select(out=net.mask_st[:, :], in_=net.mask_st[:, :], compare_op=ALU.is_ge, fill=MASKED,
                               base=0, pattern=[[-1, P]], channel_multiplier=1).then_inc(s_c, 1)
            pool.affine_select(out=net.mask_ts[:, :], in_=net.mask_ts[:, :], compare_op=ALU.is_ge, fill=MASKED,
                               base=0, pattern=[[1, P]], channel_multiplier=-1).then_inc(s_c, 1)
            pool.affine_select(out=net.before[:, :, :], in_=net.before[:, :, :], compare_op=ALU.is_ge, fill=0.0,
                               base=-1, pattern=[[1, NE], [-1, NE]], channel_multiplier=0).then_inc(s_c, 1)
            for lvl in range(LVL):
                pool.affine_select(out=net.sel[:, :, :], in_=net.sel[:, :, :], compare_op=ALU.not_equal, fill=1.0,
                                   base=-2 * NS * lvl, pattern=[[-1, 2 * NS], [0, P]],
                                   channel_multiplier=1).then_inc(s_c, 1)
                pool.wait_ge(s_c, 5 + lvl)

        @block.vector
        def _(dve):
            dve.wait_ge(s_c, 1)
            dve.tensor_copy(net.identb[:, :], net.identf[:, :]).then_inc(s_cv, 1)


def norm_stats(dve, chain, src, stats, mv):
    for i in range(TB):
        ins = dve.bn_stats(stats[:, i, :], src(i))
    chain.link(ins)
    for i in range(TB):
        ins = dve.bn_aggr(mv[:, i, :], stats[:, i, :])
    chain.link(ins)


def attn_prep(nc, net, pre):
    sem = lambda n: net.sem(pre + n)
    s_chain, s_var, s_pow = sem("dve_chain"), sem("var_ready"), sem("rstd_ready")
    s_y, s_yr, s_rope, s_tp, s_xrt = sem("y_ready"), sem("rope_products"), sem("rope_ready"), sem("xr_turned"), sem("xrt_ready")
    s_qk, s_v, s_hi, s_r, s_mid, s_lo = sem("qk_ready"), sem("v_ready"), sem("hi_ready"), sem("rest_ready"), sem("mid_ready"), sem("lo_ready")
    s_ve, s_st = sem("v_stored"), sem("parts_stored")
    with ExitStack() as ctx:
        sb = lambda n, s, d=F32: ctx.enter_context(nc.sbuf_tensor(pre + n, s, d))
        pb = lambda n, s, d=F32: ctx.enter_context(nc.psum_tensor(pre + n, s, d))
        stats, mv = sb("stats", [P, TB, 6]), sb("mv", [P, TB, 2])
        var, rstd, msq = sb("var", [P, 2, TB]), sb("rstd", [P, 2, TB]), sb("msq", [P, TB])
        y = sb("y", [P, TB, D])
        xr = sb("xr", [P, TB, D])
        ra, rb = sb("ra", [P, TB, D]), sb("rb", [P, TB, D])
        xrT = sb("xrT", [P, S])
        qp, kp = sb("qp", [P, LVL, S], BF16), sb("kp", [GROUPS * DK, LVL, S], BF16)
        qr, kr = sb("qr", [P, S]), sb("kr", [GROUPS * DK, S])
        psT, psQ = pb("psT", [P, TB, P]), pb("psQ", [P, S])
        psK, psV = pb("psK", [GROUPS * DK, S]), pb("psV", [P, TB, GROUPS, DK])
        half = D // 2
        CH = 8
        block = ctx.enter_context(nc.Block())

        @block.vector
        def _(dve):
            for b in range(NB):
                ch = Chain(dve, s_chain, b * CH)
                X = net.X[:, bass.ds(b * TB, TB), :]
                U = net.U[:, bass.ds(b * TB, TB), :]
                norm_stats(dve, ch, lambda i: X[:, i, :], stats, mv)
                dve.tensor_scalar(var[:, 0, :], mv[:, :, 1], LN_EPS, None, ALU.add).then_inc(s_var, 1)
                dve.wait_ge(s_pow, 2 * b + 1)
                for i in range(TB):
                    ins = dve.tensor_scalar(U[:, i, :], X[:, i, :], mv[:, i, 0:1], rstd[:, 0, i:i + 1],
                                            ALU.subtract, ALU.mult)
                ch.link(ins)
                norm_stats(dve, ch, lambda i: U[:, i, :], stats, mv)
                ch.link(dve.tensor_tensor(msq[:, :], mv[:, :, 0], mv[:, :, 0], ALU.mult))
                dve.scalar_tensor_tensor(var[:, 1, :], msq[:, :], RMS_EPS, mv[:, :, 1],
                                         ALU.add, ALU.add).then_inc(s_var, 1)
                dve.wait_ge(s_pow, 2 * b + 2)
                for i in range(TB):
                    ins = dve.scalar_tensor_tensor(y[:, i, :], U[:, i, :], rstd[:, 1, i:i + 1],
                                                   net.w["norm1_w"][:, :], ALU.mult, ALU.mult)
                ins.then_inc(s_y, 1)
                dve.wait_ge(s_y, b + 1)
                cos, sin = net.w["cos"][:, :, :], net.w["sin"][:, :, :]
                dve.tensor_tensor(ra[:, :, 0:half], y[:, :, 0::2], cos, ALU.mult)
                dve.tensor_tensor(rb[:, :, 0:half], y[:, :, 1::2], sin, ALU.mult)
                ch.link(dve.tensor_tensor(ra[:, :, half:D], y[:, :, 0::2], sin, ALU.mult))
                dve.wait_ge(s_yr, b + 1)
                dve.wait_ge(s_tp, b + 1)
                dve.tensor_tensor(xr[:, :, 0:half], ra[:, :, 0:half], rb[:, :, 0:half], ALU.subtract)
                dve.tensor_tensor(xr[:, :, half:D], ra[:, :, half:D], rb[:, :, half:D], ALU.add).then_inc(s_rope, 1)
                dve.wait_ge(s_hi, 2 * b + 2)
                dve.wait_ge(s_lo, 2 * b + 1)
                dve.tensor_tensor(qr[:, :], psQ[:, :], qp[:, 0, :], ALU.subtract)
                dve.tensor_tensor(kr[:, :], psK[:, :], kp[:, 0, :], ALU.subtract).then_inc(s_r, 1)
                dve.wait_ge(s_v, b + 1)
                dve.tensor_copy(net.VA[:, bass.ds(b * TB, TB), :, 0:DK], psV[:, :, :, :]).then_inc(s_ve, 1)
                assert ch.n == CH - 1 or ch.n == CH, ch.n
                while ch.n < CH:
                    ch.link(dve.tensor_copy(msq[:, :], mv[:, :, 0]))

        @block.gpsimd
        def _(pool):
            pool.sem_inc(s_lo, 1)
            for b in range(NB):
                for k in range(2):
                    pool.wait_ge(s_var, 2 * b + k + 1)
                    pool.tensor_tensor(rstd[:, k, :], var[:, k, :], net.mhalf[:, 0:TB], ALU.pow).then_inc(s_pow, 1)
                pool.wait_ge(s_y, b + 1)
                pool.tensor_tensor(rb[:, :, half:D], y[:, :, 1::2], net.w["cos"][:, :, :], ALU.mult).then_inc(s_yr, 1)
                pool.wait_ge(s_r, b + 1)
                pool.tensor_copy(qp[:, 1, :], qr[:, :])
                pool.tensor_copy(kp[:, 1, :], kr[:, :]).then_inc(s_mid, 1)
                pool.wait_ge(s_mid, b + 1)
                pool.tensor_tensor(qp[:, 2, :], qr[:, :], qp[:, 1, :], ALU.subtract).then_inc(s_lo, 1)
                pool.tensor_tensor(kp[:, 2, :], kr[:, :], kp[:, 1, :], ALU.subtract).then_inc(s_lo, 1)

        @block.tensor
        def _(pe):
            pe.sem_inc(s_tp, 1)
            with pe.Fori(0, NB) as b:
                pe.wait_ge(s_rope, b + 1)
                for i in range(TB):
                    ins = pe.transpose(psT[:, i, :], xr[:, i, :], net.identf[:, :])
                ins.then_inc(s_tp, 1)
                pe.wait_ge(s_xrt, b + 1)
                for h in range(2):
                    pe.matmul(psQ[:, h * BANK:(h + 1) * BANK], net.w["Wq"][:, :], xrT[:, h * BANK:(h + 1) * BANK],
                              start=True, stop=True)
                    ins = pe.matmul(psK[:, h * BANK:(h + 1) * BANK], net.w["Wk"][:, :],
                                    xrT[:, h * BANK:(h + 1) * BANK], start=True, stop=True)
                ins.then_inc(s_qk, 1)
                for i in range(TB):
                    ins = pe.matmul(psV[:, i, :, :], xrT[:, i * P:(i + 1) * P], net.w["Wv"][:, :],
                                    start=True, stop=True)
                ins.then_inc(s_v, 1)
                pe.wait_ge(s_r, b + 1)
                pe.wait_ge(s_ve, b + 1)

        @block.scalar
        def _(act):
            act.sem_inc(s_st, 32)
            with act.Fori(0, NB) as b:
                act.wait_ge(s_tp, b + 2)
                act.activation(xrT[:, :], psT[:, :, :].rearrange("p i t -> p (i t)"), ACT.Copy).then_inc(s_xrt, 1)
                act.wait_ge(s_qk, b + 1)
                act.wait_ge(s_st, 32 * b + 32)
                act.activation(qp[:, 0, :], psQ[:, :], ACT.Copy).then_inc(s_hi, 1)
                act.activation(kp[:, 0, :], psK[:, :], ACT.Copy).then_inc(s_hi, 1)

        @block.sync
        def _(sp):
            for name in ("W1", "W2"):
                sp.dma_start(net.w[name][:, :, :], net.d[name].rearrange("e p f -> p e f")).then_inc(net.s_experts, 16)
            sp.dma_start(net.w["W3"][:, :, :, :],
                         net.d["W3"].rearrange("e (c p) n -> p e c n", p=P)).then_inc(net.s_experts, 16)
            for b in range(NB):
                sp.wait_ge(s_lo, 2 * b + 3)
                sp.dma_start(net.qd[bass.ds(b, 1), :, :, :].rearrange("o l p t -> p (o l) t"), qp[:, :, :]).then_inc(s_st, 16)
                sp.dma_start(net.kd[bass.ds(b, 1), :, :, :].rearrange("o l p t -> p (o l) t"), kp[:, :, :]).then_inc(s_st, 16)
                sp.wait_ge(s_st, 32 * b + 64)


def attn_core(nc, net, pre):
    sem = lambda n: net.sem(pre + n)
    s_ld = [sem(f"stacks_loaded{g}") for g in range(GROUPS)]
    s_nml = [sem(f"maxima_loaded{k}") for k in range(2)]
    s_p1f, s_p1r, s_p2f, s_ex = sem("rows_scored"), sem("rows_reduced"), sem("keys_scored"), sem("exp_done")
    s_pvf, s_ev, s_oT, s_on = sem("values_met"), sem("unit_copied"), sem("unit_turned"), sem("unit_normed")
    s_nb, s_tr, s_ntc = sem("maxima_split"), sem("maxima_turned"), sem("maxima_copied")
    s_nst, s_ch, s_init = sem("maxima_stored"), sem("core_chain"), sem("core_init")
    NUNIT, NF = NB * GROUPS, len(P2)
    NPAIR, NHEAD, SLOTS = 2 * NUNIT, HPG * NUNIT, HPG * NF
    LEAD = 6
    TURN_A, READ_A, TURN_O, READ_O, TURN_B, READ_B, TURN_P, READ_P = 3, 5, 9, 12, 21, 23, 27, 30
    with ExitStack() as ctx:
        sb = lambda n, s, d=F32: ctx.enter_context(nc.sbuf_tensor(pre + n, s, d))
        pb = lambda n, s, d=F32: ctx.enter_context(nc.psum_tensor(pre + n, s, d))
        QS = sb("QS", [P, HEADS // 2, S], BF16)
        KS = sb("KS", [P, GROUPS, S], BF16)
        probs = sb("probs", [P, HPG, 3, BANK])
        mx = sb("mx", [P, 2, 2, TB, 2])
        nm, nr = sb("nm", [P, 2 * TB]), sb("nr", [P, 2 * TB])
        nb = sb("nb", [P, 2, LVL, 2 * TB], BF16)
        nmT = sb("nmT", [LVL * 2 * TB, 2, P], BF16)
        oT = sb("oT", [P, S])
        rec = sb("rec", [P, 4, HPG, 1])
        ps1 = [pb(f"ps1_{k}", [P, BANK]) for k in range(2)]
        ps2 = [pb(f"ps2_{k}", [P, BANK]) for k in range(3)]
        psO = pb("psO", [P, S])
        psT = pb("psT", [P, BANK])
        psR = psT[0:LVL * 2 * TB, 0:P // 2].bitcast(BF16)
        block = ctx.enter_context(nc.Block())

        @block.gpsimd
        def _(pool):
            pool.memset(KS[:, :, :], 1.0).then_inc(s_init, 1)

        @block.sync
        def _(sp):
            def load_unit(u):
                b, g = divmod(u, GROUPS)
                if b:
                    sp.wait_ge(s_pvf, NF * (u - GROUPS + 1))
                for par in range(2):
                    r = 64 * par
                    for r0, n in ((0, 3), (24, 2), (40, 1)):
                        for l in range(n):
                            src = net.qd[b, l, :, :].rearrange("(k h d) t -> h d k t", h=2, d=DK)
                            sp.dma_start(QS[r + r0 + DK * l:r + r0 + DK * (l + 1), 2 * g:2 * g + 2, :],
                                         src[par, :, 2 * g:2 * g + 2, :]).then_inc(s_ld[g], 16)
                    for slot, l in enumerate((0, 0, 0, 1, 1, 2)):
                        sp.dma_start(KS[r + DK * slot:r + DK * (slot + 1), g, :],
                                     net.kd[b, l, DK * g:DK * (g + 1), :]).then_inc(s_ld[g], 16)

            def maxima(j):
                k = j % 2
                sp.wait_ge(s_ntc, j + 1)
                if j >= 2:
                    sp.wait_ge(s_nml[k], 32 * (j // 2))
                sp.dma_start(net.nmd[k, :, :], nmT[:, k, :]).then_inc(s_nst, 16)
                sp.wait_ge(s_nst, 16 * (j + 1))
                src = net.nmd[k, :, :].rearrange("(l h i) t -> h l (i t)", l=LVL, h=2)
                for par in range(2):
                    r = 64 * par + QROWS
                    sp.dma_start(QS[r:r + LVL, j % (HEADS // 2), :], src[par]).then_inc(s_nml[k], 16)

            sp.wait_ge(s_init, 1)
            for u in range(GROUPS):
                load_unit(u)
            for j in range(NPAIR):
                maxima(j)
                if j % 2 and j >= 3 and (j - 3) // 2 + GROUPS < NUNIT:
                    load_unit((j - 3) // 2 + GROUPS)

        @block.tensor
        def _(pe):
            def pass1(H, f):
                b, h = divmod(H, HEADS)
                r, k, g = 64 * (h % 2), h // 2, h // HPG
                n = len(P1) * H + f
                if h % HPG == 0 and f == 0:
                    pe.wait_ge(s_ld[g], 16 * 24 * (b + 1))
                if n >= 2:
                    pe.wait_ge(s_p1r, n - 1)
                bank = ps1[n % 2]
                for i, t0, t1, c in P1[f]:
                    diag = t1 == (i + 1) * P
                    w = t1 - t0
                    ins = pe.matmul(bank[:, c:c + w], QS[r:r + QROWS, k, i * P:(i + 1) * P],
                                    KS[r:r + QROWS, g, t0:t1], start=True, stop=not diag)
                    if diag:
                        ins = pe.matmul(bank[:, c + w - P:c + w], net.identb[:, :], net.mask_st[:, :],
                                        start=False, stop=True)
                ins.then_inc(s_p1f, 1)

            def pass2(u, f, hu):
                g = u % GROUPS
                r, k = 64 * (hu % 2), 2 * g + hu // 2
                n = SLOTS * u + HPG * f + hu
                if f == 0 and hu % 2 == 0:
                    pe.wait_ge(s_nml[hu // 2], 32 * (u + 1))
                if n >= 3:
                    pe.wait_ge(s_ex, n - 2)
                bank = ps2[n % 3]
                for j, s0, s1, c in P2[f]:
                    diag, w = s0 == j * P, s1 - s0
                    ins = pe.matmul(bank[:, c:c + w], KS[r:r + STACK, g, j * P:(j + 1) * P],
                                    QS[r:r + STACK, k, s0:s1], start=True, stop=not diag)
                    if diag:
                        ins = pe.matmul(bank[:, c:c + P], net.identb[:, :], net.mask_ts[:, :],
                                        start=False, stop=True)
                ins.then_inc(s_p2f, 1)

            def values(u, f):
                b, g = divmod(u, GROUPS)
                pe.wait_ge(s_ex, SLOTS * u + HPG * (f + 1))
                if f == 0 and u:
                    pe.wait_ge(s_ev, u)
                for j, s0, s1, c in P2[f]:
                    for hu in range(HPG):
                        ins = pe.matmul(psO[32 * hu:32 * hu + VW, s0:s1], net.VA[:, b * TB + j, g, :],
                                        probs[:, hu, f % 3, c:c + s1 - s0], start=(j == 0), stop=True,
                                        skip_group_check=True)
                ins.then_inc(s_pvf, 1)

            def turn_maxima(J):
                pe.wait_ge(s_nb, J + 1)
                if J >= 5:
                    pe.wait_ge(s_on, J - 4)
                elif J:
                    pe.wait_ge(s_ntc, J)
                pe.transpose(psR, nb[:, J % 2, :, :].rearrange("p l c -> p (l c)"), net.identb[:, :]).then_inc(s_tr, 1)

            def turn_unit(u, half):
                pe.wait_ge(s_ev, u + 1)
                pe.wait_ge(s_ntc, min(2 * u + 4 + half + 1, NPAIR))
                if 2 * u + 4 + half >= NPAIR and (u or half):
                    pe.wait_ge(s_on, 2 * u + half)
                for i in range(4):
                    c = (4 * half + i) * P
                    ins = pe.transpose(psT[:, i * P:(i + 1) * P], oT[:, c:c + P], net.identf[:, :])
                ins.then_inc(s_oT, 1)

            for H in range(LEAD):
                for f in range(len(P1)):
                    pass1(H, f)
                    if f == 3 and H in (2, 4):
                        turn_maxima(H // 2 - 1)
            for u in range(NUNIT + 1):
                for q in range(SLOTS):
                    if q == TURN_A and 2 * u + 2 < NPAIR:
                        turn_maxima(2 * u + 2)
                    if q == TURN_O and u:
                        turn_unit(u - 1, 0)
                    if q == TURN_B and 2 * u + 3 < NPAIR:
                        turn_maxima(2 * u + 3)
                    if q == TURN_P and u:
                        turn_unit(u - 1, 1)
                    if u < NUNIT:
                        pass2(u, q // HPG, q % HPG)
                        H = HPG * u + LEAD + q // len(P1)
                        if H < NHEAD:
                            pass1(H, q % len(P1))
                    if q % HPG == 1:
                        if q > HPG and u < NUNIT:
                            values(u, q // HPG - 1)
                        elif q < HPG and u:
                            values(u - 1, NF - 1)

        @block.scalar
        def _(act):
            for u in range(NUNIT + 1):
                for q in range(SLOTS):
                    f, hu = divmod(q, HPG)
                    if u < NUNIT:
                        n = SLOTS * u + q
                        if hu == 0 and NF * u + f >= 3:
                            act.wait_ge(s_pvf, NF * u + f - 2)
                        act.wait_ge(s_p2f, n + 1)
                        w = sum(s1 - s0 for _, s0, s1, _ in P2[f])
                        act.activation(probs[:, hu, f % 3, 0:w], ps2[n % 3][:, 0:w], ACT.Exp,
                                       scale=DK ** -0.5).then_inc(s_ex, 1)
                    if q == 2 and u:
                        act.wait_ge(s_pvf, NF * u)
                        if u >= 2:
                            act.wait_ge(s_oT, 2 * (u - 1))
                        act.activation(oT[:, :], psO[:, :], ACT.Copy).then_inc(s_ev, 1)

        @block.vector
        def _(dve):
            ch = Chain(dve, s_ch)

            def reduce_fill(H, f):
                J, hh = divmod(H, 2)
                n = len(P1) * H + f
                dve.wait_ge(s_p1f, n + 1)
                for i, t0, t1, c in P1[f]:
                    ins = dve.tensor_reduce(mx[:, J % 2, hh, i, t0 // 512:t0 // 512 + 1],
                                            ps1[n % 2][:, c:c + t1 - t0], AX_X, ALU.max)
                ins.then_inc(s_p1r, 1)
                if hh and f == len(P1) - 1:
                    split_maxima(J)

            def split_maxima(J):
                dve.wait_ge(s_p1r, len(P1) * 2 * (J + 1))
                if J >= 2:
                    dve.wait_ge(s_tr, J - 1)
                ch.link(dve.tensor_reduce(nm[:, :], mx[:, J % 2, :, :, :], AX_X, ALU.max, negate=True))
                part = nb[:, J % 2, :, :]
                ch.link(dve.tensor_copy(part[:, 0, :], nm[:, :]))
                ch.link(dve.tensor_tensor(nr[:, :], nm[:, :], part[:, 0, :], ALU.subtract))
                ch.link(dve.tensor_copy(part[:, 1, :], nr[:, :]))
                dve.tensor_tensor(part[:, 2, :], nr[:, :], part[:, 1, :], ALU.subtract).then_inc(s_nb, 1)

            def copy_maxima(J):
                dve.wait_ge(s_tr, J + 1)
                if J >= 2:
                    dve.wait_ge(s_nst, 16 * (J - 1))
                dve.tensor_copy(nmT[:, J % 2, :], psR).then_inc(s_ntc, 1)

            def norm_unit(u, half):
                b, g = divmod(u, GROUPS)
                dve.wait_ge(s_oT, 2 * u + half + 1)
                src = psT[:, :].rearrange("p (i h r) -> p i h r", i=4, h=HPG)
                ch.link(dve.reciprocal(rec[:, :, :, :], src[:, :, :, DK:DK + 1]))
                i0 = b * TB + 4 * half
                out = net.AO[:, i0:i0 + 4, g * HPG * DK:(g + 1) * HPG * DK].rearrange("p i (h d) -> p i h d", h=HPG)
                dve.tensor_tensor(out, src[:, :, :, 0:DK], rec[:, :, :, :].to_broadcast([P, 4, HPG, DK]),
                                  ALU.mult).then_inc(s_on, 1)

            ch.link(dve.memset(mx[:, :, :, :, :], -3.0e38))
            for H in range(LEAD):
                for f in range(len(P1)):
                    reduce_fill(H, f)
                    if f == 5 and H in (2, 4):
                        copy_maxima(H // 2 - 1)
            for u in range(NUNIT + 1):
                for q in range(SLOTS):
                    H = HPG * u + LEAD + q // len(P1)
                    if H < NHEAD and u < NUNIT:
                        reduce_fill(H, q % len(P1))
                    if q == READ_A and 2 * u + 2 < NPAIR:
                        copy_maxima(2 * u + 2)
                    if q == READ_O and u:
                        norm_unit(u - 1, 0)
                    if q == READ_B and 2 * u + 3 < NPAIR:
                        copy_maxima(2 * u + 3)
                    if q == READ_P and u:
                        norm_unit(u - 1, 1)


def attn_out(nc, net, pre):
    sem = lambda n: net.sem(pre + n)
    s_ch, s_aot, s_aoc, s_o, s_var, s_pow = sem("dve_chain"), sem("ao_turned"), sem("ao_copied"), sem("proj_done"), sem("var_ready"), sem("rstd_ready")
    s_y, s_yt, s_yc, s_lg, s_lgm, s_e = sem("y_ready"), sem("y_turned"), sem("y_copied"), sem("logits_ready"), sem("logits_shifted"), sem("exp_done")
    s_cb, s_ct, s_cc, s_b3, s_h = sem("comb_ready"), sem("comb_turned"), sem("comb_copied"), sem("b3_done"), sem("h_ready")
    CH = 16
    with ExitStack() as ctx:
        sb = lambda n, s, d=F32: ctx.enter_context(nc.sbuf_tensor(pre + n, s, d))
        pb = lambda n, s, d=F32: ctx.enter_context(nc.psum_tensor(pre + n, s, d))
        stats, mv = sb("stats", [P, TB, 6]), sb("mv", [P, TB, 2])
        var, rstd, msq = sb("var", [P, TB]), sb("rstd", [P, TB]), sb("msq", [P, TB])
        aoT, y = sb("aoT", [P, S]), sb("y", [P, TB, D])
        lg, lm = sb("lg", [P, TB, NE]), sb("lm", [P, TB, NE])
        top, ssum, rsum = sb("top", [P, TB, 1]), sb("ssum", [P, TB, 1]), sb("rsum", [P, TB, 1])
        gt, eq = sb("gt", [P, TB, NE, NE]), sb("eq", [P, TB, NE, NE])
        rank, ex = sb("rank", [P, TB, NE, 1]), sb("ex", [P, TB, NE])
        combT = sb("combT", [NE, TB, P])
        psA, psH, psY = pb("psA", [P, TB, P]), pb("psH", [P, TB, P]), pb("psY", [P, TB, P])
        psL, psC = pb("psL", [P, TB, NE]), pb("psC", [NE, 4, P])
        block = ctx.enter_context(nc.Block())

        @block.tensor
        def _(pe):
            with pe.Fori(0, NB) as b:
                pe.wait_ge(s_h, 2 * b + 1)
                for i in range(TB):
                    ins = pe.transpose(psA[:, i, :], y[:, i, :], net.identf[:, :])
                ins.then_inc(s_aot, 1)
                pe.wait_ge(s_aoc, b + 1)
                for i in range(TB):
                    ins = pe.matmul(psH[:, i, :], aoT[:, i * P:(i + 1) * P], net.w["Wo"][:, :], start=True, stop=True)
                ins.then_inc(s_o, 1)
                pe.wait_ge(s_y, b + 1)
                for i in range(TB):
                    ins = pe.transpose(psY[:, i, :], y[:, i, :], net.identf[:, :])
                ins.then_inc(s_yt, 1)
                pe.wait_ge(s_yc, b + 1)
                for i in range(TB):
                    ins = pe.matmul(psL[:, i, :], aoT[:, i * P:(i + 1) * P], net.w["router_w"][:, :],
                                    start=True, stop=True)
                ins.then_inc(s_lg, 1)
                pe.wait_ge(s_cb, b + 1)
                for half in range(2):
                    if half:
                        pe.wait_ge(s_cc, 2 * b + 1)
                    for i in range(4):
                        ins = pe.transpose(psC[:, i, :], ex[:, half * 4 + i, :], net.identf[:, :])
                    ins.then_inc(s_ct, 1)
                pe.wait_ge(s_cc, 2 * b + 2)
                for i in range(TB):
                    ins = pe.matmul(psH[:, i, :], combT[:, i, :], net.w["b3"][:, :], start=True, stop=True)
                ins.then_inc(s_b3, 1)

        @block.scalar
        def _(act):
            with act.Fori(0, NB) as b:
                act.wait_ge(s_aot, b + 1)
                act.activation(aoT[:, :], psA[:, :, :].rearrange("p i t -> p (i t)"), ACT.Copy).then_inc(s_aoc, 1)
                act.wait_ge(s_yt, b + 1)
                act.activation(net.yT[:, bass.ds(b * S, S)], psY[:, :, :].rearrange("p i t -> p (i t)"), ACT.Copy)
                act.wait_ge(s_o, b + 1)
                act.activation(aoT[:, :], psY[:, :, :].rearrange("p i t -> p (i t)"), ACT.Copy).then_inc(s_yc, 1)
                act.wait_ge(s_lgm, b + 1)
                act.activation(ex[:, :, :], lm[:, :, :], ACT.Exp).then_inc(s_e, 1)
                for half in range(2):
                    act.wait_ge(s_ct, 2 * b + half + 1)
                    act.activation(combT[:, half * 4:half * 4 + 4, :], psC[:, :, :], ACT.Copy).then_inc(s_cc, 1)

        @block.gpsimd
        def _(pool):
            for b in range(NB):
                pool.wait_ge(s_var, b + 1)
                pool.tensor_tensor(rstd[:, :], var[:, :], net.mhalf[:, 0:TB], ALU.pow).then_inc(s_pow, 1)

        @block.vector
        def _(dve):
            for b in range(NB):
                ch = Chain(dve, s_ch, b * CH)
                U = net.U[:, bass.ds(b * TB, TB), :]
                comb = net.comb[:, bass.ds(b * TB, TB), :]
                dve.tensor_copy(y[:, :, :], net.AO[:, bass.ds(b * TB, TB), :]).then_inc(s_h, 1)
                dve.wait_ge(s_o, b + 1)
                ch.link(dve.tensor_tensor(U, psH[:, :, :], U, ALU.add))
                norm_stats(dve, ch, lambda i: U[:, i, :], stats, mv)
                ch.link(dve.tensor_tensor(msq[:, :], mv[:, :, 0], mv[:, :, 0], ALU.mult))
                dve.scalar_tensor_tensor(var[:, :], msq[:, :], RMS_EPS, mv[:, :, 1], ALU.add, ALU.add).then_inc(s_var, 1)
                dve.wait_ge(s_pow, b + 1)
                for i in range(TB):
                    ins = dve.scalar_tensor_tensor(y[:, i, :], U[:, i, :], rstd[:, i:i + 1], net.w["norm2_w"][:, :],
                                                   ALU.mult, ALU.mult)
                ins.then_inc(s_y, 1)
                dve.wait_ge(s_lg, b + 1)
                rbias = net.w["router_b"][:, :].rearrange("p (o e) -> p o e", o=1).to_broadcast([P, TB, NE])
                ch.link(dve.tensor_tensor(lg[:, :, :], psL[:, :, :], rbias, ALU.add))
                mine = lg[:, :, :].rearrange("p i (e o) -> p i e o", o=1).to_broadcast([P, TB, NE, NE])
                other = lg[:, :, :].rearrange("p i (o e) -> p i o e", o=1).to_broadcast([P, TB, NE, NE])
                before = net.before[:, :, :].rearrange("p (o e) f -> p o e f", o=1).to_broadcast([P, TB, NE, NE])
                dve.tensor_tensor(gt[:, :, :, :], other, mine, ALU.is_gt)
                dve.tensor_tensor(eq[:, :, :, :], other, mine, ALU.is_equal)
                ch.link(dve.tensor_reduce(top[:, :, :], lg[:, :, :], AX_X, ALU.max))
                dve.tensor_tensor(lm[:, :, :], lg[:, :, :], top[:, :, :].to_broadcast([P, TB, NE]),
                                  ALU.subtract).then_inc(s_lgm, 1)
                ch.link(dve.tensor_tensor(eq[:, :, :, :], eq[:, :, :, :], before, ALU.mult))
                ch.link(dve.tensor_tensor(gt[:, :, :, :], gt[:, :, :, :], eq[:, :, :, :], ALU.add))
                ch.link(dve.tensor_reduce(rank[:, :, :, :], gt[:, :, :, :], AX_X, ALU.add))
                dve.wait_ge(s_e, b + 1)
                rk = rank[:, :, :, :].rearrange("p i e o -> p i (e o)")
                ch.link(dve.scalar_tensor_tensor(lm[:, :, :], rk, 1.5, ex[:, :, :], ALU.is_lt, ALU.mult))
                ch.link(dve.tensor_reduce(ssum[:, :, :], lm[:, :, :], AX_X, ALU.add))
                ch.link(dve.reciprocal(rsum[:, :, :], ssum[:, :, :]))
                dve.tensor_tensor(comb, lm[:, :, :], rsum[:, :, :].to_broadcast([P, TB, NE]), ALU.mult)
                dve.tensor_tensor(ex[:, :, :], lm[:, :, :], rsum[:, :, :].to_broadcast([P, TB, NE]),
                                  ALU.mult).then_inc(s_cb, 1)
                dve.wait_ge(s_b3, b + 1)
                dve.tensor_tensor(U, psH[:, :, :], U, ALU.add).then_inc(s_h, 1)
                while ch.n < CH:
                    ch.link(dve.tensor_copy(msq[:, :], mv[:, :, 0]))


def moe(nc, net, pre):
    sem = lambda n: net.sem(pre + n)
    s_h, s_sil, s_g, s_eo, s_acc, s_x = sem("h_ready"), sem("silu_done"), sem("gated"), sem("expert_out"), sem("expert_added"), sem("x_done")
    NCH = NT // 4
    N = NE * FC
    CREDIT = 2
    with ExitStack() as ctx:
        sb = lambda n, s, d=F32: ctx.enter_context(nc.sbuf_tensor(pre + n, s, d))
        pb = lambda n, s, d=F32: ctx.enter_context(nc.psum_tensor(pre + n, s, d))
        sil = [sb(f"sil{k}", [P, BANK]) for k in range(2)]
        hb = [sb(f"hb{k}", [P, FC, BANK]) for k in range(2)]
        ps1 = [pb(f"h1_{k}", [P, BANK]) for k in range(2)]
        ps2 = [pb(f"h2_{k}", [P, BANK]) for k in range(2)]
        pse = [pb(f"eo_{k}", [P, 4, D]) for k in range(2)]
        block = ctx.enter_context(nc.Block())

        @block.tensor
        def _(pe):
            pe.sem_inc(s_eo, CREDIT)
            pe.wait_ge(net.s_experts, 48)
            with pe.Fori(0, NCH) as c:
                xs = net.yT[:, bass.ds(c * BANK, BANK)]

                def up(e, fc):
                    n = e * FC + fc
                    pe.wait_ge(s_g, N * c + n + 1)
                    cols = slice(fc * P, (fc + 1) * P)
                    pe.matmul(ps1[n % 2][:, :], net.w["W1"][:, e, cols], xs, start=True, stop=True)
                    pe.matmul(ps2[n % 2][:, :], net.w["W2"][:, e, cols], xs, start=True, stop=True).then_inc(s_h, 1)

                def down(e):
                    pe.wait_ge(s_g, N * c + (e + 1) * FC + CREDIT)
                    pe.wait_ge(s_acc, NE * c + e + 1)
                    for t in range(4):
                        for fc in range(FC):
                            ins = pe.matmul(pse[e % 2][:, t, :], hb[e % 2][:, fc, t * P:(t + 1) * P],
                                            net.w["W3"][:, e, fc, :], start=(fc == 0), stop=(fc == FC - 1))
                    ins.then_inc(s_eo, 1)

                for e in range(NE):
                    for fc in range(FC):
                        up(e, fc)
                        if fc == 1 and e:
                            down(e - 1)
                down(NE - 1)

        @block.scalar
        def _(act):
            with act.Fori(0, NCH) as c:
                for n in range(N):
                    act.wait_ge(s_h, N * c + n + 1)
                    act.wait_ge(s_g, N * c + n + 1)
                    act.activation(sil[n % 2][:, :], ps1[n % 2][:, :], ACT.Silu,
                                   bias=net.w["b1"][:, n:n + 1]).then_inc(s_sil, 1)

        @block.vector
        def _(dve):
            dve.sem_inc(s_g, CREDIT)
            dve.sem_inc(s_acc, CREDIT)
            with dve.Fori(0, NCH) as c:
                H = net.U[:, bass.ds(c * 4, 4), :]
                X = net.X[:, bass.ds(c * 4, 4), :]
                comb = net.comb[:, bass.ds(c * 4, 4), :]

                def add(e):
                    dve.wait_ge(s_eo, NE * c + e + 1 + CREDIT)
                    dve.wait_ge(s_acc, NE * c + e + CREDIT)
                    for t in range(4):
                        ins = dve.scalar_tensor_tensor(H[:, t, :], pse[e % 2][:, t, :], comb[:, t, e:e + 1],
                                                       H[:, t, :], ALU.mult, ALU.add)
                    ins.then_inc(s_acc, 1)

                for e in range(NE):
                    dve.wait_ge(s_eo, NE * c + e + 1)
                    for fc in range(FC):
                        n = e * FC + fc
                        dve.wait_ge(s_sil, N * c + n + 1)
                        dve.scalar_tensor_tensor(hb[e % 2][:, fc, :], ps2[n % 2][:, :], net.w["b2"][:, n:n + 1],
                                                 sil[n % 2][:, :], ALU.add, ALU.mult).then_inc(s_g, 1)
                        if fc == 3 and e:
                            add(e - 1)
                add(NE - 1)
                dve.wait_ge(s_acc, NE * c + NE + CREDIT)
                dve.scalar_tensor_tensor(X, H, 0.5, X, ALU.mult, ALU.add).then_inc(s_x, 1)


def mamba_norm(nc, net, pre):
    sem = lambda n: net.sem(pre + n)
    s_ch, s_var, s_pow, s_y, s_yg, s_yb, s_t, s_c = (sem(n) for n in (
        "dve_chain", "var_ready", "rstd_ready", "y_ready", "y_scaled", "y_shifted", "y_turned", "y_copied"))
    CH = 6
    with ExitStack() as ctx:
        sb = lambda n, s, d=F32: ctx.enter_context(nc.sbuf_tensor(pre + n, s, d))
        pb = lambda n, s, d=F32: ctx.enter_context(nc.psum_tensor(pre + n, s, d))
        stats, mv = sb("stats", [P, TB, 6]), sb("mv", [P, TB, 2])
        var, rstd = sb("var", [P, 2, TB]), sb("rstd", [P, 2, TB])
        y = sb("y", [P, TB, D])
        psT = pb("psT", [P, TB, P])
        block = ctx.enter_context(nc.Block())

        @block.vector
        def _(dve):
            for b in range(NB):
                ch = Chain(dve, s_ch, b * CH)
                X = net.X[:, bass.ds(b * TB, TB), :]
                U = net.U[:, bass.ds(b * TB, TB), :]
                for k, src in enumerate((X, U)):
                    norm_stats(dve, ch, lambda i: src[:, i, :], stats, mv)
                    dve.tensor_scalar(var[:, k, :], mv[:, :, 1], LN_EPS, None, ALU.add).then_inc(s_var, 1)
                    dve.wait_ge(s_pow, 2 * b + k + 1)
                    if k == 1:
                        dve.wait_ge(s_t, b + 1)
                    for i in range(TB):
                        out = U[:, i, :] if k == 0 else y[:, i, :]
                        ins = dve.tensor_scalar(out, src[:, i, :], mv[:, i, 0:1], rstd[:, k, i:i + 1],
                                                ALU.subtract, ALU.mult)
                    if k == 0:
                        ch.link(ins)
                ins.then_inc(s_y, 1)
                ch.link(dve.tensor_tensor(X, X, U, ALU.add))

        @block.gpsimd
        def _(pool):
            for b in range(NB):
                for k in range(2):
                    pool.wait_ge(s_var, 2 * b + k + 1)
                    pool.tensor_tensor(rstd[:, k, :], var[:, k, :], net.mhalf[:, 0:TB], ALU.pow).then_inc(s_pow, 1)
                pool.wait_ge(s_y, b + 1)
                g = net.w["ln_g"][:, :].rearrange("p (o d) -> p o d", o=1).to_broadcast([P, TB, D])
                bb = net.w["ln_b"][:, :].rearrange("p (o d) -> p o d", o=1).to_broadcast([P, TB, D])
                pool.tensor_tensor(y[:, :, :], y[:, :, :], g, ALU.mult).then_inc(s_yg, 1)
                pool.wait_ge(s_yg, b + 1)
                pool.tensor_tensor(y[:, :, :], y[:, :, :], bb, ALU.add).then_inc(s_yb, 1)

        @block.tensor
        def _(pe):
            pe.sem_inc(s_t, 1)
            with pe.Fori(0, NB) as b:
                pe.wait_ge(s_yb, b + 1)
                pe.wait_ge(s_c, b + 1)
                for i in range(TB):
                    ins = pe.transpose(psT[:, i, :], y[:, i, :], net.identf[:, :])
                ins.then_inc(s_t, 1)

        @block.scalar
        def _(act):
            act.sem_inc(s_c, 1)
            with act.Fori(0, NB) as b:
                act.wait_ge(s_t, b + 2)
                act.activation(net.yT[:, bass.ds(b * S, S)], psT[:, :, :].rearrange("p i t -> p (i t)"),
                               ACT.Copy).then_inc(s_c, 1)


def mamba_scan(nc, net, pre):
    sem = lambda n: net.sem(pre + n)
    s_w0, s_w1, s_w2, s_w3 = sem("weights_product"), sem("weights_copied"), sem("a_exp"), sem("a_ready")
    s_pad = sem("pads_zero")
    s_in, s_ev, s_conv, s_cc = sem("in_proj"), sem("in_read"), sem("conv_done"), sem("conv_chain")
    s_u, s_xp, s_hi, s_r, s_mid, s_bc = sem("u_ready"), sem("x_proj"), sem("bc_hi"), sem("bc_rest"), sem("bc_mid"), sem("bc_ready")
    s_dts, s_dp, s_ab, s_sp, s_mxd, s_dl, s_du = sem("dt_ready"), sem("dt_proj"), sem("sp_chain"), sem("sp_log"), sem("sp_max"), sem("delta_ready"), sem("du_ready")
    s_B, s_C, s_Cc, s_da, s_bx, s_sc = sem("b_spread"), sem("c_spread"), sem("c_copied"), sem("decay_ready"), sem("input_ready"), sem("scanned")
    s_hc, s_y, s_yr, s_g, s_o, s_oc = sem("hc_ready"), sem("y_added"), sem("y_read"), sem("gated"), sem("out_proj"), sem("out_copied")
    PAD = DC - 1
    with ExitStack() as ctx:
        sb = lambda n, s, d=F32: ctx.enter_context(nc.sbuf_tensor(pre + n, s, d))
        pb = lambda n, s, d=F32: ctx.enter_context(nc.psum_tensor(pre + n, s, d))
        MT = sb("MT", [P, 2, CI, D])
        negA = sb("negA", [P, CI, NS])
        diagD = sb("diagD", [P, CI, P])
        xi = sb("xi", [P, CI, S + 2 * PAD])
        sz = sb("sz", [P, CI, S])
        u = sb("u", [P, CI, S])
        cv = sb("cv", [P, CI, S])
        bc = sb("bc", [LVL * 2 * NS, S], BF16)
        delta, du = sb("delta", [P, CI, S]), sb("du", [P, CI, S])
        dA = [sb(f"dA{k}", [P, S]) for k in range(2)]
        bx = [sb(f"bx{k}", [P, S]) for k in range(2)]
        hs = [sb(f"hs{k}", [P, S]) for k in range(2)]
        hc = [sb(f"hc{k}", [P, S]) for k in range(2)]
        Cs = sb("Cs", [P, 2, S])
        dts, bcr = hc[0][0:DTR, :], hc[1]
        g = net.U[:, :, :].rearrange("p (k c i) d -> p k c (i d)", k=2, c=CI)
        psB, psC = pb("psB", [P, S]), pb("psC", [P, S])
        psY = [pb(f"psY{c}", [P, S]) for c in range(CI)]
        block = ctx.enter_context(nc.Block())
        halves = [slice(0, BANK), slice(BANK, S)]
        NIN = 2 * CI
        ND = NB * 2

        @block.tensor
        def _(pe):
            for k in range(2):
                for c in range(CI):
                    ins = pe.matmul(psB[:, (k * CI + c) * P:(k * CI + c + 1) * P], net.w["out_w"][:, c * P:(c + 1) * P],
                                    net.w["dr_w"][:, k, :], start=True, stop=True)
            ins.then_inc(s_w0, 1)
            pe.wait_ge(s_w1, 1)
            pe.sem_inc(s_y, 2)
            with pe.Fori(0, NB) as b:
                xs = net.yT[:, bass.ds(b * S, S)]
                pe.wait_ge(s_oc, b + 1)
                for m in range(NIN):
                    out = (psY + [psB, psC])[m]
                    for hf in halves:
                        ins = pe.matmul(out[:, hf], net.w["in_w"][:, m * P:(m + 1) * P], xs[:, hf],
                                        start=True, stop=True)
                    ins.then_inc(s_in, 1)
                for d in range(2):
                    st = 2 * b + d
                    pe.wait_ge(s_u, CI * st + CI)
                    pe.wait_ge(s_ev, NIN * b + NIN)
                    for hf in halves:
                        for c in range(CI):
                            ins = pe.matmul(psB[0:DTR + 2 * NS, hf], net.w["x_w"][:, c, :], u[:, c, hf],
                                            start=(c == 0), stop=(c == CI - 1))
                    ins.then_inc(s_xp, 1)
                    pe.wait_ge(s_dts, st + 1)
                    for c in range(CI):
                        for hf in halves:
                            ins = pe.matmul(psY[c][:, hf], net.w["dt_w"][:, c * P:(c + 1) * P], dts[:, hf],
                                            start=True, stop=True)
                    ins.then_inc(s_dp, 1)
                    pe.wait_ge(s_mxd, CI * st + CI)
                    pe.wait_ge(s_ab, 2 * CI * st + 2 * CI)
                    for c in range(CI):
                        for hf in halves:
                            pe.matmul(psY[c][:, hf], diagD[:, c, :], u[:, c, hf], start=True, stop=False,
                                      skip_group_check=True)
                    pe.wait_ge(s_bc, st + 1)

                    def spread(n):
                        k = NS * st + n
                        if n:
                            pe.wait_ge(s_bx, CI * k)
                        for hf in halves:
                            ins = pe.matmul(psB[:, hf], net.sel[:, n, :], bc[:, hf], start=True, stop=True)
                        ins.then_inc(s_B, 1)
                        if n:
                            pe.wait_ge(s_Cc, k)
                        for hf in halves:
                            ins = pe.matmul(psC[:, hf], net.sel[:, NS + n, :], bc[:, hf], start=True, stop=True)
                        ins.then_inc(s_C, 1)

                    def add_y(n):
                        k = NS * st + n
                        for c in range(CI):
                            pe.wait_ge(s_hc, CI * k + c + 1)
                            for hf in halves:
                                ins = pe.matmul(psY[c][:, hf], net.identf[:, :], hc[c][:, hf], start=False,
                                                stop=(n == NS - 1), skip_group_check=True)
                            ins.then_inc(s_y, 1)

                    for n in range(NS):
                        spread(n)
                        if n:
                            add_y(n - 1)
                    add_y(NS - 1)
                pe.wait_ge(s_g, 2 * CI * b + 2 * CI)
                for hf in halves:
                    for k in range(2 * CI):
                        ins = pe.matmul(psB[:, hf], MT[:, k // CI, k % CI, :], g[:, k // CI, k % CI, hf],
                                        start=(k == 0), stop=(k == 2 * CI - 1))
                ins.then_inc(s_o, 1)

        @block.scalar
        def _(act):
            act.activation(negA[:, :, :], net.w["A_log"][:, :, :], ACT.Exp).then_inc(s_w2, 1)
            act.wait_ge(s_w0, 1)
            act.activation(MT[:, :, :, :].rearrange("p k c o -> p (k c o)"), psB[:, 0:2 * CI * P], ACT.Copy).then_inc(s_w1, 1)
            act.sem_inc(s_oc, 1)
            act.wait_ge(s_w3, 1)
            with act.Fori(0, NB) as b:
                for m in range(CI):
                    act.wait_ge(s_in, NIN * b + m + 1)
                    act.activation(xi[:, m, PAD:PAD + S], psY[m][:, :], ACT.Copy).then_inc(s_ev, 1)
                for m in range(CI):
                    act.wait_ge(s_in, NIN * b + CI + m + 1)
                    act.activation(sz[:, m, :], [psB, psC][m][:, :], ACT.Silu).then_inc(s_ev, 1)
                for d in range(2):
                    st = 2 * b + d
                    for c in range(CI):
                        act.wait_ge(s_conv, CI * st + c + 1)
                        act.activation(u[:, c, :], cv[:, c, :], ACT.Silu).then_inc(s_u, 1)
                    act.wait_ge(s_xp, st + 1)
                    act.activation(dts[:, :], psB[0:DTR, :], ACT.Copy).then_inc(s_dts, 1)
                    act.activation(bc[0:2 * NS, :], psB[DTR:DTR + 2 * NS, :], ACT.Copy).then_inc(s_hi, 1)
                    act.wait_ge(s_dp, st + 1)
                    for c in range(CI):
                        act.activation(cv[:, c, :], psY[c][:, :], ACT.Abs, bias=net.w["dt_b"][:, c:c + 1]).then_inc(s_ab, 1)
                    act.wait_ge(s_ab, 2 * CI * st + CI)
                    for c in range(CI):
                        act.activation(cv[:, c, :], cv[:, c, :], ACT.Exp, scale=-1.0).then_inc(s_ab, 1)
                    act.wait_ge(s_ab, 2 * CI * st + 2 * CI)
                    for c in range(CI):
                        act.activation(cv[:, c, :], cv[:, c, :], ACT.Ln, bias=1.0).then_inc(s_sp, 1)
                    for n in range(NS):
                        k = NS * st + n
                        for c in range(CI):
                            if c == 0 and n == 0:
                                act.wait_ge(s_dl, CI * st + CI)
                            if n:
                                act.wait_ge(s_sc, CI * (k - 1) + c + 1)
                            act.activation(dA[c][:, :], delta[:, c, :], ACT.Exp,
                                           scale=negA[:, c, n:n + 1]).then_inc(s_da, 1)
                        act.wait_ge(s_C, k + 1)
                        if n >= 2:
                            act.wait_ge(s_hc, CI * (k - 1))
                        act.activation(Cs[:, n % 2, :], psC[:, :], ACT.Copy).then_inc(s_Cc, 1)
                act.wait_ge(s_o, b + 1)
                act.activation(net.yT[:, bass.ds(b * S, S)], psB[:, :], ACT.Copy).then_inc(s_oc, 1)

        @block.vector
        def _(dve):
            dve.memset(xi[:, :, 0:PAD], 0.0).then_inc(s_pad, 1)
            dve.memset(xi[:, :, PAD + S:], 0.0).then_inc(s_pad, 1)
            dve.wait_ge(s_pad, 2)
            dve.wait_ge(s_w2, 1)
            dve.tensor_scalar(negA[:, :, :], negA[:, :, :], -1.0, None, ALU.mult).then_inc(s_pad, 1)
            for c in range(CI):
                ins = dve.tensor_scalar(diagD[:, c, :], net.identf[:, :], net.w["Dv"][:, c:c + 1], None, ALU.mult)
            ins.then_inc(s_w3, 1)
            with dve.Fori(0, NB) as b:
                for d in range(2):
                    st = 2 * b + d
                    for k in range(DC):
                        for c in range(CI):
                            if d == 0 and k == 0:
                                dve.wait_ge(s_ev, NIN * b + c + 1)
                            o = k if d == 0 else 2 * PAD - k
                            tap = net.w["conv_w"][:, c, k:k + 1]
                            src = xi[:, c, o:o + S]
                            if k == 0:
                                ins = dve.tensor_scalar(cv[:, c, :], src, tap, net.w["conv_b"][:, c:c + 1], ALU.mult, ALU.add)
                            else:
                                dve.wait_ge(s_cc, (DC - 1) * CI * st + (k - 1) * CI + c + 1)
                                ins = dve.scalar_tensor_tensor(cv[:, c, :], src, tap, cv[:, c, :], ALU.mult, ALU.add)
                            ins.then_inc(s_conv if k == DC - 1 else s_cc, 1)
                    dve.wait_ge(s_hi, st + 1)
                    dve.tensor_tensor(bcr[2 * NS:4 * NS, :], psB[DTR:DTR + 2 * NS, :], bc[0:2 * NS, :],
                                      ALU.subtract).then_inc(s_r, 1)
                    dve.wait_ge(s_r, st + 1)
                    dve.tensor_copy(bc[2 * NS:4 * NS, :], bcr[2 * NS:4 * NS, :]).then_inc(s_mid, 1)
                    dve.wait_ge(s_mid, st + 1)
                    dve.tensor_tensor(bc[4 * NS:6 * NS, :], bcr[2 * NS:4 * NS, :], bc[2 * NS:4 * NS, :],
                                      ALU.subtract).then_inc(s_bc, 1)
                    dve.wait_ge(s_dp, st + 1)
                    dve.wait_ge(s_ab, 2 * CI * st + CI)
                    for c in range(CI):
                        ins = dve.tensor_scalar(delta[:, c, :], psY[c][:, :], net.w["dt_b"][:, c:c + 1], 0.0,
                                                ALU.add, ALU.max).then_inc(s_mxd, 1)
                    dve.wait_ge(s_mxd, CI * st + CI)
                    for c in range(CI):
                        dve.wait_ge(s_sp, CI * st + c + 1)
                        dve.tensor_tensor(delta[:, c, :], delta[:, c, :], cv[:, c, :], ALU.add).then_inc(s_dl, 1)
                    for c in range(CI):
                        dve.wait_ge(s_dl, CI * st + c + 1)
                        dve.tensor_tensor(du[:, c, :], delta[:, c, :], u[:, c, :], ALU.mult).then_inc(s_du, 1)
                    dve.wait_ge(s_du, CI * st + CI)
                    way = slice(None) if d == 0 else slice(None, None, -1)
                    for n in range(NS):
                        k = NS * st + n
                        dve.wait_ge(s_B, k + 1)
                        for c in range(CI):
                            if n:
                                dve.wait_ge(s_sc, CI * (k - 1) + c + 1)
                            dve.tensor_tensor(bx[c][:, :], psB[:, :], du[:, c, :], ALU.mult).then_inc(s_bx, 1)
                        for c in range(CI):
                            dve.wait_ge(s_bx, CI * k + c + 1)
                            dve.wait_ge(s_da, CI * k + c + 1)
                            if n:
                                dve.wait_ge(s_hc, CI * (k - 1) + c + 1)
                            dve.tensor_tensor_scan(hs[c][:, way], dA[c][:, way], bx[c][:, way], 0.0,
                                                   ALU.mult, ALU.add).then_inc(s_sc, 1)
                    for c in range(CI):
                        dve.wait_ge(s_y, CI * NS * st + CI * NS + 2)
                        dve.tensor_tensor(g[:, d, c, :], psY[c][:, :], sz[:, c, :], ALU.mult).then_inc(s_g, 1)

        @block.gpsimd
        def _(pool):
            with pool.Fori(0, NB) as b:
                for d in range(2):
                    st = 2 * b + d
                    for n in range(NS):
                        k = NS * st + n
                        pool.wait_ge(s_Cc, k + 1)
                        for c in range(CI):
                            pool.wait_ge(s_sc, CI * k + c + 1)
                            pool.wait_ge(s_y, CI * k + c + 1)
                            pool.tensor_tensor(hc[c][:, :], hs[c][:, :], Cs[:, n % 2, :], ALU.mult).then_inc(s_hc, 1)


def mamba_out(nc, net, pre):
    sem = lambda n: net.sem(pre + n)
    s_ge, s_p, s_sg, s_m, s_t, s_x = (sem(n) for n in ("gelu_done", "glu_ready", "sigmoid_done", "glu_done", "turned", "added"))
    NCH = NT // 4
    with ExitStack() as ctx:
        sb = lambda n, s, d=F32: ctx.enter_context(nc.sbuf_tensor(pre + n, s, d))
        pb = lambda n, s, d=F32: ctx.enter_context(nc.psum_tensor(pre + n, s, d))
        gl = sb("gl", [P, NT * P])
        sg = [sb(f"sg{k}", [P, BANK]) for k in range(2)]
        yy = [sb(f"yy{k}", [P, BANK]) for k in range(2)]
        psA = [pb(f"psA{k}", [P, BANK]) for k in range(2)]
        psG = [pb(f"psG{k}", [P, BANK]) for k in range(2)]
        psT = [pb(f"psT{k}", [P, 4, P]) for k in range(2)]
        block = ctx.enter_context(nc.Block())

        @block.scalar
        def _(act):
            for c in range(NB):
                act.activation(gl[:, c * S:(c + 1) * S], net.yT[:, c * S:(c + 1) * S], ACT.Gelu,
                               bias=net.w["dr_b"][:, 0:1]).then_inc(s_ge, 1)
            for c in range(NCH):
                act.wait_ge(s_p, c + 1)
                if c >= 2:
                    act.wait_ge(s_m, c - 1)
                act.activation(sg[c % 2][:, :], psG[c % 2][:, :], ACT.Sigmoid, bias=net.w["glu_b"][:, 1:2]).then_inc(s_sg, 1)

        @block.tensor
        def _(pe):
            def turn(c):
                pe.wait_ge(s_m, c + 1)
                if c >= 2:
                    pe.wait_ge(s_x, c - 1)
                for t in range(4):
                    ins = pe.transpose(psT[c % 2][:, t, :], yy[c % 2][:, t * P:(t + 1) * P], net.identf[:, :])
                ins.then_inc(s_t, 1)

            for c in range(NCH):
                pe.wait_ge(s_ge, c // 2 + 1)
                if c >= 2:
                    pe.wait_ge(s_m, c - 1)
                src = gl[:, c * BANK:(c + 1) * BANK]
                pe.matmul(psA[c % 2][:, :], net.w["glu_w"][:, 0:D], src, start=True, stop=True)
                pe.matmul(psG[c % 2][:, :], net.w["glu_w"][:, D:2 * D], src, start=True, stop=True).then_inc(s_p, 1)
                if c:
                    turn(c - 1)
            turn(NCH - 1)

        @block.vector
        def _(dve):
            def add(c):
                dve.wait_ge(s_t, c + 1)
                X = net.X[:, 4 * c:4 * c + 4, :]
                dve.tensor_tensor(X, psT[c % 2][:, :, :], X, ALU.add).then_inc(s_x, 1)

            for c in range(NCH):
                dve.wait_ge(s_sg, c + 1)
                if c >= 2:
                    dve.wait_ge(s_t, c - 1)
                dve.scalar_tensor_tensor(yy[c % 2][:, :], psA[c % 2][:, :], net.w["glu_b"][:, 0:1], sg[c % 2][:, :],
                                         ALU.add, ALU.mult).then_inc(s_m, 1)
                if c:
                    add(c - 1)
            add(NCH - 1)


def store(nc, net):
    s_out = net.sem("stored")
    with nc.Block() as block:
        @block.sync
        def _(sp):
            sp.dma_start(net.out.rearrange("b (i p) d -> p (b i) d", p=P), net.X[:, :, :]).then_inc(s_out, 16)
            sp.wait_ge(s_out, 16)


SMALL = {
    "Wq": [P, D], "Wk": [P, GROUPS * DK], "Wv": [P, GROUPS * DK], "Wo": [P, D], "router_w": [P, NE],
    "norm1_w": [P, D], "norm2_w": [P, D], "router_b": [P, NE], "b1": [P, NE * FC], "b2": [P, NE * FC],
    "b3": [NE, D], "in_w": [P, 2 * DI], "x_w": [P, CI, DTR + 2 * NS], "dt_w": [DTR, DI], "out_w": [P, DI],
    "dr_w": [P, 2, D], "glu_w": [P, 2 * D], "conv_w": [P, CI, DC], "conv_b": [P, CI], "dt_b": [P, CI],
    "Dv": [P, CI], "A_log": [P, CI, NS], "dr_b": [P, 1], "glu_b": [P, 2], "ln_g": [P, D], "ln_b": [P, D],
    "cos": [P, TB, D // 2], "sin": [P, TB, D // 2],
}
EXPERTS = {"W1": [P, NE, FF], "W2": [P, NE, FF], "W3": [P, NE, FC, D]}


def program(nc, x, d, out):
    with ExitStack() as ctx:
        net = Net()
        sb = lambda n, s, t=F32: ctx.enter_context(nc.sbuf_tensor(n, s, t))

        def phase(build, *name):
            own = []

            def sem(n):
                own.append(nc.alloc_semaphore(name=n))
                return own[-1]

            net.sem = sem
            build(nc, net, *name)
            nc.clear_and_free_semaphores(own)
            nc.all_engine_barrier()

        net.x, net.d, net.out = x, d, out
        net.w = {n: sb(f"w_{n}", s) for n, s in SMALL.items()}
        net.X, net.U = sb("X", [P, NT, D]), sb("U", [P, NT, D])
        net.yT = sb("yT", [P, NT * P])
        net.VA = sb("VA", [P, NT, GROUPS, VW])
        net.comb = sb("comb", [P, NT, NE])
        net.identf, net.identb = sb("identf", [P, P]), sb("identb", [P, P], BF16)
        net.mask_st, net.mask_ts = sb("mask_st", [P, P], BF16), sb("mask_ts", [P, P], BF16)
        net.sel = sb("sel", [LVL * 2 * NS, 2 * NS, P], BF16)
        net.before, net.mhalf = sb("before", [P, NE, NE]), sb("mhalf", [P, TB])
        net.qd = nc.dram_tensor("q_parts", (NB, LVL, P, S), BF16, kind="Internal").ap()
        net.kd = nc.dram_tensor("k_parts", (NB, LVL, GROUPS * DK, S), BF16, kind="Internal").ap()
        net.nmd = nc.dram_tensor("max_parts", (2, LVL * 2 * TB, P), BF16, kind="Internal").ap()
        net.AO = net.yT[:, :].rearrange("p (i d) -> p i d", d=D)
        phase(setup)
        for k in range(2):
            with ExitStack() as layer:
                net.s_experts = layer.enter_context(nc.semaphore(f"f{k}_experts_loaded"))
                for n, s in EXPERTS.items():
                    net.w[n] = layer.enter_context(nc.sbuf_tensor(f"f{k}_{n}", s, F32))
                phase(attn_prep, f"f{k}p_")
                phase(attn_core, f"f{k}c_")
                phase(attn_out, f"f{k}o_")
                phase(moe, f"f{k}m_")
            if k == 0:
                phase(mamba_norm, "mn_")
                phase(mamba_scan, "ms_")
                phase(mamba_out, "mo_")
        phase(store)


def layouts(inputs):
    import numpy as np

    f = lambda n: np.asarray(inputs["L0_ffn_" + n])
    a = lambda n: np.asarray(inputs["L0_attn_" + n])
    rows = lambda v: np.broadcast_to(v[None, :], (P, v.shape[0]))
    cols = lambda v: v.reshape(-1, P).T
    d = {n: f(n) for n in ("Wq", "Wk", "Wv", "Wo", "router_w", "W1", "W2", "W3", "b3")}
    d |= {n: rows(f(n)) for n in ("norm1_w", "norm2_w", "router_b")}
    d |= {n: cols(f(n)) for n in ("b1", "b2")}
    d |= {"in_w": a("in_proj_w").T, "x_w": a("x_proj_w").T, "dt_w": a("dt_proj_w").T, "out_w": a("out_proj_w"),
          "dr_w": a("dim_reduce_w").T, "glu_w": a("glu_w").T, "conv_b": cols(a("conv_b")), "dt_b": cols(a("dt_proj_b")),
          "Dv": cols(a("D")), "dr_b": cols(a("dim_reduce_b")), "glu_b": cols(a("glu_b")),
          "conv_w": a("conv_w").reshape(CI, P, DC).transpose(1, 0, 2),
          "A_log": a("A_log").reshape(CI, P, NS).transpose(1, 0, 2), "ln_g": rows(a("ln_g")), "ln_b": rows(a("ln_b"))}
    half = D // 2
    theta = np.float32(1.0) / np.power(np.float32(10000.0), np.arange(half, dtype=np.float32) / np.float32(half))
    ang = np.arange(S, dtype=np.float32)[:, None] * theta[None, :]
    d |= {"cos": np.cos(ang).astype(np.float32), "sin": np.sin(ang).astype(np.float32)}
    return {n: np.ascontiguousarray(v) for n, v in d.items()}


def kernel(**inputs):
    import numpy as _np
    import concourse.bacc as _bacc
    from concourse import mybir as _mybir
    from concourse.bass_utils import run_bass_kernel_spmd as _run

    nc = _bacc.Bacc("TRN2", target_bir_lowering=False, num_devices=1)
    arrays = {"in_x": _np.ascontiguousarray(inputs["L0_attn_x"])}
    arrays |= {f"in_{n}": v for n, v in layouts(inputs).items()}
    args = {k: nc.dram_tensor(k, v.shape, _mybir.dt.from_np(v.dtype), kind="ExternalInput").ap()
            for k, v in arrays.items()}
    out = nc.dram_tensor("out_x", (NB, S, D), F32, kind="ExternalOutput").ap()
    program(nc, args["in_x"], {k[3:]: v for k, v in args.items()}, out)
    r = _run(nc, [arrays], core_ids=[0])
    return r.results[0]["out_x"]
```

```python
from contextlib import ExitStack

import concourse.bass as bass
from concourse import mybir

ALU = mybir.AluOpType
ACT = mybir.ActivationFunctionType
F32 = mybir.dt.float32
F32R = mybir.dt.float32r
BF16 = mybir.dt.bfloat16
AX_X = mybir.AxisListType.X

P = 128
NB, S, D = 4, 1024, 128
TB = S // P
NT = NB * TB
HEADS, GROUPS, DK = 16, 4, 8
HPG = HEADS // GROUPS
NE, FF = 8, 512
FC = FF // P
DI, NS, DTR, DC = 256, 16, 64, 4
CI = DI // P
PAD = DC - 1
Z_AT, SILU_AT, XP_AT, D_AT, MID_AT, DT_AT, EXP_AT, LN_AT, DL_AT = 1, 4, 5, 6, 7, 8, 12, 13, 14
BANK = 512
LVL = 3
QROWS = 2 * LVL * DK
HALF_AT = 32
EPB = NE // NB
VW = 32
MASKED = -1.0e30
RMS_EPS, LN_EPS = 1e-6, 1e-5


class Chain:

    def __init__(self, eng, sem, base=0):
        self.eng, self.sem, self.base, self.n = eng, sem, base, 0

    def link(self, ins):
        self.n += 1
        ins.then_inc(self.sem, 1)
        self.eng.wait_ge(self.sem, self.base + self.n)


class Net:
    pass


def p1_fills():
    fills = [[(3, 0, 512, 0)]] + [[(i, 0, 512, 0)] for i in range(4, 8)] + [[(7, 512, 1024, 0)]]
    for i in (6, 5, 4):
        w = (i + 1) * P - 512
        fills.append([(i, 512, 512 + w, 0), (6 - i, 0, 512 - w, w)])
    return fills


def p2_fills():
    right = [[(j, 512, 1024, 0)] for j in range(5)]
    left = [[(1, 128, 512, 0), (3, 384, 512, 384)], [(2, 256, 512, 0), (6, 768, 1024, 256)],
            [(5, 640, 1024, 0), (7, 896, 1024, 384)]]
    return [[(0, 0, 512, 0)]] + right + left


P1, P2 = p1_fills(), p2_fills()


def setup(nc, net):
    sem = net.sem
    s_ld, s_c, s_cv = sem("setup_loads"), sem("setup_consts"), sem("setup_conv")
    s_m = sem("setup_memsets")
    with nc.Block() as block:
        loads = [(net.X[:, :, :], net.x.rearrange("b (i p) d -> p (b i) d", p=P))]
        for name in ("Wq", "Wk", "Wv", "Wo", "router_w", "norm1_w", "norm2_w", "router_b", "b1", "b2", "b3",
                     "conv_b", "dt_b", "Dv", "dr_b", "glu_b", "ln_g", "ln_b"):
            loads.append((net.w[name][:], net.d[name]))
        @block.sync
        def _(sp):
            for out, src in loads:
                sp.dma_start(out, src).then_inc(s_ld, 16)
            sp.wait_ge(s_ld, 16 * len(loads))

        @block.gpsimd
        def _(pool):
            pool.memset(net.identf[:, :], 0.0).then_inc(s_m, 1)
            pool.memset(net.mask_st[:, :], 0.0).then_inc(s_m, 1)
            pool.memset(net.before[:, :, :], 1.0).then_inc(s_m, 1)
            pool.memset(net.mhalf[:, :], -0.5).then_inc(s_m, 1)
            pool.wait_ge(s_m, 4)
            pool.affine_select(out=net.identf[:, :], in_=net.identf[:, :], compare_op=ALU.not_equal, fill=1.0,
                               base=0, pattern=[[-1, P]], channel_multiplier=1).then_inc(s_c, 1)
            pool.affine_select(out=net.mask_st[:, :], in_=net.mask_st[:, :], compare_op=ALU.is_ge, fill=MASKED,
                               base=0, pattern=[[-1, P]], channel_multiplier=1).then_inc(s_c, 1)
            pool.affine_select(out=net.before[:, :, :], in_=net.before[:, :, :], compare_op=ALU.is_ge, fill=0.0,
                               base=-1, pattern=[[1, NE], [-1, NE]], channel_multiplier=0).then_inc(s_c, 1)

        @block.vector
        def _(dve):
            dve.wait_ge(s_c, 1)
            dve.tensor_copy(net.identb[:, :], net.identf[:, :]).then_inc(s_cv, 1)


def norm_stats(dve, chain, src, stats, mv):
    for i in range(TB):
        ins = dve.bn_stats(stats[:, i, :], src(i))
    chain.link(ins)
    for i in range(TB):
        ins = dve.bn_aggr(mv[:, i, :], stats[:, i, :])
    chain.link(ins)


UNIT_LOADS = 16


AHEAD = 2


def load_unit(sp, net, u):
    b, g = divmod(u, GROUPS)
    for par in range(2):
        r = 64 * par
        for r0, n in ((0, 3), (24, 2)):
            for k in range(2 * g, 2 * g + 2):
                h = DK * (2 * k + par)
                sp.dma_start(net.QS[r + r0:r + r0 + n * DK, k, :], net.qd[b, 0:n, h:h + DK, :]).then_inc(net.s_ld[g], 16)
        src = net.qd[b, 0, :, :].rearrange("(k h d) t -> h d k t", h=2, d=DK)[par, :, 2 * g:2 * g + 2, :]
        sp.dma_start(net.QS[r + 40:r + 48, 2 * g:2 * g + 2, :], src).then_inc(net.s_ld[g], 16)
        for r0, n, l in ((0, 3, 0), (24, 2, 1), (40, 1, 2)):
            src = net.kd[b, l:l + 1, DK * g:DK * (g + 1), :].to_broadcast([n, DK, S])
            sp.dma_start(net.KS[r + r0:r + r0 + n * DK, par, g, :], src).then_inc(net.s_ld[g], 16)


def attn_prep(nc, net, pre):
    sem = lambda n: net.sem(pre + n)
    s_chain, s_var, s_pow = sem("dve_chain"), sem("var_ready"), sem("rstd_ready")
    s_y, s_yr, s_rope, s_tp, s_xrt = sem("y_ready"), sem("rope_products"), sem("rope_ready"), sem("xr_turned"), sem("xrt_ready")
    s_qk, s_v, s_hi, s_r, s_mid, s_lo = sem("qk_ready"), sem("v_ready"), sem("hi_ready"), sem("rest_ready"), sem("mid_ready"), sem("lo_ready")
    s_rot, s_fill = sem("angles_loaded"), sem("stacks_filled")
    s_ve, s_st, s_one = sem("v_stored"), [sem(f"parts_stored{k}") for k in range(2)], sem("ones_set")
    with ExitStack() as ctx:
        sb = lambda n, s, d=F32: ctx.enter_context(nc.sbuf_tensor(pre + n, s, d))
        pb = lambda n, s, d=F32: ctx.enter_context(nc.psum_tensor(pre + n, s, d))
        stats, mv = sb("stats", [P, 2, TB, 6]), sb("mv", [P, 2, TB, 2])
        var, rstd, msq = sb("var", [P, 2, TB]), sb("rstd", [P, 2, TB]), sb("msq", [P, TB])
        y = sb("y", [P, TB, D])
        xr = sb("xr", [P, TB, D])
        ra, rb = sb("ra", [P, TB, D]), sb("rb", [P, TB, D])
        xrT = sb("xrT", [P, S])
        qp, kp = sb("qp", [P, 2, LVL, S], BF16), sb("kp", [GROUPS * DK, 2, LVL, S], BF16)
        qr, kr = sb("qr", [P, S]), sb("kr", [GROUPS * DK, S])
        psT, psQ = pb("psT", [P, TB, P]), pb("psQ", [P, S])
        psK, psV = pb("psK", [GROUPS * DK, S]), pb("psV", [P, TB, GROUPS, DK])
        half = D // 2
        block = ctx.enter_context(nc.Block())

        def store_parts(eng, b):
            eng.wait_ge(s_lo, 2 * b + 2)
            for t, home in ((qp, net.qd), (kp, net.kd)):
                eng.dma_start(home[b].rearrange("l p t -> p l t"), t[:, b % 2, :, :]).then_inc(s_st[b % 2], 16)

        @block.vector
        def _(dve):
            ch = Chain(dve, s_chain)
            tiles = lambda t, b: t[:, b * TB:(b + 1) * TB, :]

            def x_stats(b):
                norm_stats(dve, ch, lambda i: net.X[:, b * TB + i, :], stats[:, 0], mv[:, 0])
                dve.tensor_scalar(var[:, 0, :], mv[:, 0, :, 1], LN_EPS, None, ALU.add).then_inc(s_var, 1)

            def layernorm(b):
                dve.wait_ge(s_pow, 2 * b + 1)
                for i in range(TB):
                    ins = dve.tensor_scalar(net.U[:, b * TB + i, :], net.X[:, b * TB + i, :], mv[:, 0, i, 0:1],
                                            rstd[:, 0, i:i + 1], ALU.subtract, ALU.mult)
                ch.link(ins)
                norm_stats(dve, ch, lambda i: net.U[:, b * TB + i, :], stats[:, 1], mv[:, 1])
                ch.link(dve.tensor_tensor(msq[:, :], mv[:, 1, :, 0], mv[:, 1, :, 0], ALU.mult))
                dve.scalar_tensor_tensor(var[:, 1, :], msq[:, :], RMS_EPS, mv[:, 1, :, 1],
                                         ALU.add, ALU.add).then_inc(s_var, 1)

            def rope(b):
                dve.wait_ge(s_pow, 2 * b + 2)
                for i in range(TB):
                    ins = dve.scalar_tensor_tensor(y[:, i, :], net.U[:, b * TB + i, :], rstd[:, 1, i:i + 1],
                                                   net.w["norm1_w"][:, :], ALU.mult, ALU.mult)
                ins.then_inc(s_y, 1)
                dve.wait_ge(s_y, b + 1)
                dve.wait_ge(s_rot, 32)
                cos, sin = net.w["cos"][:, :, :], net.w["sin"][:, :, :]
                dve.tensor_tensor(ra[:, :, 0:half], y[:, :, 0::2], cos, ALU.mult)
                dve.tensor_tensor(rb[:, :, 0:half], y[:, :, 1::2], sin, ALU.mult)
                ch.link(dve.tensor_tensor(ra[:, :, half:D], y[:, :, 0::2], sin, ALU.mult))
                dve.wait_ge(s_yr, b + 1)
                if b:
                    dve.wait_ge(s_tp, b)
                dve.tensor_tensor(xr[:, :, 0:half], ra[:, :, 0:half], rb[:, :, 0:half], ALU.subtract)
                dve.tensor_tensor(xr[:, :, half:D], ra[:, :, half:D], rb[:, :, half:D], ALU.add).then_inc(s_rope, 1)

            def rest(b):
                dve.wait_ge(s_hi, 2 * b + 2)
                if b:
                    dve.wait_ge(s_lo, 2 * b)
                dve.tensor_tensor(qr[:, :], psQ[:, :], qp[:, b % 2, 0, :], ALU.subtract)
                dve.tensor_tensor(kr[:, :], psK[:, :], kp[:, b % 2, 0, :], ALU.subtract).then_inc(s_r, 1)
                dve.wait_ge(s_v, b + 1)
                dve.wait_ge(s_one, 1)
                dve.tensor_copy(tiles(net.VA, b)[:, :, :, 0:DK], psV[:, :, :, :]).then_inc(s_ve, 1)

            x_stats(0)
            layernorm(0)
            for b in range(NB):
                if b + 1 < NB:
                    x_stats(b + 1)
                rope(b)
                if b:
                    rest(b - 1)
                if b + 1 < NB:
                    layernorm(b + 1)
            rest(NB - 1)

        @block.gpsimd
        def _(pool):
            def power(b, k):
                pool.wait_ge(s_var, 2 * b + k + 1)
                pool.tensor_tensor(rstd[:, k, :], var[:, k, :], net.mhalf[:, 0:TB], ALU.pow).then_inc(s_pow, 1)

            def low(b):
                pool.wait_ge(s_mid, b + 1)
                pool.tensor_tensor(qp[:, b % 2, 2, :], qr[:, :], qp[:, b % 2, 1, :], ALU.subtract).then_inc(s_lo, 1)
                pool.tensor_tensor(kp[:, b % 2, 2, :], kr[:, :], kp[:, b % 2, 1, :], ALU.subtract).then_inc(s_lo, 1)

            power(0, 0)
            power(0, 1)
            for b in range(NB):
                if b + 1 < NB:
                    power(b + 1, 0)
                pool.wait_ge(s_y, b + 1)
                pool.wait_ge(s_rot, 32)
                pool.tensor_tensor(rb[:, :, half:D], y[:, :, 1::2], net.w["cos"][:, :, :], ALU.mult).then_inc(s_yr, 1)
                if b == 0:
                    pool.memset(net.VA[:, :, :, DK:VW], 1.0).then_inc(s_one, 1)
                else:
                    low(b - 1)
                if b + 1 < NB:
                    power(b + 1, 1)
            low(NB - 1)

        @block.tensor
        def _(pe):
            pe.sem_inc(s_r, 1)
            pe.sem_inc(s_ve, 1)
            with pe.Fori(0, NB) as b:
                pe.wait_ge(s_rope, b + 1)
                for i in range(TB):
                    ins = pe.transpose(psT[:, i, :], xr[:, i, :], net.identf[:, :])
                ins.then_inc(s_tp, 1)
                pe.wait_ge(s_xrt, b + 1)
                pe.wait_ge(s_r, b + 1)
                for h in range(2):
                    pe.matmul(psQ[:, h * BANK:(h + 1) * BANK], net.w["Wq"][:, :], xrT[:, h * BANK:(h + 1) * BANK],
                              start=True, stop=True)
                    ins = pe.matmul(psK[:, h * BANK:(h + 1) * BANK], net.w["Wk"][:, :],
                                    xrT[:, h * BANK:(h + 1) * BANK], start=True, stop=True)
                ins.then_inc(s_qk, 1)
                pe.wait_ge(s_ve, b + 1)
                for i in range(TB):
                    ins = pe.matmul(psV[:, i, :, :], xrT[:, i * P:(i + 1) * P], net.w["Wv"][:, :],
                                    start=True, stop=True)
                ins.then_inc(s_v, 1)

        @block.scalar
        def _(act):
            def mid(b):
                act.wait_ge(s_r, b + 2)
                act.activation(qp[:, b % 2, 1, :], qr[:, :], ACT.Copy)
                act.activation(kp[:, b % 2, 1, :], kr[:, :], ACT.Copy).then_inc(s_mid, 1)

            def fill(out, value):
                n = out.shape[1] * out.shape[2] // P
                tiles = net.identb[0:out.shape[0], :].rearrange("p (o t) -> p o t", o=1).to_broadcast([out.shape[0], n, P])
                act.activation(out.rearrange("p g (o t) -> p (g o) t", t=P), tiles, ACT.Copy,
                               scale=0.0, bias=value).then_inc(s_fill, 1)

            for par in range(2):
                fill(net.KS[64 * par:64 * par + 64, par, :, :], 1.0)
                fill(net.KS[64 - 64 * par:128 - 64 * par, par, :, :], 0.0)
            fill(net.QS[:, :, :], 0.0)
            for b in range(NB):
                act.wait_ge(s_tp, b + 1)
                if b:
                    act.wait_ge(s_v, b)
                act.activation(xrT[:, :], psT[:, :, :].rearrange("p i t -> p (i t)"), ACT.Copy).then_inc(s_xrt, 1)
                if b:
                    mid(b - 1)
                act.wait_ge(s_qk, b + 1)
                if b >= 2:
                    act.wait_ge(s_st[b % 2], 32 * (b // 2))
                act.activation(qp[:, b % 2, 0, :], psQ[:, :], ACT.Copy).then_inc(s_hi, 1)
                act.activation(kp[:, b % 2, 0, :], psK[:, :], ACT.Copy).then_inc(s_hi, 1)
            mid(NB - 1)
            store_parts(act, NB - 1)

        @block.sync
        def _(sp):
            for n in ("cos", "sin"):
                sp.dma_start(net.w[n][:, :, :], net.d[n].rearrange("(i p) k -> p i k", p=P)).then_inc(s_rot, 16)
            for b in range(NB - 1):
                store_parts(sp, b)
                if b == 0:
                    sp.wait_ge(s_st[0], 32)
                    sp.wait_ge(s_fill, 5)
                if b < AHEAD:
                    load_unit(sp, net, b)
            for k in range(2):
                sp.wait_ge(s_st[k], 32 * (NB // 2))


def attn_core(nc, net, pre):
    sem = lambda n: net.sem(pre + n)
    s_ld, QS, KS = net.s_ld, net.QS, net.KS
    s_nml = [sem(f"maxima_loaded{k}") for k in range(2)]
    s_p1f, s_p1r, s_p2f, s_ex = sem("rows_scored"), sem("rows_reduced"), sem("keys_scored"), sem("exp_done")
    s_pvf, s_ev, s_oT, s_on = sem("values_met"), sem("unit_copied"), sem("unit_turned"), sem("unit_normed")
    s_nb, s_tr, s_ntc = sem("maxima_split"), sem("maxima_turned"), sem("maxima_copied")
    s_nst, s_ch, s_mk = sem("maxima_stored"), sem("core_chain"), sem("later_keys_cleared")
    NUNIT, NF = NB * GROUPS, len(P2)
    NPAIR, NHEAD, SLOTS = 2 * NUNIT, HPG * NUNIT, HPG * NF
    LEAD = 6
    TURN_A, READ_A, TURN_O, READ_O, TURN_B, READ_B, TURN_P, READ_P = 3, 5, 9, 12, 21, 23, 27, 30
    with ExitStack() as ctx:
        sb = lambda n, s, d=F32: ctx.enter_context(nc.sbuf_tensor(pre + n, s, d))
        pb = lambda n, s, d=F32: ctx.enter_context(nc.psum_tensor(pre + n, s, d))
        probs = sb("probs", [P, HPG, 3, BANK])
        mx = sb("mx", [P, 2, 2, TB, 2])
        nm, nr = sb("nm", [P, 2 * TB]), sb("nr", [P, 2 * TB])
        nb = sb("nb", [P, 2, LVL, 2 * TB], BF16)
        nmT = sb("nmT", [LVL * 2 * TB, 2, P], BF16)
        oT = sb("oT", [P, S])
        rec = sb("rec", [P, 4, HPG, 1])
        ps1 = [pb(f"ps1_{k}", [P, BANK]) for k in range(2)]
        ps2 = [pb(f"ps2_{k}", [P, BANK]) for k in range(3)]
        psO = pb("psO", [P, S])
        psT = pb("psT", [P, BANK])
        psR = psT[0:LVL * 2 * TB, 0:P // 2].bitcast(BF16)
        block = ctx.enter_context(nc.Block())

        def diagonals(*fills):
            return sum(s0 == j * P for f in fills for j, s0, _, _ in P2[f])

        @block.gpsimd
        def _(pool):
            for u in range(NUNIT):
                for f in range(NF):
                    for j, s0, _, c in P2[f]:
                        if s0 == j * P:
                            pool.wait_ge(s_ex, SLOTS * u + HPG * (f + 1))
                            tile = probs[:, :, f % 3, c:c + P]
                            pool.affine_select(out=tile, in_=tile, compare_op=ALU.is_ge, fill=0.0, base=0,
                                               pattern=[[0, HPG], [1, P]], channel_multiplier=-1).then_inc(s_mk, 1)

        @block.sync
        def _(sp):
            def maxima(j):
                k = j % 2
                sp.wait_ge(s_ntc, j + 1)
                if j >= 2:
                    sp.wait_ge(s_nml[k], 32 * (j // 2))
                sp.dma_start(net.nmd[k, :, :], nmT[:, k, :]).then_inc(s_nst, 16)
                sp.wait_ge(s_nst, 16 * (j + 1))
                src = net.nmd[k, :, :].rearrange("(l h i) t -> h l (i t)", l=LVL, h=2)
                for par in range(2):
                    r = 64 * par + QROWS
                    sp.dma_start(QS[r:r + LVL, j % (HEADS // 2), :], src[par]).then_inc(s_nml[k], 16)

            for u in range(AHEAD, GROUPS):
                load_unit(sp, net, u)
            for j in range(NPAIR):
                maxima(j)
                if j % 2 and j >= 3 and (j - 3) // 2 + GROUPS < NUNIT:
                    u = (j - 3) // 2 + GROUPS
                    sp.wait_ge(s_pvf, NF * (u - GROUPS + 1))
                    load_unit(sp, net, u)

        @block.tensor
        def _(pe):
            def pass1(H, f):
                b, h = divmod(H, HEADS)
                r, k, g = 64 * (h % 2), h // 2, h // HPG
                n = len(P1) * H + f
                if h % HPG == 0 and f == 0:
                    pe.wait_ge(s_ld[g], 16 * UNIT_LOADS * (b + 1))
                if n >= 2:
                    pe.wait_ge(s_p1r, n - 1)
                bank = ps1[n % 2]
                for i, t0, t1, c in P1[f]:
                    diag = t1 == (i + 1) * P
                    w = t1 - t0
                    ins = pe.matmul(bank[:, c:c + w], QS[r:r + QROWS, k, i * P:(i + 1) * P],
                                    KS[r:r + QROWS, h % 2, g, t0:t1], start=True, stop=not diag)
                    if diag:
                        ins = pe.matmul(bank[:, c + w - P:c + w], net.identb[:, :], net.mask_st[:, :],
                                        start=False, stop=True)
                ins.then_inc(s_p1f, 1)

            def pass2(u, f, hu):
                g = u % GROUPS
                k = 2 * g + hu // 2
                n = SLOTS * u + HPG * f + hu
                if f == 0 and hu % 2 == 0:
                    pe.wait_ge(s_nml[hu // 2], 32 * (u + 1))
                if n >= 3:
                    pe.wait_ge(s_ex, n - 2)
                bank = ps2[n % 3]
                for j, s0, s1, c in P2[f]:
                    ins = pe.matmul(bank[:, c:c + s1 - s0], KS[:, hu % 2, g, j * P:(j + 1) * P],
                                    QS[:, k, s0:s1], start=True, stop=True)
                ins.then_inc(s_p2f, 1)

            def values(u, f):
                b, g = divmod(u, GROUPS)
                pe.wait_ge(s_ex, SLOTS * u + HPG * (f + 1))
                if diagonals(f):
                    pe.wait_ge(s_mk, TB * u + diagonals(*range(f + 1)))
                if f == 0 and u:
                    pe.wait_ge(s_ev, u)
                for j, s0, s1, c in P2[f]:
                    for hu in range(HPG):
                        ins = pe.matmul(psO[32 * hu:32 * hu + VW, s0:s1], net.VA[:, b * TB + j, g, :],
                                        probs[:, hu, f % 3, c:c + s1 - s0], start=(j == 0), stop=True,
                                        skip_group_check=True)
                ins.then_inc(s_pvf, 1)

            def turn_maxima(J):
                pe.wait_ge(s_nb, J + 1)
                if J >= 5:
                    pe.wait_ge(s_on, J - 4)
                elif J:
                    pe.wait_ge(s_ntc, J)
                pe.transpose(psR, nb[:, J % 2, :, :].rearrange("p l c -> p (l c)"), net.identb[:, :]).then_inc(s_tr, 1)

            def turn_unit(u, half):
                pe.wait_ge(s_ev, u + 1)
                pe.wait_ge(s_ntc, min(2 * u + 4 + half + 1, NPAIR))
                if 2 * u + 4 + half >= NPAIR and (u or half):
                    pe.wait_ge(s_on, 2 * u + half)
                for i in range(4):
                    c = (4 * half + i) * P
                    ins = pe.transpose(psT[:, i * P:(i + 1) * P], oT[:, c:c + P], net.identf[:, :])
                ins.then_inc(s_oT, 1)

            for H in range(LEAD):
                for f in range(len(P1)):
                    pass1(H, f)
                    if f == 3 and H in (2, 4):
                        turn_maxima(H // 2 - 1)
            for u in range(NUNIT + 1):
                for q in range(SLOTS):
                    if q == TURN_A and 2 * u + 2 < NPAIR:
                        turn_maxima(2 * u + 2)
                    if q == TURN_O and u:
                        turn_unit(u - 1, 0)
                    if q == TURN_B and 2 * u + 3 < NPAIR:
                        turn_maxima(2 * u + 3)
                    if q == TURN_P and u:
                        turn_unit(u - 1, 1)
                    if u < NUNIT:
                        pass2(u, q // HPG, q % HPG)
                        H = HPG * u + LEAD + q // len(P1)
                        if H < NHEAD:
                            pass1(H, q % len(P1))
                    if q % HPG == HPG - 1:
                        if q > HPG and u < NUNIT:
                            values(u, q // HPG - 1)
                        elif q < HPG and u:
                            values(u - 1, NF - 1)

        @block.scalar
        def _(act):
            for u in range(NUNIT + 1):
                for q in range(SLOTS):
                    f, hu = divmod(q, HPG)
                    if u < NUNIT:
                        n = SLOTS * u + q
                        if hu == 0 and NF * u + f >= 3:
                            act.wait_ge(s_pvf, NF * u + f - 2)
                        act.wait_ge(s_p2f, n + 1)
                        w = sum(s1 - s0 for _, s0, s1, _ in P2[f])
                        act.activation(probs[:, hu, f % 3, 0:w], ps2[n % 3][:, 0:w], ACT.Exp,
                                       scale=DK ** -0.5).then_inc(s_ex, 1)
                    if q == HPG and u:
                        act.wait_ge(s_pvf, NF * u)
                        if u >= 2:
                            act.wait_ge(s_oT, 2 * (u - 1))
                        act.activation(oT[:, :], psO[:, :], ACT.Copy).then_inc(s_ev, 1)

        @block.vector
        def _(dve):
            ch = Chain(dve, s_ch)

            def reduce_fill(H, f):
                J, hh = divmod(H, 2)
                n = len(P1) * H + f
                dve.wait_ge(s_p1f, n + 1)
                for i, t0, t1, c in P1[f]:
                    ins = dve.tensor_reduce(mx[:, J % 2, hh, i, t0 // 512:t0 // 512 + 1],
                                            ps1[n % 2][:, c:c + t1 - t0], AX_X, ALU.max)
                ins.then_inc(s_p1r, 1)
                if hh and f == len(P1) - 1:
                    split_maxima(J)

            def split_maxima(J):
                dve.wait_ge(s_p1r, len(P1) * 2 * (J + 1))
                if J >= 2:
                    dve.wait_ge(s_tr, J - 1)
                ch.link(dve.tensor_reduce(nm[:, :], mx[:, J % 2, :, :, :], AX_X, ALU.max, negate=True))
                part = nb[:, J % 2, :, :]
                ch.link(dve.tensor_copy(part[:, 0, :], nm[:, :]))
                ch.link(dve.tensor_tensor(nr[:, :], nm[:, :], part[:, 0, :], ALU.subtract))
                ch.link(dve.tensor_copy(part[:, 1, :], nr[:, :]))
                dve.tensor_tensor(part[:, 2, :], nr[:, :], part[:, 1, :], ALU.subtract).then_inc(s_nb, 1)

            def copy_maxima(J):
                dve.wait_ge(s_tr, J + 1)
                if J >= 2:
                    dve.wait_ge(s_nst, 16 * (J - 1))
                dve.tensor_copy(nmT[:, J % 2, :], psR).then_inc(s_ntc, 1)

            def norm_unit(u, half):
                b, g = divmod(u, GROUPS)
                dve.wait_ge(s_oT, 2 * u + half + 1)
                src = psT[:, :].rearrange("p (i h r) -> p i h r", i=4, h=HPG)
                ch.link(dve.reciprocal(rec[:, :, :, :], src[:, :, :, DK:DK + 1]))
                i0 = b * TB + 4 * half
                out = net.AO[:, i0:i0 + 4, g * HPG * DK:(g + 1) * HPG * DK].rearrange("p i (h d) -> p i h d", h=HPG)
                dve.tensor_tensor(out, src[:, :, :, 0:DK], rec[:, :, :, :].to_broadcast([P, 4, HPG, DK]),
                                  ALU.mult).then_inc(s_on, 1)

            ch.link(dve.memset(mx[:, :, :, :, :], -3.0e38))
            for H in range(LEAD):
                for f in range(len(P1)):
                    reduce_fill(H, f)
                    if f == 5 and H in (2, 4):
                        copy_maxima(H // 2 - 1)
            for u in range(NUNIT + 1):
                for q in range(SLOTS):
                    H = HPG * u + LEAD + q // len(P1)
                    if H < NHEAD and u < NUNIT:
                        reduce_fill(H, q % len(P1))
                    if q == READ_A and 2 * u + 2 < NPAIR:
                        copy_maxima(2 * u + 2)
                    if q == READ_O and u:
                        norm_unit(u - 1, 0)
                    if q == READ_B and 2 * u + 3 < NPAIR:
                        copy_maxima(2 * u + 3)
                    if q == READ_P and u:
                        norm_unit(u - 1, 1)


def attn_out(nc, net, pre):
    sem = lambda n: net.sem(pre + n)
    s_ch, s_aot, s_aoc, s_o, s_hv, s_pow = sem("dve_chain"), sem("ao_turned"), sem("ao_copied"), sem("proj_done"), sem("h_var_ready"), sem("rstd_ready")
    s_y, s_yt, s_yc, s_lg, s_lgm, s_e = sem("y_ready"), sem("y_turned"), sem("y_copied"), sem("logits_ready"), sem("logits_shifted"), sem("exp_done")
    s_cb, s_ct, s_cc, s_cl, s_lr = sem("comb_ready"), sem("comb_turned"), sem("comb_high"), sem("comb_low"), sem("logits_read")
    s_w, s_wh, s_wl, s_z, s_k = [sem(f"weights_loaded{k}") for k in range(2)], sem("weights_high"), sem("weights_low"), sem("zeros_set"), sem("selector_set")
    with ExitStack() as ctx:
        sb = lambda n, s, d=F32: ctx.enter_context(nc.sbuf_tensor(pre + n, s, d))
        pb = lambda n, s, d=F32: ctx.enter_context(nc.psum_tensor(pre + n, s, d))
        stats, mv = sb("stats", [P, TB, 6]), sb("mv", [P, TB, 2])
        var, rstd, msq = sb("var", [P, 2, TB]), sb("rstd", [P, 2, TB]), sb("msq", [P, TB])
        aoT, y = sb("aoT", [P, S]), sb("y", [P, TB, D])
        lg, lm = sb("lg", [P, TB, NE]), sb("lm", [P, TB, NE])
        top, ssum, rsum = sb("top", [P, TB, 1]), sb("ssum", [P, TB, 1]), sb("rsum", [P, TB, 1])
        gt, eq = sb("gt", [P, TB, NE, NE]), sb("eq", [P, TB, NE, NE])
        rank, ex, comb = sb("rank", [P, TB, NE, 1]), sb("ex", [P, TB, NE]), sb("comb", [P, TB, NE])
        raw = {n: sb(f"raw_{n}", [P, 2, FF]) for n in EXPERTS}
        psA, psH, psY = pb("psA", [P, TB, P]), pb("psH", [P, TB, P]), pb("psY", [P, TB, P])
        psL, psC = pb("psL", [P, TB, NE]), pb("psC", [NE, BANK])
        block = ctx.enter_context(nc.Block())
        at = lambda b: 0 <= b < NB
        TURNS = range(-2, NB + 2)
        TH = TB // 2

        @block.tensor
        def _(pe):
            def turn_comb(b, half):
                if half:
                    pe.wait_ge(s_cl, 2 * b + 1)
                else:
                    pe.wait_ge(s_cb, b + 1)
                    if b:
                        pe.wait_ge(s_cl, 2 * b)
                for i in range(TH):
                    ins = pe.transpose(psC[:, i * P:(i + 1) * P], comb[:, half * TH + i, :], net.identf[:, :])
                ins.then_inc(s_ct, 1)

            for b in TURNS:
                if at(b + 2):
                    for i in range(TB):
                        ins = pe.transpose(psA[:, i, :], net.AO[:, (b + 2) * TB + i, :], net.identf[:, :])
                    ins.then_inc(s_aot, 1)
                if at(b - 2):
                    turn_comb(b - 2, 0)
                if at(b + 2):
                    pe.wait_ge(s_aoc, b + 3)
                    if b + 2:
                        pe.wait_ge(s_hv, b + 2)
                    for i in range(TB):
                        ins = pe.matmul(psH[:, i, :], aoT[:, i * P:(i + 1) * P], net.w["Wo"][:, :], start=True, stop=True)
                    ins.then_inc(s_o, 1)
                if at(b):
                    pe.wait_ge(s_y, b + 1)
                    if b:
                        pe.wait_ge(s_yc, b)
                    for i in range(TB):
                        ins = pe.transpose(psY[:, i, :], y[:, i, :], net.identf[:, :])
                    ins.then_inc(s_yt, 1)
                if at(b - 2):
                    turn_comb(b - 2, 1)
                if at(b):
                    pe.wait_ge(s_yc, b + 1)
                    if b:
                        pe.wait_ge(s_lr, b)
                    for i in range(TB):
                        c = b * S + i * P
                        ins = pe.matmul(psL[:, i, :], net.yT[:, c:c + P], net.w["router_w"][:, :], start=True, stop=True)
                    ins.then_inc(s_lg, 1)

        @block.scalar
        def _(act):
            def high_weights(e):
                act.wait_ge(s_w[e % 2], 16 * len(EXPERTS) * (e // 2 + 1))
                for name in EXPERTS:
                    act.activation(net.w[name + "h"][:, e, :], raw[name][:, e % 2, :], ACT.Copy).then_inc(s_wh, 1)

            def high_comb(b, half):
                act.wait_ge(s_z, 1)
                act.wait_ge(s_ct, 2 * b + half + 1)
                c = b * S + half * BANK
                act.activation(net.combT[0:NE, c:c + BANK], psC[:, :], ACT.Copy).then_inc(s_cc, 1)

            for b in TURNS:
                if at(b + 2):
                    act.wait_ge(s_aot, b + 3)
                    if b + 2:
                        act.wait_ge(s_o, b + 2)
                    act.activation(aoT[:, :], psA[:, :, :].rearrange("p i t -> p (i t)"), ACT.Copy).then_inc(s_aoc, 1)
                if at(b - 2):
                    high_comb(b - 2, 0)
                if at(b):
                    high_weights(EPB * b)
                    act.wait_ge(s_yt, b + 1)
                    act.activation(net.yT[:, b * S:(b + 1) * S], psY[:, :, :].rearrange("p i t -> p (i t)"),
                                   ACT.Copy).then_inc(s_yc, 1)
                if at(b - 1):
                    act.wait_ge(s_lgm, b)
                    act.activation(ex[:, :, :], lm[:, :, :], ACT.Exp).then_inc(s_e, 1)
                if at(b - 2):
                    high_comb(b - 2, 1)
                if at(b):
                    high_weights(EPB * b + 1)

        @block.gpsimd
        def _(pool):
            pool.memset(net.combT[:, :].bitcast(F32), 0.0).then_inc(s_z, 1)
            pool.memset(net.pick[:, :, :].bitcast(F32), 0.0).then_inc(s_k, 1)
            for k in range(2):
                pool.wait_ge(s_k, k + 1)
                pool.affine_select(out=net.pick[:, :, :], in_=net.pick[:, :, :], compare_op=ALU.not_equal, fill=1.0,
                                   base=-HALF_AT * k, pattern=[[-1, NE], [0, P]], channel_multiplier=1).then_inc(s_k, 1)
            for b in TURNS:
                if at(b + 1):
                    pool.wait_ge(s_hv, b + 2)
                    pool.tensor_tensor(rstd[:, (b + 1) % 2, :], var[:, (b + 1) % 2, :], net.mhalf[:, 0:TB], ALU.pow).then_inc(s_pow, 1)
                if at(b):
                    for e in range(b * EPB, (b + 1) * EPB):
                        for k, name in enumerate(EXPERTS):
                            pool.wait_ge(s_wh, len(EXPERTS) * e + k + 1)
                            pool.tensor_tensor(net.w[name + "l"][:, e, :], raw[name][:, e % 2, :],
                                               net.w[name + "h"][:, e, :].bitcast(F32), ALU.subtract).then_inc(s_wl, 1)

        @block.sync
        def _(sp):
            for e in range(NE):
                if e >= 2:
                    sp.wait_ge(s_wl, len(EXPERTS) * (e - 1))
                for name in ("W1", "W2"):
                    sp.dma_start(raw[name][:, e % 2, :], net.d[name][e]).then_inc(s_w[e % 2], 16)
                sp.dma_start(raw["W3"][:, e % 2, :].rearrange("p (c n) -> p c n", n=D),
                             net.d["W3"][e].rearrange("(c p) n -> p c n", p=P)).then_inc(s_w[e % 2], 16)

        @block.vector
        def _(dve):
            ch = Chain(dve, s_ch)

            def residual(b):
                U = net.U[:, b * TB:(b + 1) * TB, :]
                dve.wait_ge(s_o, b + 1)
                ch.link(dve.tensor_tensor(U, psH[:, :, :], U, ALU.add))
                norm_stats(dve, ch, lambda i: U[:, i, :], stats, mv)
                ch.link(dve.tensor_tensor(msq[:, :], mv[:, :, 0], mv[:, :, 0], ALU.mult))
                dve.scalar_tensor_tensor(var[:, b % 2, :], msq[:, :], RMS_EPS, mv[:, :, 1], ALU.add, ALU.add).then_inc(s_hv, 1)

            def normed(b):
                dve.wait_ge(s_pow, b + 1)
                if b:
                    dve.wait_ge(s_yt, b)
                for i in range(TB):
                    ins = dve.scalar_tensor_tensor(y[:, i, :], net.U[:, b * TB + i, :], rstd[:, b % 2, i:i + 1],
                                                   net.w["norm2_w"][:, :], ALU.mult, ALU.mult)
                ins.then_inc(s_y, 1)

            def ranks(b):
                dve.wait_ge(s_lg, b + 1)
                if b:
                    dve.wait_ge(s_cb, b)
                rbias = net.w["router_b"][:, :].rearrange("p (o e) -> p o e", o=1).to_broadcast([P, TB, NE])
                dve.tensor_tensor(lg[:, :, :], psL[:, :, :], rbias, ALU.add).then_inc(s_lr, 1)
                dve.wait_ge(s_lr, b + 1)
                mine = lg[:, :, :].rearrange("p i (e o) -> p i e o", o=1).to_broadcast([P, TB, NE, NE])
                other = lg[:, :, :].rearrange("p i (o e) -> p i o e", o=1).to_broadcast([P, TB, NE, NE])
                before = net.before[:, :, :].rearrange("p (o e) f -> p o e f", o=1).to_broadcast([P, TB, NE, NE])
                ch.link(dve.tensor_reduce(top[:, :, :], lg[:, :, :], AX_X, ALU.max))
                dve.tensor_tensor(lm[:, :, :], lg[:, :, :], top[:, :, :].to_broadcast([P, TB, NE]),
                                  ALU.subtract).then_inc(s_lgm, 1)
                dve.tensor_tensor(gt[:, :, :, :], other, mine, ALU.is_gt)
                ch.link(dve.tensor_tensor(eq[:, :, :, :], other, mine, ALU.is_equal))
                ch.link(dve.tensor_tensor(eq[:, :, :, :], eq[:, :, :, :], before, ALU.mult))
                ch.link(dve.tensor_tensor(gt[:, :, :, :], gt[:, :, :, :], eq[:, :, :, :], ALU.add))
                ch.link(dve.tensor_reduce(rank[:, :, :, :], gt[:, :, :, :], AX_X, ALU.add))

            def weights(b):
                dve.wait_ge(s_e, b + 1)
                rk = rank[:, :, :, :].rearrange("p i e o -> p i (e o)")
                ch.link(dve.scalar_tensor_tensor(lm[:, :, :], rk, 1.5, ex[:, :, :], ALU.is_lt, ALU.mult))
                ch.link(dve.tensor_reduce(ssum[:, :, :], lm[:, :, :], AX_X, ALU.add))
                ch.link(dve.reciprocal(rsum[:, :, :], ssum[:, :, :]))
                if b:
                    dve.wait_ge(s_ct, 2 * b)
                dve.tensor_tensor(comb[:, :, :], lm[:, :, :], rsum[:, :, :].to_broadcast([P, TB, NE]),
                                  ALU.mult).then_inc(s_cb, 1)

            def low_comb(b, half):
                dve.wait_ge(s_cc, 2 * b + half + 1)
                c = b * S + half * BANK
                dve.tensor_tensor(net.combT[HALF_AT:HALF_AT + NE, c:c + BANK], psC[:, :],
                                  net.combT[0:NE, c:c + BANK].bitcast(F32), ALU.subtract).then_inc(s_cl, 1)

            for b in TURNS:
                if at(b + 1):
                    residual(b + 1)
                if at(b - 2):
                    low_comb(b - 2, 0)
                if at(b):
                    normed(b)
                if at(b - 1):
                    ranks(b - 1)
                if at(b - 2):
                    low_comb(b - 2, 1)
                if at(b - 1):
                    weights(b - 1)


def moe(nc, net, pre):
    sem = lambda n: net.sem(pre + n)
    s_xh, s_xl, s_h, s_sil, s_g = sem("x_high"), sem("x_low"), sem("up_done"), sem("silu_done"), sem("gated")
    s_gh, s_gl, s_dn, s_bc = sem("gated_high"), sem("gated_low"), sem("down_done"), sem("comb_copied")
    s_mu, s_ad, s_t, s_u, s_x = sem("expert_weighted"), sem("expert_added"), sem("sum_turned"), sem("h_done"), sem("x_done")
    NCH = NT // 4
    N = NE * FC
    LAG, RING = 3, 4
    CREDIT = 2
    with ExitStack() as ctx:
        sb = lambda n, s, d=F32: ctx.enter_context(nc.sbuf_tensor(pre + n, s, d))
        pb = lambda n, s, d=F32: ctx.enter_context(nc.psum_tensor(pre + n, s, d))
        xh, xl = sb("xh", [P, BANK], F32R), sb("xl", [P, BANK], F32R)
        sil = [sb(f"sil{k}", [P, BANK]) for k in range(2)]
        g = [sb(f"g{k}", [P, BANK]) for k in range(2)]
        gh = [sb(f"gh{k}", [P, BANK], F32R) for k in range(RING)]
        gl = [sb(f"gl{k}", [P, BANK], F32R) for k in range(RING)]
        bcs, wo, acc = sb("bcs", [P, BANK]), sb("wo", [P, BANK]), sb("acc", [P, BANK])
        ps1 = [pb(f"h1_{k}", [P, BANK]) for k in range(2)]
        ps2 = [pb(f"h2_{k}", [P, BANK]) for k in range(2)]
        pse = [pb(f"eo_{k}", [P, BANK]) for k in range(2)]
        psB, psT = pb("comb", [P, BANK]), pb("turned", [P, 4, P])
        block = ctx.enter_context(nc.Block())

        @block.tensor
        def _(pe):
            def product(out, wh, wl, rh, rl, start, stop):
                pe.matmul(out, wh, rh, start=start, stop=False)
                pe.matmul(out, wh, rl, start=False, stop=False)
                return pe.matmul(out, wl, rh, start=False, stop=stop)

            def up(c, n):
                e, fc = divmod(n, FC)
                if n == 0:
                    pe.wait_ge(s_xl, c + 1)
                pe.wait_ge(s_g, N * c + n + 1)
                cols = slice(fc * P, (fc + 1) * P)
                for ps, name in ((ps1, "W1"), (ps2, "W2")):
                    ins = product(ps[n % 2][:, :], net.w[name + "h"][:, e, cols], net.w[name + "l"][:, e, cols],
                                  xh[:, :], xl[:, :], True, True)
                ins.then_inc(s_h, 1)

            def down(c, n):
                e, fc = divmod(n, FC)
                cols = slice(fc * P, (fc + 1) * P)
                if fc == 0:
                    pe.wait_ge(s_mu, NE * c + e + 1)
                if fc == FC - 1:
                    pe.wait_ge(s_bc, NE * c + e + 1)
                    pe.matmul(psB[:, :], net.pick[:, e, :], net.combT[:, bass.ds(c * BANK, BANK)],
                              start=True, stop=True)
                pe.wait_ge(s_gl, N * c + n + 1 + CREDIT)
                ins = product(pse[e % 2][:, :], net.w["W3h"][:, e, cols], net.w["W3l"][:, e, cols],
                              gh[n % RING][:, :], gl[n % RING][:, :], fc == 0, fc == FC - 1)
                ins.then_inc(s_dn, 1)

            def turn(c):
                pe.wait_ge(s_ad, NE * (c + 1))
                pe.wait_ge(s_u, c + 1)
                for t in range(4):
                    ins = pe.transpose(psT[:, t, :], acc[:, t * P:(t + 1) * P], net.identf[:, :])
                ins.then_inc(s_t, 1)

            def chunk(c, last):
                for n in range(LAG, N):
                    up(c, n)
                    down(c, n - LAG)
                down(c, N - 3)
                if not last:
                    up(c + 1, 0)
                down(c, N - 2)
                down(c, N - 1)
                if not last:
                    up(c + 1, 1)
                    up(c + 1, 2)
                turn(c)

            pe.sem_inc(s_t, 1)
            for n in range(LAG):
                up(0, n)
            with pe.Fori(0, NCH - 1) as c:
                chunk(c, False)
            chunk(NCH - 1, True)

        @block.scalar
        def _(act):
            def high_x(c):
                if not isinstance(c, int) or c:
                    act.wait_ge(s_h, N * c)
                act.activation(xh[:, :], net.yT[:, bass.ds(c * BANK, BANK)], ACT.Copy).then_inc(s_xh, 1)

            def silu(c, n):
                act.wait_ge(s_h, N * c + n + 1)
                act.wait_ge(s_g, N * c + n + 1)
                act.activation(sil[n % 2][:, :], ps1[n % 2][:, :], ACT.Silu,
                               bias=net.w["b1"][:, n:n + 1]).then_inc(s_sil, 1)

            def high_g(c, n):
                act.wait_ge(s_g, N * c + n + 1 + CREDIT)
                act.wait_ge(s_dn, N * c + n + 1)
                act.activation(gh[n % RING][:, :], g[n % 2][:, :], ACT.Copy).then_inc(s_gh, 1)

            def weight(c, e):
                act.wait_ge(s_dn, N * c + (e + 1) * FC + RING)
                act.wait_ge(s_mu, NE * c + e + CREDIT)
                act.activation(bcs[:, :], psB[:, :], ACT.Copy).then_inc(s_bc, 1)

            def chunk(c, last):
                for n in range(LAG, N):
                    silu(c, n)
                    high_g(c, n - 1)
                    if n % FC == 2 and n > FC:
                        weight(c, (n - LAG) // FC)
                if not last:
                    high_x(c + 1)
                high_g(c, N - 1)
                if not last:
                    silu(c + 1, 0)
                weight(c, NE - 1)
                if not last:
                    silu(c + 1, 1)
                    high_g(c + 1, 0)
                    silu(c + 1, 2)
                    high_g(c + 1, 1)

            act.sem_inc(s_dn, RING)
            act.sem_inc(s_bc, 1)
            high_x(0)
            silu(0, 0)
            silu(0, 1)
            high_g(0, 0)
            silu(0, 2)
            high_g(0, 1)
            with act.Fori(0, NCH - 1) as c:
                chunk(c, False)
            chunk(NCH - 1, True)

        @block.gpsimd
        def _(pool):
            pool.sem_inc(s_gl, CREDIT)
            with pool.Fori(0, NCH) as c:
                for n in range(N):
                    pool.wait_ge(s_gh, N * c + n + 1)
                    pool.tensor_tensor(gl[n % RING][:, :], g[n % 2][:, :], gh[n % RING][:, :].bitcast(F32),
                                       ALU.subtract).then_inc(s_gl, 1)

        @block.vector
        def _(dve):
            def low_x(c):
                dve.wait_ge(s_xh, c + 1)
                dve.tensor_tensor(xl[:, :], net.yT[:, bass.ds(c * BANK, BANK)], xh[:, :].bitcast(F32),
                                  ALU.subtract).then_inc(s_xl, 1)

            def gate(c, n):
                dve.wait_ge(s_sil, N * c + n + 1)
                dve.wait_ge(s_gl, N * c + n + 1)
                dve.scalar_tensor_tensor(g[n % 2][:, :], ps2[n % 2][:, :], net.w["b2"][:, n:n + 1],
                                         sil[n % 2][:, :], ALU.add, ALU.mult).then_inc(s_g, 1)

            def weigh(c, e):
                dve.wait_ge(s_bc, NE * c + e + 2)
                if e == 0:
                    dve.wait_ge(s_t, c + 1)
                else:
                    dve.wait_ge(s_ad, NE * c + e)
                out = wo if e else acc
                ins = dve.scalar_tensor_tensor(out[:, :], pse[e % 2][:, :], net.w["b3"][:, e:e + 1], bcs[:, :],
                                               ALU.add, ALU.mult)
                ins.then_inc(s_mu, 1)
                if e == 0:
                    dve.sem_inc(s_ad, 1)
                else:
                    dve.wait_ge(s_mu, NE * c + e + 1 + CREDIT)
                    dve.tensor_tensor(acc[:, :], acc[:, :], wo[:, :], ALU.add).then_inc(s_ad, 1)

            def add(c):
                H = net.U[:, bass.ds(c * 4, 4), :]
                X = net.X[:, bass.ds(c * 4, 4), :]
                dve.wait_ge(s_t, c + 2)
                dve.tensor_tensor(H, psT[:, :, :], H, ALU.add).then_inc(s_u, 1)
                dve.wait_ge(s_u, c + 2)
                dve.scalar_tensor_tensor(X, H, 0.5, X, ALU.mult, ALU.add).then_inc(s_x, 1)

            def chunk(c, last):
                for n in range(LAG, N):
                    gate(c, n)
                    if n % FC == 2 and n > FC:
                        weigh(c, (n - LAG) // FC)
                if not last:
                    low_x(c + 1)
                    gate(c + 1, 0)
                weigh(c, NE - 1)
                if not last:
                    gate(c + 1, 1)
                    gate(c + 1, 2)
                add(c)

            dve.sem_inc(s_g, CREDIT)
            dve.sem_inc(s_mu, CREDIT)
            dve.sem_inc(s_u, 1)
            low_x(0)
            for n in range(LAG):
                gate(0, n)
            with dve.Fori(0, NCH - 1) as c:
                chunk(c, False)
            chunk(NCH - 1, True)


def mamba_norm(nc, net, pre):
    sem = lambda n: net.sem(pre + n)
    s_ch, s_var, s_pow, s_y, s_t, s_c = (sem(n) for n in (
        "dve_chain", "var_ready", "rstd_ready", "y_ready", "y_turned", "y_copied"))
    s_sel, s_ld = sem("selector_set"), sem("mamba_weights")
    with ExitStack() as ctx:
        sb = lambda n, s, d=F32: ctx.enter_context(nc.sbuf_tensor(pre + n, s, d))
        pb = lambda n, s, d=F32: ctx.enter_context(nc.psum_tensor(pre + n, s, d))
        stats, mv = sb("stats", [P, 2, TB, 6]), sb("mv", [P, 2, TB, 2])
        var, rstd = sb("var", [P, 2, TB]), sb("rstd", [P, 2, TB])
        y = [sb(f"y{k}", [P, TB, D]) for k in range(2)]
        psT = [pb(f"psT{k}", [P, TB, P]) for k in range(2)]
        block = ctx.enter_context(nc.Block())

        @block.sync
        def _(sp):
            loads = [(net.w[n][:], net.d[n]) for n in MAMBA if n not in ("x_w", "dr_w")]
            loads += [(net.w[n][:, :, :], net.d[n].rearrange("(c p) n -> p c n", p=P)) for n in ("x_w", "dr_w")]
            for out, src in loads:
                sp.dma_start(out, src).then_inc(s_ld, 16)
            sp.wait_ge(s_ld, 16 * len(loads))

        @block.vector
        def _(dve):
            ch = Chain(dve, s_ch)

            def stats_of(t, b, k):
                norm_stats(dve, ch, lambda i: t[:, b * TB + i, :], stats[:, k], mv[:, k])
                dve.tensor_scalar(var[:, k, :], mv[:, k, :, 1], LN_EPS, None, ALU.add).then_inc(s_var, 1)

            def scaled(t, b, k, out):
                dve.wait_ge(s_pow, 2 * b + k + 1)
                for i in range(TB):
                    ins = dve.tensor_scalar(out(i), t[:, b * TB + i, :], mv[:, k, i, 0:1], rstd[:, k, i:i + 1],
                                            ALU.subtract, ALU.mult)
                return ins

            for b in range(NB + 1):
                if b < NB:
                    stats_of(net.X, b, 0)
                if b:
                    if b > 2:
                        dve.wait_ge(s_t, b - 2)
                    scaled(net.U, b - 1, 1, lambda i: y[(b - 1) % 2][:, i, :]).then_inc(s_y, 1)
                    X, U = (t[:, (b - 1) * TB:b * TB, :] for t in (net.X, net.U))
                    ch.link(dve.tensor_tensor(X, X, U, ALU.add))
                if b < NB:
                    ch.link(scaled(net.X, b, 0, lambda i: net.U[:, b * TB + i, :]))
                    stats_of(net.U, b, 1)

        @block.gpsimd
        def _(pool):
            for b in range(NB):
                for k in range(2):
                    pool.wait_ge(s_var, 2 * b + k + 1)
                    pool.tensor_tensor(rstd[:, k, :], var[:, k, :], net.mhalf[:, 0:TB], ALU.pow).then_inc(s_pow, 1)
                if b == 0:
                    pool.memset(net.sel[:, :], 0.0).then_inc(s_sel, 1)
                elif b <= LVL:
                    pool.wait_ge(s_sel, b)
                    pool.affine_select(out=net.sel[:, :], in_=net.sel[:, :], compare_op=ALU.not_equal, fill=1.0,
                                       base=-2 * NS * (b - 1), pattern=[[-1, 2 * NS]],
                                       channel_multiplier=1).then_inc(s_sel, 1)

        @block.tensor
        def _(pe):
            for b in range(NB):
                pe.wait_ge(s_y, b + 1)
                if b >= 2:
                    pe.wait_ge(s_c, b - 1)
                for i in range(TB):
                    ins = pe.transpose(psT[b % 2][:, i, :], y[b % 2][:, i, :], net.identf[:, :])
                ins.then_inc(s_t, 1)

        @block.scalar
        def _(act):
            for b in range(NB):
                act.wait_ge(s_t, b + 1)
                act.activation(net.yT[:, b * S:(b + 1) * S], psT[b % 2][:, :, :].rearrange("p i t -> p (i t)"),
                               ACT.Identity, bias=net.w["ln_b"][:, 0:1], scale=net.w["ln_g"][:, 0:1]).then_inc(s_c, 1)


def mamba_scan(nc, net, pre):
    sem = lambda n: net.sem(pre + n)
    s_w0, s_w1, s_w2, s_w3 = sem("weights_product"), sem("weights_copied"), sem("a_exp"), sem("a_ready")
    s_pad, s_in, s_ev, s_cc = sem("pads_zero"), sem("xi_proj"), sem("xi_read"), sem("conv_chain")
    s_rd, s_rl, s_zr, s_sz = sem("round_ready"), sem("round_released"), sem("z_raw"), sem("z_silu")
    s_u, s_dts, s_hi, s_mid, s_bc = sem("u_ready"), sem("dt_ready"), sem("bc_hi"), sem("bc_mid"), sem("bc_ready")
    s_ex, s_sp, s_dl, s_du = sem("sp_exp"), sem("sp_log"), sem("delta_ready"), sem("du_ready")
    s_B, s_C, s_Cc, s_da, s_bx, s_sc = sem("b_spread"), sem("c_spread"), sem("c_copied"), sem("decay_ready"), sem("input_ready"), sem("scanned")
    s_D, s_hc, s_y, s_g = sem("d_term"), sem("hc_ready"), sem("y_added"), sem("gated")
    STEPS = NB * 2
    K = STEPS * NS
    Z_ROUNDS, XP_ROUNDS, DT_ROUNDS = 2 * CI, 2, 2 * CI
    PREP_ROUNDS = XP_ROUNDS + DT_ROUNDS

    def rounds_before(st):
        return PREP_ROUNDS * min(st + 1, STEPS) + Z_ROUNDS * ((st + 1) // 2)

    def z_round(st, i):
        return rounds_before(st) + i

    def prep_round(st, i):
        if st == 0:
            return i
        return rounds_before(st - 1) + Z_ROUNDS * (st % 2) + i

    with ExitStack() as ctx:
        sb = lambda n, s, d=F32: ctx.enter_context(nc.sbuf_tensor(pre + n, s, d))
        pb = lambda n, s, d=F32: ctx.enter_context(nc.psum_tensor(pre + n, s, d))
        negA = sb("negA", [P, CI, NS])
        diagD = sb("diagD", [P, CI, P])
        sz = sb("sz", [P, CI, S])
        u = [sb(f"u{k}", [P, CI, S]) for k in range(2)]
        cv = sb("cv", [P, CI, S])
        dts = sb("dts", [DTR, S])
        bc = [sb(f"bc{k}", [LVL * 2 * NS, S], BF16) for k in range(2)]
        delta = [sb(f"delta{k}", [P, CI, S]) for k in range(2)]
        du = sb("du", [P, CI, S])
        dA = [sb(f"dA{k}", [P, S]) for k in range(2)]
        bx = [sb(f"bx{k}", [P, S]) for k in range(2)]
        hs = [sb(f"hs{k}", [P, S]) for k in range(2)]
        hc = [sb(f"hc{k}", [P, 2, S]) for k in range(CI)]
        Cs = sb("Cs", [P, 2, S])
        bcr = cv[2 * NS:4 * NS, 0, :]
        psB, psC, psS = pb("psB", [P, S]), pb("psC", [P, BANK]), pb("psS", [P, BANK])
        psY = [pb(f"psY{c}", [P, S]) for c in range(CI)]
        block = ctx.enter_context(nc.Block())
        halves = [slice(0, BANK), slice(BANK, S)]
        xi = net.xi
        ring = psY + [psB]

        @block.tensor
        def _(pe):
            for k in range(2):
                for c in range(CI):
                    ins = pe.matmul(psB[:, (k * CI + c) * P:(k * CI + c + 1) * P], net.w["out_w"][:, c * P:(c + 1) * P],
                                    net.w["dr_w"][:, k, :], start=True, stop=True)
            ins.then_inc(s_w0, 1)
            for m in range(NB * CI):
                if m == 2:
                    pe.wait_ge(s_w1, 1)
                if m >= 3:
                    pe.wait_ge(s_ev, m - 2)
                b, c = divmod(m, CI)
                for hf in halves:
                    ins = pe.matmul(ring[m % 3][:, hf], net.w["in_w"][:, c * P:(c + 1) * P],
                                    net.yT[:, b * S + hf.start:b * S + hf.stop], start=True, stop=True)
                ins.then_inc(s_in, 1)

            def z(st, i):
                R, (c, h), b = z_round(st, i), divmod(i, 2), st // 2
                pe.wait_ge(s_rl, R)
                pe.matmul(psS[:, :], net.w["in_w"][:, (CI + c) * P:(CI + c + 1) * P],
                          net.yT[:, b * S + h * BANK:b * S + (h + 1) * BANK], start=True, stop=True).then_inc(s_rd, 1)

            def x_proj(st, h):
                R = prep_round(st, h)
                if R:
                    pe.wait_ge(s_rl, R)
                pe.wait_ge(s_u, CI * (st + 1))
                for c in range(CI):
                    ins = pe.matmul(psS[0:DTR + 2 * NS, :], net.w["x_w"][:, c, :], u[st % 2][:, c, halves[h]],
                                    start=(c == 0), stop=(c == CI - 1))
                ins.then_inc(s_rd, 1)

            def dt_proj(st, i):
                R, (c, h) = prep_round(st, XP_ROUNDS + i), divmod(i, 2)
                pe.wait_ge(s_rl, R)
                pe.wait_ge(s_dts, XP_ROUNDS * (st + 1))
                pe.matmul(psS[:, :], net.w["dt_w"][:, c * P:(c + 1) * P], dts[:, halves[h]],
                          start=True, stop=True).then_inc(s_rd, 1)

            def prepare(st, n):
                if XP_AT <= n < XP_AT + XP_ROUNDS:
                    x_proj(st, n - XP_AT)
                if DT_AT <= n < DT_AT + DT_ROUNDS:
                    dt_proj(st, n - DT_AT)

            def spread_B(k):
                st, n = divmod(k, NS)
                if n == 0:
                    pe.wait_ge(s_bc, st + 1)
                if k:
                    pe.wait_ge(s_bx, CI * k)
                for hf in halves:
                    ins = pe.matmul(psB[:, hf], net.sel[:, n:n + 1].to_broadcast([LVL * 2 * NS, P]), bc[st % 2][:, hf], start=True, stop=True)
                ins.then_inc(s_B, 1)

            def spread_C(k, h):
                st, n = divmod(k, NS)
                if k or h:
                    pe.wait_ge(s_Cc, 2 * k + h)
                pe.matmul(psC[:, :], net.sel[:, NS + n:NS + n + 1].to_broadcast([LVL * 2 * NS, P]), bc[st % 2][:, halves[h]], start=True, stop=True).then_inc(s_C, 1)

            def add_y(k, c):
                st, n = divmod(k, NS)
                if n == 0 and st:
                    pe.wait_ge(s_g, CI * (st - 1) + c + 1)
                pe.wait_ge(s_hc, CI * k + c + 1)
                for hf in halves:
                    ins = pe.matmul(psY[c][:, hf], net.identf[:, :], hc[c][:, k % 2, hf], start=(n == 0),
                                    stop=(n == NS - 1), skip_group_check=True)
                ins.then_inc(s_y, 1)

            def d_term(st):
                for c in range(CI):
                    for hf in halves:
                        ins = pe.matmul(psY[c][:, hf], diagD[:, c, :], u[st % 2][:, c, hf], start=False, stop=False,
                                        skip_group_check=True)
                    ins.then_inc(s_D, 1)

            pe.wait_ge(s_w3, 1)
            for n in range(NS):
                prepare(0, n)
            pe.wait_ge(s_ev, NB * CI)
            spread_B(0)
            spread_C(0, 0)
            spread_C(0, 1)
            for k in range(K):
                st, n = divmod(k, NS)
                if k + 1 < K:
                    spread_B(k + 1)
                    spread_C(k + 1, 0)
                if k:
                    add_y(k - 1, 0)
                if k + 1 < K:
                    spread_C(k + 1, 1)
                if k:
                    add_y(k - 1, 1)
                if n == D_AT:
                    d_term(st)
                if st % 2 == 0 and Z_AT <= n + 1 < Z_AT + Z_ROUNDS:
                    z(st, n + 1 - Z_AT)
                if st + 1 < STEPS:
                    prepare(st + 1, n + 1)
            for c in range(CI):
                add_y(K - 1, c)

        @block.scalar
        def _(act):
            act.activation(negA[:, :, :], net.w["A_log"][:, :, :], ACT.Exp).then_inc(s_w2, 1)
            act.wait_ge(s_w0, 1)
            act.activation(net.MT[:, :, :, :].rearrange("p k c o -> p (k c o)"), psB[:, 0:2 * CI * P],
                           ACT.Copy).then_inc(s_w1, 1)
            for m in range(NB * CI):
                act.wait_ge(s_in, m + 1)
                act.activation(xi[:, m // CI, m % CI, PAD:PAD + S], ring[m % 3][:, :], ACT.Copy).then_inc(s_ev, 1)
            act.wait_ge(s_w3, 1)

            def prepare(st, n):
                hi, cvt = bc[st % 2], cv
                if n == SILU_AT:
                    for c in range(CI):
                        act.wait_ge(s_cc, DC * CI * (st + 1) - CI + c + 1)
                        if st >= 2:
                            act.wait_ge(s_D, CI * (st - 1))
                            act.wait_ge(s_du, CI * (st - 1))
                        act.activation(u[st % 2][:, c, :], cvt[:, c, :], ACT.Silu).then_inc(s_u, 1)
                if XP_AT <= n < XP_AT + XP_ROUNDS:
                    h = n - XP_AT
                    act.wait_ge(s_rd, prep_round(st, h) + 1)
                    act.activation(dts[:, halves[h]], psS[0:DTR, :], ACT.Copy).then_inc(s_dts, 1)
                    act.activation(hi[0:2 * NS, halves[h]], psS[DTR:DTR + 2 * NS, :], ACT.Copy).then_inc(s_hi, 1)
                if n == MID_AT:
                    act.wait_ge(s_rl, prep_round(st, XP_ROUNDS))
                    act.activation(hi[2 * NS:4 * NS, :], bcr, ACT.Copy).then_inc(s_mid, 1)
                if DT_AT <= n < DT_AT + DT_ROUNDS:
                    i = n - DT_AT
                    c, h = divmod(i, 2)
                    act.wait_ge(s_bc, st + 1)
                    act.wait_ge(s_rd, prep_round(st, XP_ROUNDS + i) + 1)
                    if st >= 2 and i == 0:
                        act.wait_ge(s_du, CI * (st - 1))
                    act.activation(cvt[:, c, halves[h]], psS[:, :], ACT.Abs, bias=net.w["dt_b"][:, c:c + 1])
                    act.activation(delta[st % 2][:, c, halves[h]], psS[:, :], ACT.Relu,
                                   bias=net.w["dt_b"][:, c:c + 1]).then_inc(s_rl, 1)
                if n == EXP_AT:
                    act.wait_ge(s_rl, prep_round(st, PREP_ROUNDS))
                    for c in range(CI):
                        act.activation(cvt[:, c, :], cvt[:, c, :], ACT.Exp, scale=-1.0).then_inc(s_ex, 1)
                if n == LN_AT:
                    act.wait_ge(s_ex, CI * (st + 1))
                    for c in range(CI):
                        act.activation(cvt[:, c, :], cvt[:, c, :], ACT.Ln, bias=1.0).then_inc(s_sp, 1)

            def copy_C(k, h):
                act.wait_ge(s_C, 2 * k + h + 1)
                if k >= 2 and h == 0:
                    act.wait_ge(s_hc, CI * (k - 1))
                act.activation(Cs[:, k % 2, halves[h]], psC[:, :], ACT.Copy).then_inc(s_Cc, 1)

            def decay(k, c):
                st, n = divmod(k, NS)
                if n == 0:
                    act.wait_ge(s_dl, CI * st + c + 1)
                if k:
                    act.wait_ge(s_sc, CI * (k - 1) + c + 1)
                act.activation(dA[c][:, :], delta[st % 2][:, c, :], ACT.Exp, scale=negA[:, c, n:n + 1]).then_inc(s_da, 1)

            for n in range(NS):
                prepare(0, n)
            for k in range(K):
                st, n = divmod(k, NS)
                for c in range(CI):
                    copy_C(k, c)
                    decay(k, c)
                if st % 2 == 0:
                    if Z_AT <= n < Z_AT + Z_ROUNDS:
                        i = n - Z_AT
                        act.wait_ge(s_rd, z_round(st, i) + 1)
                        if st:
                            act.wait_ge(s_g, CI * st)
                        act.activation(sz[:, i // 2, halves[i % 2]], psS[:, :], ACT.Copy).then_inc(s_rl, 1)
                    if n == SILU_AT:
                        for c in range(CI):
                            act.wait_ge(s_rl, z_round(st, Z_ROUNDS))
                            act.activation(sz[:, c, :], sz[:, c, :], ACT.Silu).then_inc(s_sz, 1)
                if st + 1 < STEPS:
                    prepare(st + 1, n)

        @block.vector
        def _(dve):
            dve.memset(xi[:, :, :, 0:PAD], 0.0).then_inc(s_pad, 1)
            dve.memset(xi[:, :, :, PAD + S:], 0.0).then_inc(s_pad, 1)
            dve.wait_ge(s_pad, 2)
            dve.wait_ge(s_w2, 1)
            dve.tensor_scalar(negA[:, :, :], negA[:, :, :], -1.0, None, ALU.mult).then_inc(s_pad, 1)
            for c in range(CI):
                ins = dve.tensor_scalar(diagD[:, c, :], net.identf[:, :], net.w["Dv"][:, c:c + 1], None, ALU.mult)
            ins.then_inc(s_w3, 1)

            def conv(st, k, c):
                b, d = divmod(st, 2)
                o = k if d == 0 else 2 * PAD - k
                tap, src = net.w["conv_w"][:, c, k:k + 1], xi[:, b, c, o:o + S]
                if k == 0:
                    dve.wait_ge(s_ev, CI * b + c + 1)
                    ins = dve.tensor_scalar(cv[:, c, :], src, tap, net.w["conv_b"][:, c:c + 1], ALU.mult, ALU.add)
                else:
                    dve.wait_ge(s_cc, DC * CI * st + (k - 1) * CI + c + 1)
                    ins = dve.scalar_tensor_tensor(cv[:, c, :], src, tap, cv[:, c, :], ALU.mult, ALU.add)
                ins.then_inc(s_cc, 1)

            def prepare(st, n):
                mine, dl = bc[st % 2], delta[st % 2]
                if n < DC:
                    for c in range(CI):
                        conv(st, n, c)
                if XP_AT <= n < XP_AT + XP_ROUNDS:
                    h = n - XP_AT
                    dve.wait_ge(s_u, CI * (st + 1))
                    dve.wait_ge(s_hi, XP_ROUNDS * st + h + 1)
                    dve.tensor_tensor(bcr[:, halves[h]], psS[DTR:DTR + 2 * NS, :], mine[0:2 * NS, halves[h]],
                                      ALU.subtract).then_inc(s_rl, 1)
                if n == MID_AT:
                    dve.wait_ge(s_mid, st + 1)
                    dve.tensor_tensor(mine[4 * NS:6 * NS, :], bcr, mine[2 * NS:4 * NS, :], ALU.subtract).then_inc(s_bc, 1)
                if n == DL_AT:
                    for c in range(CI):
                        dve.wait_ge(s_rl, prep_round(st, PREP_ROUNDS))
                        dve.wait_ge(s_sp, CI * st + c + 1)
                        dve.tensor_tensor(dl[:, c, :], dl[:, c, :], cv[:, c, :], ALU.add).then_inc(s_dl, 1)

            def gate(st, c):
                b, d = divmod(st, 2)
                dve.wait_ge(s_y, CI * NS * (st + 1) - CI + c + 1)
                if d == 0:
                    dve.wait_ge(s_cc, DC * CI * (st + 2))
                dve.wait_ge(s_sz, CI * (b + 1))
                dve.tensor_tensor(net.g(b, d)[:, c, :], psY[c][:, :], sz[:, c, :], ALU.mult).then_inc(s_g, 1)

            for n in range(NS):
                prepare(0, n)
            for k in range(K):
                st, n = divmod(k, NS)
                way = slice(None) if st % 2 == 0 else slice(None, None, -1)
                if n == 0:
                    if st:
                        dve.wait_ge(s_bx, CI * k)
                    for c in range(CI):
                        dve.wait_ge(s_dl, CI * st + c + 1)
                        dve.tensor_tensor(du[:, c, :], delta[st % 2][:, c, :], u[st % 2][:, c, :], ALU.mult).then_inc(s_du, 1)
                    dve.wait_ge(s_du, CI * (st + 1))
                dve.wait_ge(s_B, k + 1)
                for c in range(CI):
                    if k:
                        dve.wait_ge(s_sc, CI * (k - 1) + c + 1)
                    dve.tensor_tensor(bx[c][:, :], psB[:, :], du[:, c, :], ALU.mult).then_inc(s_bx, 1)
                for c in range(CI):
                    if n == 0 and st:
                        gate(st - 1, c)
                    dve.wait_ge(s_bx, CI * k + c + 1)
                    dve.wait_ge(s_da, CI * k + c + 1)
                    if k:
                        dve.wait_ge(s_hc, CI * (k - 1) + c + 1)
                    dve.tensor_tensor_scan(hs[c][:, way], dA[c][:, way], bx[c][:, way], 0.0,
                                           ALU.mult, ALU.add).then_inc(s_sc, 1)
                if st + 1 < STEPS:
                    prepare(st + 1, n)
            for c in range(CI):
                gate(STEPS - 1, c)

        @block.gpsimd
        def _(pool):
            for k in range(K):
                pool.wait_ge(s_Cc, 2 * (k + 1))
                for c in range(CI):
                    pool.wait_ge(s_sc, CI * k + c + 1)
                    if k >= 2:
                        pool.wait_ge(s_y, CI * (k - 2) + c + 1)
                    pool.tensor_tensor(hc[c][:, k % 2, :], hs[c][:, :], Cs[:, k % 2, :], ALU.mult).then_inc(s_hc, 1)


def mamba_out(nc, net, pre):
    sem = lambda n: net.sem(pre + n)
    s_o, s_ge, s_p, s_sg, s_m, s_t, s_x = (sem(n) for n in (
        "out_proj", "gelu_done", "glu_ready", "sigmoid_done", "glu_done", "turned", "added"))
    NCH = NT // 4
    with ExitStack() as ctx:
        sb = lambda n, s, d=F32: ctx.enter_context(nc.sbuf_tensor(pre + n, s, d))
        pb = lambda n, s, d=F32: ctx.enter_context(nc.psum_tensor(pre + n, s, d))
        gl = sb("gl", [P, NT * P])
        sg = [sb(f"sg{k}", [P, BANK]) for k in range(2)]
        yy = [sb(f"yy{k}", [P, BANK]) for k in range(2)]
        psA = [pb(f"psA{k}", [P, BANK]) for k in range(2)]
        psG = [pb(f"psG{k}", [P, BANK]) for k in range(2)]
        psT = [pb(f"psT{k}", [P, 4, P]) for k in range(2)]
        ps1 = [pb(f"ps1{k}", [P, BANK]) for k in range(2)]
        block = ctx.enter_context(nc.Block())

        @block.scalar
        def _(act):
            for c in range(NCH):
                act.wait_ge(s_o, c + 1)
                act.activation(gl[:, c * BANK:(c + 1) * BANK], ps1[c % 2][:, :], ACT.Gelu,
                               bias=net.w["dr_b"][:, 0:1]).then_inc(s_ge, 1)
            for c in range(NCH):
                act.wait_ge(s_p, c + 1)
                if c >= 2:
                    act.wait_ge(s_m, c - 1)
                act.activation(sg[c % 2][:, :], psG[c % 2][:, :], ACT.Sigmoid, bias=net.w["glu_b"][:, 1:2]).then_inc(s_sg, 1)

        @block.tensor
        def _(pe):
            def turn(c):
                pe.wait_ge(s_m, c + 1)
                if c >= 2:
                    pe.wait_ge(s_x, c - 1)
                for t in range(4):
                    ins = pe.transpose(psT[c % 2][:, t, :], yy[c % 2][:, t * P:(t + 1) * P], net.identf[:, :])
                ins.then_inc(s_t, 1)

            for c in range(NCH):
                if c >= 2:
                    pe.wait_ge(s_ge, c - 1)
                b, hf = divmod(c, 2)
                for k in range(2 * CI):
                    ins = pe.matmul(ps1[c % 2][:, :], net.MT[:, k // CI, k % CI, :],
                                    net.g(b, k // CI)[:, k % CI, hf * BANK:(hf + 1) * BANK],
                                    start=(k == 0), stop=(k == 2 * CI - 1))
                ins.then_inc(s_o, 1)
            for c in range(NCH):
                pe.wait_ge(s_ge, c + 1)
                if c >= 2:
                    pe.wait_ge(s_m, c - 1)
                src = gl[:, c * BANK:(c + 1) * BANK]
                pe.matmul(psA[c % 2][:, :], net.w["glu_w"][:, 0:D], src, start=True, stop=True)
                pe.matmul(psG[c % 2][:, :], net.w["glu_w"][:, D:2 * D], src, start=True, stop=True).then_inc(s_p, 1)
                if c:
                    turn(c - 1)
            turn(NCH - 1)

        @block.vector
        def _(dve):
            def add(c):
                dve.wait_ge(s_t, c + 1)
                X = net.X[:, 4 * c:4 * c + 4, :]
                dve.tensor_tensor(X, psT[c % 2][:, :, :], X, ALU.add).then_inc(s_x, 1)

            for c in range(NCH):
                dve.wait_ge(s_sg, c + 1)
                if c >= 2:
                    dve.wait_ge(s_t, c - 1)
                dve.scalar_tensor_tensor(yy[c % 2][:, :], psA[c % 2][:, :], net.w["glu_b"][:, 0:1], sg[c % 2][:, :],
                                         ALU.add, ALU.mult).then_inc(s_m, 1)
                if c:
                    add(c - 1)
            add(NCH - 1)


def store(nc, net):
    s_out = net.sem("stored")
    with nc.Block() as block:
        @block.sync
        def _(sp):
            sp.dma_start(net.out.rearrange("b (i p) d -> p (b i) d", p=P), net.X[:, :, :]).then_inc(s_out, 16)
            sp.wait_ge(s_out, 16)


SMALL = {
    "Wq": [P, D], "Wk": [P, GROUPS * DK], "Wv": [P, GROUPS * DK], "Wo": [P, D], "router_w": [P, NE],
    "norm1_w": [P, D], "norm2_w": [P, D], "router_b": [P, NE], "b1": [P, NE * FC], "b2": [P, NE * FC],
    "b3": [P, NE], "conv_b": [P, CI], "dt_b": [P, CI], "Dv": [P, CI], "dr_b": [P, 1], "glu_b": [P, 2], "ln_g": [P, 1], "ln_b": [P, 1],
}
MAMBA = {
    "in_w": [P, 2 * DI], "x_w": [P, CI, DTR + 2 * NS], "dt_w": [DTR, DI], "out_w": [P, DI],
    "dr_w": [P, 2, D], "glu_w": [P, 2 * D], "conv_w": [P, CI, DC], "A_log": [P, CI, NS],
}
EXPERTS = ("W1", "W2", "W3")


def program(nc, x, d, out):
    with ExitStack() as ctx:
        net = Net()
        sb = lambda n, s, t=F32: ctx.enter_context(nc.sbuf_tensor(n, s, t))

        def phase(build, *name):
            own = []

            def sem(n):
                own.append(nc.alloc_semaphore(name=n))
                return own[-1]

            net.sem = sem
            build(nc, net, *name)
            nc.clear_and_free_semaphores(own)
            nc.all_engine_barrier()

        net.x, net.d, net.out = x, d, out
        net.w = {n: sb(f"w_{n}", s) for n, s in SMALL.items()}
        net.X, net.U = sb("X", [P, NT, D]), sb("U", [P, NT, D])
        net.yT = sb("yT", [P, NT * P])
        net.identf, net.identb = sb("identf", [P, P]), sb("identb", [P, P], BF16)
        net.mask_st = sb("mask_st", [P, P], BF16)
        net.before, net.mhalf = sb("before", [P, NE, NE]), sb("mhalf", [P, TB])
        net.qd = nc.dram_tensor("q_parts", (NB, LVL, P, S), BF16, kind="Internal").ap()
        net.kd = nc.dram_tensor("k_parts", (NB, LVL, GROUPS * DK, S), BF16, kind="Internal").ap()
        net.nmd = nc.dram_tensor("max_parts", (2, LVL * 2 * TB, P), BF16, kind="Internal").ap()
        net.AO = net.yT[:, :].rearrange("p (i d) -> p i d", d=D)
        phase(setup)
        for k in range(2):
            with ExitStack() as layer:
                net.s_ld = [layer.enter_context(nc.semaphore(f"f{k}_stacks_loaded{g}")) for g in range(GROUPS)]
                net.QS = layer.enter_context(nc.sbuf_tensor(f"f{k}_QS", [P, HEADS // 2, S], BF16))
                net.KS = layer.enter_context(nc.sbuf_tensor(f"f{k}_KS", [P, 2, GROUPS, S], BF16))
                for n in ("cos", "sin"):
                    net.w[n] = layer.enter_context(nc.sbuf_tensor(f"f{k}_{n}", [P, TB, D // 2], F32))
                net.VA = layer.enter_context(nc.sbuf_tensor(f"f{k}_VA", [P, NT, GROUPS, VW], F32))
                phase(attn_prep, f"f{k}p_")
                phase(attn_core, f"f{k}c_")
            with ExitStack() as layer:
                for n in EXPERTS:
                    for part in "hl":
                        net.w[n + part] = layer.enter_context(nc.sbuf_tensor(f"f{k}_{n}{part}", [P, NE, FF], F32R))
                net.combT = layer.enter_context(nc.sbuf_tensor(f"f{k}_combT", [P, NT * P], F32R))
                net.pick = layer.enter_context(nc.sbuf_tensor(f"f{k}_pick", [P, NE, P], F32R))
                phase(attn_out, f"f{k}o_")
                phase(moe, f"f{k}m_")
            if k == 0:
                with ExitStack() as mid:
                    net.sel = mid.enter_context(nc.sbuf_tensor("sel", [LVL * 2 * NS, 2 * NS], BF16))
                    for n, shape in MAMBA.items():
                        net.w[n] = mid.enter_context(nc.sbuf_tensor(f"w_{n}", shape, F32))
                    phase(mamba_norm, "mn_")
                    net.xi = mid.enter_context(nc.sbuf_tensor("xi", [P, NB, CI, S + 2 * PAD], F32))
                    net.MT = mid.enter_context(nc.sbuf_tensor("MT", [P, 2, CI, D], F32))

                    def gated(b, d):
                        if d == 0:
                            return net.xi[:, b, :, PAD:PAD + S]
                        home = net.U[:, :, :].rearrange("p i d -> p (i d)") if b < 2 else net.yT[:, :]
                        return home[:, b % 2 * CI * S:(b % 2 + 1) * CI * S].rearrange("p (c t) -> p c t", c=CI)

                    net.g = gated
                    phase(mamba_scan, "ms_")
                    phase(mamba_out, "mo_")
        phase(store)


def layouts(inputs):
    import numpy as np

    f = lambda n: np.asarray(inputs["L0_ffn_" + n])
    a = lambda n: np.asarray(inputs["L0_attn_" + n])
    rows = lambda v: np.broadcast_to(v[None, :], (P, v.shape[0]))
    cols = lambda v: v.reshape(-1, P).T
    d = {n: f(n) for n in ("Wq", "Wk", "Wv", "Wo", "router_w", "W1", "W2", "W3")}
    d["b3"] = f("b3").T
    d |= {n: rows(f(n)) for n in ("norm1_w", "norm2_w", "router_b")}
    d |= {n: cols(f(n)) for n in ("b1", "b2")}
    d |= {"in_w": a("in_proj_w").T, "x_w": a("x_proj_w").T, "dt_w": a("dt_proj_w").T, "out_w": a("out_proj_w"),
          "dr_w": a("dim_reduce_w").T, "glu_w": a("glu_w").T, "conv_b": cols(a("conv_b")), "dt_b": cols(a("dt_proj_b")),
          "Dv": cols(a("D")), "dr_b": cols(a("dim_reduce_b")), "glu_b": cols(a("glu_b")),
          "conv_w": a("conv_w").reshape(CI, P, DC).transpose(1, 0, 2),
          "A_log": a("A_log").reshape(CI, P, NS).transpose(1, 0, 2), "ln_g": cols(a("ln_g")), "ln_b": cols(a("ln_b"))}
    half = D // 2
    theta = np.float32(1.0) / np.power(np.float32(10000.0), np.arange(half, dtype=np.float32) / np.float32(half))
    ang = np.arange(S, dtype=np.float32)[:, None] * theta[None, :]
    d |= {"cos": np.cos(ang).astype(np.float32), "sin": np.sin(ang).astype(np.float32)}
    return {n: np.ascontiguousarray(v) for n, v in d.items()}


def kernel(**inputs):
    import numpy as _np
    import concourse.bacc as _bacc
    from concourse import mybir as _mybir
    from concourse.bass_utils import run_bass_kernel_spmd as _run

    nc = _bacc.Bacc("TRN2", target_bir_lowering=False, num_devices=1)
    arrays = {"in_x": _np.ascontiguousarray(inputs["L0_attn_x"])}
    arrays |= {f"in_{n}": v for n, v in layouts(inputs).items()}
    args = {k: nc.dram_tensor(k, v.shape, _mybir.dt.from_np(v.dtype), kind="ExternalInput").ap()
            for k, v in arrays.items()}
    out = nc.dram_tensor("out_x", (NB, S, D), F32, kind="ExternalOutput").ap()
    program(nc, args["in_x"], {k[3:]: v for k, v in args.items()}, out)
    r = _run(nc, [arrays], core_ids=[0])
    return r.results[0]["out_x"]
```
